# Optimizing a Trainium2 kernel written in Bass

```python
import numpy as np
import jax
import jax.numpy as jnp

def _softmax(x, axis=-1):
    return jax.nn.softmax(x, axis=axis)

def _gelu(x):
    return jax.nn.gelu(x, approximate=True)

def _silu(x):
    return jax.nn.silu(x)

def _sigmoid(x):
    return jax.nn.sigmoid(x)

def _layernorm(x, axis=-1, eps=1e-05):
    m = jnp.mean(x, axis=axis, keepdims=True)
    v = jnp.var(x, axis=axis, keepdims=True)
    return (x - m) / jnp.sqrt(v + eps)

def _scatter_add(tgt, idx, src, axis=0):
    return tgt.at[idx].add(src)

def _segment_sum(src, seg, n):
    return jax.ops.segment_sum(src, seg, n)
kernel_name = 'mk_flamingo_gated_d4_seqx_r8_c6f1cf'

def setup_inputs(seed: int=0):
    np.random.seed(seed)
    _w = jnp.asarray

    def _rec_inputs():
        import jax
        import jax.numpy as jnp
        _rk = jax.random.key(seed)
        x = -0.0002928 + 1 * jax.random.normal(jax.random.fold_in(_rk, 1), (4, 256, 128), jnp.float32)
        _lenS = 256 - jax.random.randint(jax.random.fold_in(_rk, 7), (4,), 0, max(1, 256 // 4) + 1, jnp.int32)
        _lenS2 = 256 - jax.random.randint(jax.random.fold_in(_rk, 8), (4,), 0, max(1, 256 // 4) + 1, jnp.int32)
        _ctx_1024P = jax.random.normal(jax.random.fold_in(_rk, 11), (4, 16, 128), jnp.float32)
        _ctx_1024c = jax.random.dirichlet(jax.random.fold_in(_rk, 511), 0.3 * jnp.ones((16,), jnp.float32), (4, 256))
        _ctx_1024t = jnp.einsum('bsk,bkd->bsd', _ctx_1024c, _ctx_1024P)
        _ctx_1024t = _ctx_1024t * jax.lax.rsqrt(jnp.mean(jnp.square(_ctx_1024t)) + 1e-12) * 0.953939
        ctx_1024 = 4.13588e-05 + 0.999923 * (_ctx_1024t + 0.3 * jax.random.normal(jax.random.fold_in(_rk, 611), (4, 256, 128), jnp.float32))
        _validS = jnp.arange(256)[None, :] < _lenS[:, None]
        _validS2 = jnp.arange(256)[None, :] < _lenS2[:, None]
        _causal = jnp.tril(jnp.ones((256, 256), dtype=bool))
        mask_BxSxS2_bk0 = jnp.logical_not(jnp.broadcast_to(_validS2[:, None, :], (4, 256, 256)))
        _g = jax.random.normal(jax.random.fold_in(_rk, 9001), (2, 4), jnp.float32)
        _g = jnp.sign(_g) * jnp.maximum(jnp.abs(_g), 1.0) + (_g == 0) * 1.0
        g_xattn = _g[0]
        g_ffn = _g[1]
        return (x, ctx_1024, mask_BxSxS2_bk0, g_xattn, g_ffn)
    x, ctx_1024, mask_BxSxS2_bk0, g_xattn, g_ffn = _rec_inputs()

    def _L0_xattn_setup():
        import jax, jax.numpy as jnp
        import numpy as np
        D_MODEL = 128
        N_HEADS = 16
        D_HEAD = D_MODEL // N_HEADS
        key = jax.random.key(seed)
        ks = jax.random.split(key, 6)
        query = jax.random.normal(ks[0], (2, 256, D_MODEL), dtype=jnp.float32)
        context = jax.random.normal(ks[1], (2, 512, D_MODEL), dtype=jnp.float32)
        s = 1.0 / np.sqrt(D_MODEL)
        Wq = jax.random.normal(ks[2], (D_MODEL, D_MODEL), dtype=jnp.float32) * s
        Wk = jax.random.normal(ks[3], (D_MODEL, D_MODEL), dtype=jnp.float32) * s
        Wv = jax.random.normal(ks[4], (D_MODEL, D_MODEL), dtype=jnp.float32) * s
        Wo = jax.random.normal(ks[5], (D_MODEL, D_MODEL), dtype=jnp.float32) * s
        return {'query': query, 'context': context, 'Wq': Wq, 'Wk': Wk, 'Wv': Wv, 'Wo': Wo}
    _L0_xattn_all = _L0_xattn_setup()
    _L0_xattn_in = {k: v for k, v in _L0_xattn_all.items() if k in ('Wq', 'Wk', 'Wv', 'Wo')}
    del _L0_xattn_all

    def _L0_ffn_setup():
        import jax, jax.numpy as jnp
        import numpy as np
        B, T, D, R, KEXP = (4, 512, 128, 64, 8)
        RH = max(D, 32)
        SCALE = 0.02

        def _fused_branch(Q_side, K_side, V, W, U, b, router_w1, router_b1, router_w2, router_b2, expert_bias):
            xV = jnp.einsum('btd,kdr->btkr', Q_side, V)
            yW = jnp.einsum('btd,kdr->btkr', K_side, W)
            cum_yW = jnp.cumsum(yW, axis=1)
            prod = xV * cum_yW
            h = jax.nn.gelu(Q_side @ router_w1.T + router_b1, approximate=False)
            logits = h @ router_w2.T + router_b2 + expert_bias
            weights = jax.nn.softmax(logits, axis=-1)
            out = jnp.einsum('btkr,kdr->btd', prod * weights[..., None], U)
            out = out + weights @ b
            n_valid = jnp.arange(1, Q_side.shape[1] + 1, dtype=Q_side.dtype)
            return out / n_valid[None, :, None]
        key = jax.random.key(seed)
        ks = jax.random.split(key, 20)
        x = jax.random.normal(ks[0], (B, T, D), dtype=jnp.float32)
        W_Q = jax.random.normal(ks[1], (D, D), dtype=jnp.float32) * (1.0 / np.sqrt(D))
        W_K = jax.random.normal(ks[2], (D, D), dtype=jnp.float32) * (1.0 / np.sqrt(D))
        W_O = jax.random.normal(ks[3], (D, D), dtype=jnp.float32) * (1.0 / np.sqrt(D))
        W_inv = jnp.eye(D, dtype=jnp.float32) + 0.01 * jax.random.normal(ks[4], (D, D), dtype=jnp.float32)
        V_fwd = jax.random.normal(ks[5], (KEXP, D, R), dtype=jnp.float32) * SCALE
        W_fwd = jax.random.normal(ks[6], (KEXP, D, R), dtype=jnp.float32) * SCALE
        U_fwd = jax.random.normal(ks[7], (KEXP, D, R), dtype=jnp.float32) * SCALE
        b_fwd = jnp.zeros((KEXP, D), dtype=jnp.float32)
        V_inv = jax.random.normal(ks[8], (KEXP, D, R), dtype=jnp.float32) * SCALE
        W_inv_exp = jax.random.normal(ks[9], (KEXP, D, R), dtype=jnp.float32) * SCALE
        U_inv = jax.random.normal(ks[10], (KEXP, D, R), dtype=jnp.float32) * SCALE
        b_inv = jnp.zeros((KEXP, D), dtype=jnp.float32)
        router_w1 = jax.random.normal(ks[11], (RH, D), dtype=jnp.float32) * (1.0 / np.sqrt(D))
        router_b1 = jnp.zeros((RH,), dtype=jnp.float32)
        router_w2 = jax.random.normal(ks[12], (KEXP, RH), dtype=jnp.float32) * (1.0 / np.sqrt(RH))
        router_b2 = jnp.zeros((KEXP,), dtype=jnp.float32)
        alpha_bi = jnp.asarray(0.5, dtype=jnp.float32)
        expert_bias = jnp.zeros((KEXP,), dtype=jnp.float32)
        return dict(x=x, W_Q=W_Q, W_K=W_K, W_O=W_O, W_inv=W_inv, V_fwd=V_fwd, W_fwd=W_fwd, U_fwd=U_fwd, b_fwd=b_fwd, V_inv=V_inv, W_inv_exp=W_inv_exp, U_inv=U_inv, b_inv=b_inv, router_w1=router_w1, router_b1=router_b1, router_w2=router_w2, router_b2=router_b2, alpha_bi=alpha_bi, expert_bias=expert_bias)
    _L0_ffn_all = _L0_ffn_setup()
    _L0_ffn_in = {k: v for k, v in _L0_ffn_all.items() if k in ('W_Q', 'W_K', 'W_O', 'W_inv', 'V_fwd', 'W_fwd', 'U_fwd', 'b_fwd', 'V_inv', 'W_inv_exp', 'U_inv', 'b_inv', 'router_w1', 'router_b1', 'router_w2', 'router_b2', 'alpha_bi', 'expert_bias')}
    del _L0_ffn_all

    def _L1_xattn_setup():
        import jax, jax.numpy as jnp
        import numpy as np
        NUM_HEAD = 16
        ADIM = 64
        IEPS = 1e-32
        MASK_FILL = -1e+32

        def sparse_norm(scores, nbias):
            t = jax.nn.relu(scores + nbias)
            t = t * t
            return t / (t.sum(-1, keepdims=True) + IEPS)
        key = jax.random.key(seed)
        ks = jax.random.split(key, 7)
        b, q, s, d = (2, 256, 256, 128)
        hsize = NUM_HEAD * ADIM
        iQ = jax.random.normal(ks[0], (b, q, d), dtype=jnp.float32)
        iK = jax.random.normal(ks[1], (b, s, d), dtype=jnp.float32)
        mask = jax.random.randint(ks[2], (b, q, s), 0, 2) == 1
        Wq = jax.random.normal(ks[3], (hsize, d), dtype=jnp.float32) * 0.02
        Wkv = jax.random.normal(ks[4], (2 * hsize, d), dtype=jnp.float32) * 0.02
        Wo = jax.random.normal(ks[5], (d, hsize), dtype=jnp.float32) * 0.02
        nbias = jnp.zeros((1,), dtype=jnp.float32)
        return {'iQ': iQ, 'iK': iK, 'mask': mask, 'Wq': Wq, 'Wkv': Wkv, 'Wo': Wo, 'nbias': nbias}
    _L1_xattn_all = _L1_xattn_setup()
    _L1_xattn_in = {k: v for k, v in _L1_xattn_all.items() if k in ('Wq', 'Wkv', 'Wo', 'nbias')}
    del _L1_xattn_all

    def _L1_ffn_setup():
        import jax, jax.numpy as jnp
        import numpy as np
        B, S, D, F, E = (1, 128, 128, 512, 8)
        EPS = 1e-05

        def _sublayer(xs, g, b, W1e, b1e, W2e, b2e):
            mu = jnp.mean(xs, axis=-1, keepdims=True)
            var = jnp.mean(jnp.square(xs - mu), axis=-1, keepdims=True)
            h = (xs - mu) * jax.lax.rsqrt(var + EPS) * g + b
            return xs + jax.nn.relu(h @ W1e.T + b1e) @ W2e.T + b2e
        key = jax.random.key(seed)
        ks = jax.random.split(key, 4)
        x = jax.random.normal(ks[0], (B, S, D), jnp.float32)
        centroids = jax.random.normal(ks[1], (E, D), jnp.float32) * 0.1
        gamma = jnp.ones((E, D), jnp.float32)
        beta = jnp.zeros((E, D), jnp.float32)
        W1 = jax.random.normal(ks[2], (E, F, D), jnp.float32) * 0.02
        b1 = jnp.zeros((E, F), jnp.float32)
        W2 = jax.random.normal(ks[3], (E, D, F), jnp.float32) * 0.02
        b2 = jnp.zeros((E, D), jnp.float32)
        return {'x': x, 'centroids': centroids, 'gamma': gamma, 'beta': beta, 'W1': W1, 'b1': b1, 'W2': W2, 'b2': b2}
    _L1_ffn_all = _L1_ffn_setup()
    _L1_ffn_in = {k: v for k, v in _L1_ffn_all.items() if k in ('centroids', 'gamma', 'beta', 'W1', 'b1', 'W2', 'b2')}
    del _L1_ffn_all

    def _L2_xattn_setup():
        import jax, jax.numpy as jnp
        import numpy as np
        EMBED_DIM = 128
        NUM_HEADS = 16
        HEAD_DIM = EMBED_DIM // NUM_HEADS
        key = jax.random.key(seed)
        kq, kk, kv = jax.random.split(key, 3)
        B, S, E = (4, 256, EMBED_DIM)
        return {'query': jax.random.normal(kq, (B, S, E), dtype=jnp.float32), 'key': jax.random.normal(kk, (B, S, E), dtype=jnp.float32), 'value': jax.random.normal(kv, (B, S, E), dtype=jnp.float32)}
    _L2_xattn_all = _L2_xattn_setup()
    _L2_xattn_in = {k: v for k, v in _L2_xattn_all.items() if k in ()}
    del _L2_xattn_all

    def _L2_ffn_setup():
        import jax, jax.numpy as jnp
        import numpy as np
        INT4_QMAX = 7.0

        def simulate_quantize_int4(w):
            scale = jnp.max(jnp.abs(w)) / INT4_QMAX
            q = jnp.clip(jnp.round(w / scale), -8.0, 7.0)
            return q * scale
        key = jax.random.key(seed)
        k_x, k_w, k_bias, k_a, k_b = jax.random.split(key, 5)
        d_in, features, rank = (128, 128, 16)
        x = jax.random.normal(k_x, (4, 1024, d_in), dtype=jnp.float32)
        kernel = jax.random.normal(k_w, (d_in, features), dtype=jnp.float32)
        bias = jax.random.normal(k_bias, (features,), dtype=jnp.float32)
        a = jax.random.normal(k_a, (d_in, rank), dtype=jnp.float32) * (1.0 / np.sqrt(d_in))
        b = jax.random.normal(k_b, (rank, features), dtype=jnp.float32) * 0.01
        return {'x': x, 'kernel': kernel, 'bias': bias, 'a': a, 'b': b}
    _L2_ffn_all = _L2_ffn_setup()
    _L2_ffn_in = {k: v for k, v in _L2_ffn_all.items() if k in ('kernel', 'bias', 'a', 'b')}
    del _L2_ffn_all

    def _L3_xattn_setup():
        import jax, jax.numpy as jnp
        import numpy as np
        DIM = 128
        H = 16
        D = 64
        INNER = H * D
        EPS = 1e-05

        def layernorm(x, w, b):
            mu = jnp.mean(x, axis=-1, keepdims=True)
            var = jnp.var(x, axis=-1, keepdims=True)
            return (x - mu) * jax.lax.rsqrt(var + EPS) * w + b
        key = jax.random.key(seed)
        ks = jax.random.split(key, 8)
        B, N, S = (4, 32, 1024)
        s = 1.0 / np.sqrt(DIM)
        return {'latents': jax.random.normal(ks[0], (B, N, DIM), jnp.float32), 'context': jax.random.normal(ks[1], (B, S, DIM), jnp.float32), 'ln_l_w': jnp.ones((DIM,), jnp.float32), 'ln_l_b': jnp.zeros((DIM,), jnp.float32), 'ln_c_w': jnp.ones((DIM,), jnp.float32), 'ln_c_b': jnp.zeros((DIM,), jnp.float32), 'Wq': jax.random.normal(ks[2], (DIM, INNER), jnp.float32) * s, 'Wkv': jax.random.normal(ks[3], (DIM, 2 * INNER), jnp.float32) * s, 'Wo': jax.random.normal(ks[4], (INNER, DIM), jnp.float32) * (1.0 / np.sqrt(INNER)), 'bo': jnp.zeros((DIM,), jnp.float32)}
    _L3_xattn_all = _L3_xattn_setup()
    _L3_xattn_in = {k: v for k, v in _L3_xattn_all.items() if k in ('ln_l_w', 'ln_l_b', 'ln_c_w', 'ln_c_b', 'Wq', 'Wkv', 'Wo', 'bo')}
    del _L3_xattn_all

    def _L3_ffn_setup():
        import jax, jax.numpy as jnp
        import numpy as np
        E = 8
        K = 2
        D = 128
        F = 512
        FS = 256
        B, S = (2, 128)
        key = jax.random.key(seed)
        ks = jax.random.split(key, 8)
        scale = jnp.float32(0.02)
        return {'x': jax.random.normal(ks[0], (B, S, D), jnp.float32), 'gate_w': jax.random.normal(ks[1], (E, D), jnp.float32) * scale, 'gate_k': jax.random.normal(ks[2], (E, D, F), jnp.float32) * scale, 'up_k': jax.random.normal(ks[3], (E, D, F), jnp.float32) * scale, 'down_k': jax.random.normal(ks[4], (E, F, D), jnp.float32) * scale, 'sh_gate': jax.random.normal(ks[5], (D, FS), jnp.float32) * scale, 'sh_up': jax.random.normal(ks[6], (D, FS), jnp.float32) * scale, 'sh_down': jax.random.normal(ks[7], (FS, D), jnp.float32) * scale}
    _L3_ffn_all = _L3_ffn_setup()
    _L3_ffn_in = {k: v for k, v in _L3_ffn_all.items() if k in ('gate_w', 'gate_k', 'up_k', 'down_k', 'sh_gate', 'sh_up', 'sh_down')}
    del _L3_ffn_all
    return {'x': x, 'ctx_1024': ctx_1024, 'mask_BxSxS2_bk0': mask_BxSxS2_bk0, 'g_xattn': g_xattn, 'g_ffn': g_ffn, 'L0_xattn_Wq': _L0_xattn_in['Wq'], 'L0_xattn_Wk': _L0_xattn_in['Wk'], 'L0_xattn_Wv': _L0_xattn_in['Wv'], 'L0_xattn_Wo': _L0_xattn_in['Wo'], 'L0_ffn_W_Q': _L0_ffn_in['W_Q'], 'L0_ffn_W_K': _L0_ffn_in['W_K'], 'L0_ffn_W_O': _L0_ffn_in['W_O'], 'L0_ffn_W_inv': _L0_ffn_in['W_inv'], 'L0_ffn_V_fwd': _L0_ffn_in['V_fwd'], 'L0_ffn_W_fwd': _L0_ffn_in['W_fwd'], 'L0_ffn_U_fwd': _L0_ffn_in['U_fwd'], 'L0_ffn_b_fwd': _L0_ffn_in['b_fwd'], 'L0_ffn_V_inv': _L0_ffn_in['V_inv'], 'L0_ffn_W_inv_exp': _L0_ffn_in['W_inv_exp'], 'L0_ffn_U_inv': _L0_ffn_in['U_inv'], 'L0_ffn_b_inv': _L0_ffn_in['b_inv'], 'L0_ffn_router_w1': _L0_ffn_in['router_w1'], 'L0_ffn_router_b1': _L0_ffn_in['router_b1'], 'L0_ffn_router_w2': _L0_ffn_in['router_w2'], 'L0_ffn_router_b2': _L0_ffn_in['router_b2'], 'L0_ffn_alpha_bi': _L0_ffn_in['alpha_bi'], 'L0_ffn_expert_bias': _L0_ffn_in['expert_bias'], 'L1_xattn_Wq': _L1_xattn_in['Wq'], 'L1_xattn_Wkv': _L1_xattn_in['Wkv'], 'L1_xattn_Wo': _L1_xattn_in['Wo'], 'L1_xattn_nbias': _L1_xattn_in['nbias'], 'L1_ffn_centroids': _L1_ffn_in['centroids'], 'L1_ffn_gamma': _L1_ffn_in['gamma'], 'L1_ffn_beta': _L1_ffn_in['beta'], 'L1_ffn_W1': _L1_ffn_in['W1'], 'L1_ffn_b1': _L1_ffn_in['b1'], 'L1_ffn_W2': _L1_ffn_in['W2'], 'L1_ffn_b2': _L1_ffn_in['b2'], 'L2_ffn_kernel': _L2_ffn_in['kernel'], 'L2_ffn_bias': _L2_ffn_in['bias'], 'L2_ffn_a': _L2_ffn_in['a'], 'L2_ffn_b': _L2_ffn_in['b'], 'L3_xattn_ln_l_w': _L3_xattn_in['ln_l_w'], 'L3_xattn_ln_l_b': _L3_xattn_in['ln_l_b'], 'L3_xattn_ln_c_w': _L3_xattn_in['ln_c_w'], 'L3_xattn_ln_c_b': _L3_xattn_in['ln_c_b'], 'L3_xattn_Wq': _L3_xattn_in['Wq'], 'L3_xattn_Wkv': _L3_xattn_in['Wkv'], 'L3_xattn_Wo': _L3_xattn_in['Wo'], 'L3_xattn_bo': _L3_xattn_in['bo'], 'L3_ffn_gate_w': _L3_ffn_in['gate_w'], 'L3_ffn_gate_k': _L3_ffn_in['gate_k'], 'L3_ffn_up_k': _L3_ffn_in['up_k'], 'L3_ffn_down_k': _L3_ffn_in['down_k'], 'L3_ffn_sh_gate': _L3_ffn_in['sh_gate'], 'L3_ffn_sh_up': _L3_ffn_in['sh_up'], 'L3_ffn_sh_down': _L3_ffn_in['sh_down']}

def reference(x, ctx_1024, mask_BxSxS2_bk0, g_xattn, g_ffn, L0_xattn_Wq, L0_xattn_Wk, L0_xattn_Wv, L0_xattn_Wo, L0_ffn_W_Q, L0_ffn_W_K, L0_ffn_W_O, L0_ffn_W_inv, L0_ffn_V_fwd, L0_ffn_W_fwd, L0_ffn_U_fwd, L0_ffn_b_fwd, L0_ffn_V_inv, L0_ffn_W_inv_exp, L0_ffn_U_inv, L0_ffn_b_inv, L0_ffn_router_w1, L0_ffn_router_b1, L0_ffn_router_w2, L0_ffn_router_b2, L0_ffn_alpha_bi, L0_ffn_expert_bias, L1_xattn_Wq, L1_xattn_Wkv, L1_xattn_Wo, L1_xattn_nbias, L1_ffn_centroids, L1_ffn_gamma, L1_ffn_beta, L1_ffn_W1, L1_ffn_b1, L1_ffn_W2, L1_ffn_b2, L2_ffn_kernel, L2_ffn_bias, L2_ffn_a, L2_ffn_b, L3_xattn_ln_l_w, L3_xattn_ln_l_b, L3_xattn_ln_c_w, L3_xattn_ln_c_b, L3_xattn_Wq, L3_xattn_Wkv, L3_xattn_Wo, L3_xattn_bo, L3_ffn_gate_w, L3_ffn_gate_k, L3_ffn_up_k, L3_ffn_down_k, L3_ffn_sh_gate, L3_ffn_sh_up, L3_ffn_sh_down):
    import jax
    import jax.numpy as jnp

    def _L0_xattn_ref(query, context, Wq, Wk, Wv, Wo):
        import jax, jax.numpy as jnp
        import numpy as np
        D_MODEL = 128
        N_HEADS = 16
        D_HEAD = D_MODEL // N_HEADS
        B, T_q, D = query.shape
        T_c = context.shape[1]
        Q = (query @ Wq.T).reshape(B, T_q, N_HEADS, D_HEAD)
        K = (context @ Wk.T).reshape(B, T_c, N_HEADS, D_HEAD)
        V = (context @ Wv.T).reshape(B, T_c, N_HEADS, D_HEAD)
        scale = jnp.sqrt(jnp.asarray(D_HEAD, dtype=query.dtype))
        scores = jnp.einsum('bqhd,bkhd->bhqk', Q, K) / scale
        attn = jax.nn.softmax(scores, axis=-1)
        out = jnp.einsum('bhqk,bkhd->bqhd', attn, V).reshape(B, T_q, D)
        return out @ Wo.T

    def _L0_ffn_ref(x, W_Q, W_K, W_O, W_inv, V_fwd, W_fwd, U_fwd, b_fwd, V_inv, W_inv_exp, U_inv, b_inv, router_w1, router_b1, router_w2, router_b2, alpha_bi, expert_bias):
        import jax, jax.numpy as jnp
        import numpy as np
        B, T, D, R, KEXP = (4, 512, 128, 64, 8)
        RH = max(D, 32)
        SCALE = 0.02

        def _fused_branch(Q_side, K_side, V, W, U, b, router_w1, router_b1, router_w2, router_b2, expert_bias):
            xV = jnp.einsum('btd,kdr->btkr', Q_side, V)
            yW = jnp.einsum('btd,kdr->btkr', K_side, W)
            cum_yW = jnp.cumsum(yW, axis=1)
            prod = xV * cum_yW
            h = jax.nn.gelu(Q_side @ router_w1.T + router_b1, approximate=False)
            logits = h @ router_w2.T + router_b2 + expert_bias
            weights = jax.nn.softmax(logits, axis=-1)
            out = jnp.einsum('btkr,kdr->btd', prod * weights[..., None], U)
            out = out + weights @ b
            n_valid = jnp.arange(1, Q_side.shape[1] + 1, dtype=Q_side.dtype)
            return out / n_valid[None, :, None]
        Q = x @ W_Q.T
        K = x @ W_K.T
        invQ = Q @ W_inv.T
        invK = K @ W_inv.T
        fwd = _fused_branch(Q, K, V_fwd, W_fwd, U_fwd, b_fwd, router_w1, router_b1, router_w2, router_b2, expert_bias)
        inv = _fused_branch(invQ, invK, W_inv_exp, V_inv, U_inv, b_inv, router_w1, router_b1, router_w2, router_b2, expert_bias)
        out = fwd + alpha_bi * inv
        return out @ W_O.T

    def _L1_xattn_ref(iQ, iK, mask, Wq, Wkv, Wo, nbias):
        import jax, jax.numpy as jnp
        import numpy as np
        NUM_HEAD = 16
        ADIM = 64
        IEPS = 1e-32
        MASK_FILL = -1e+32

        def sparse_norm(scores, nbias):
            t = jax.nn.relu(scores + nbias)
            t = t * t
            return t / (t.sum(-1, keepdims=True) + IEPS)
        b, q, _ = iQ.shape
        s = iK.shape[1]
        h, a = (NUM_HEAD, ADIM)
        hsize = h * a
        rq = (iQ @ Wq.T).reshape(b, q, h, a)
        kv = iK @ Wkv.T
        rk = kv[..., :hsize].reshape(b, s, h, a)
        rv = kv[..., hsize:].reshape(b, s, h, a)
        scores = jnp.einsum('bqha,bsha->bhqs', rq, rk) / np.float32(np.sqrt(a))
        scores = jnp.where(mask[:, None, :, :], jnp.float32(MASK_FILL), scores)
        attn = sparse_norm(scores, nbias)
        o = jnp.einsum('bhqs,bsha->bqha', attn, rv).reshape(b, q, hsize)
        return o @ Wo.T

    def _L1_ffn_ref(x, centroids, gamma, beta, W1, b1, W2, b2):
        import jax, jax.numpy as jnp
        import numpy as np
        B, S, D, F, E = (1, 128, 128, 512, 8)
        EPS = 1e-05

        def _sublayer(xs, g, b, W1e, b1e, W2e, b2e):
            mu = jnp.mean(xs, axis=-1, keepdims=True)
            var = jnp.mean(jnp.square(xs - mu), axis=-1, keepdims=True)
            h = (xs - mu) * jax.lax.rsqrt(var + EPS) * g + b
            return xs + jax.nn.relu(h @ W1e.T + b1e) @ W2e.T + b2e
        feats = x.reshape(-1, x.shape[-1])
        scores = jax.lax.stop_gradient(feats @ centroids.T)
        expert = jnp.argmax(scores, axis=1)
        onehot = jax.nn.one_hot(expert, E, dtype=feats.dtype)
        alpha = jax.nn.sigmoid(jnp.sum(feats * centroids[expert], axis=-1, keepdims=True))
        ys = jax.vmap(_sublayer, in_axes=(None, 0, 0, 0, 0, 0, 0))(feats, gamma, beta, W1, b1, W2, b2)
        y = jnp.einsum('te,etd->td', onehot, ys)
        out = alpha * y + (1.0 - alpha) * feats
        return out.reshape(x.shape)

    def _L2_xattn_ref(query, key, value):
        import jax, jax.numpy as jnp
        import numpy as np
        EMBED_DIM = 128
        NUM_HEADS = 16
        HEAD_DIM = EMBED_DIM // NUM_HEADS
        B, Sq, E = query.shape
        Skv = key.shape[1]
        H, D = (NUM_HEADS, HEAD_DIM)
        Q = query.reshape(B, Sq, H, D).transpose(0, 2, 1, 3)
        K = key.reshape(B, Skv, H, D).transpose(0, 2, 1, 3)
        V = value.reshape(B, Skv, H, D).transpose(0, 2, 1, 3)
        scores = jnp.einsum('bhqd,bhkd->bhqk', Q, K) / jnp.sqrt(jnp.asarray(D, Q.dtype))
        weights = jax.nn.softmax(scores, axis=-1)
        out = jnp.einsum('bhqk,bhkd->bhqd', weights, V)
        return out.transpose(0, 2, 1, 3).reshape(B, Sq, E)

    def _L2_ffn_ref(x, kernel, bias, a, b):
        import jax, jax.numpy as jnp
        import numpy as np
        INT4_QMAX = 7.0

        def simulate_quantize_int4(w):
            scale = jnp.max(jnp.abs(w)) / INT4_QMAX
            q = jnp.clip(jnp.round(w / scale), -8.0, 7.0)
            return q * scale
        w = simulate_quantize_int4(kernel)
        y = jnp.einsum('bsd,df->bsf', x, w) + bias
        lora = jnp.einsum('bsr,rf->bsf', jnp.einsum('bsd,dr->bsr', x, a), b)
        return y + lora

    def _L3_xattn_ref(latents, context, ln_l_w, ln_l_b, ln_c_w, ln_c_b, Wq, Wkv, Wo, bo):
        import jax, jax.numpy as jnp
        import numpy as np
        DIM = 128
        H = 16
        D = 64
        INNER = H * D
        EPS = 1e-05

        def layernorm(x, w, b):
            mu = jnp.mean(x, axis=-1, keepdims=True)
            var = jnp.var(x, axis=-1, keepdims=True)
            return (x - mu) * jax.lax.rsqrt(var + EPS) * w + b
        b, n, _ = latents.shape
        s = context.shape[1]
        lat = layernorm(latents, ln_l_w, ln_l_b)
        ctx = layernorm(context, ln_c_w, ln_c_b)
        q = (lat @ Wq).reshape(b, n, H, D).transpose(0, 2, 1, 3)
        kv = ctx @ Wkv
        k, v = jnp.split(kv, 2, axis=-1)
        k = k.reshape(b, s, H, D).transpose(0, 2, 1, 3)
        v = v.reshape(b, s, H, D).transpose(0, 2, 1, 3)
        scale = D ** (-0.5)
        attn = jnp.einsum('bhnd,bhsd->bhns', q, k) * scale
        attn = jnp.clip(attn, -11.0, 11.0)
        attn = jax.nn.softmax(attn, axis=-1)
        out = jnp.einsum('bhns,bhsd->bhnd', attn, v)
        out = out.transpose(0, 2, 1, 3).reshape(b, n, INNER)
        return out @ Wo + bo

    def _L3_ffn_ref(x, gate_w, gate_k, up_k, down_k, sh_gate, sh_up, sh_down):
        import jax, jax.numpy as jnp
        import numpy as np
        E = 8
        K = 2
        D = 128
        F = 512
        FS = 256
        B, S = (2, 128)
        b, s, d = x.shape
        xt = x.reshape(-1, d)
        logits = xt @ gate_w.T
        scores = jax.nn.softmax(logits, axis=-1)
        topk_w, topk_i = jax.lax.top_k(scores, K)
        combine = (jax.nn.one_hot(topk_i, E, dtype=xt.dtype) * topk_w[..., None]).sum(axis=1)
        g = jnp.einsum('nd,edf->enf', xt, gate_k)
        u = jnp.einsum('nd,edf->enf', xt, up_k)
        a = jax.nn.silu(g) * u
        eo = jnp.einsum('enf,efd->end', a, down_k)
        y = jnp.einsum('end,ne->nd', eo, combine)
        shared = jax.nn.silu(xt @ sh_gate) * (xt @ sh_up) @ sh_down
        return (y + shared).reshape(b, s, d)
    x = x + jnp.tanh(g_xattn[0]) * _L0_xattn_ref(_layernorm(x, axis=-1), ctx_1024, L0_xattn_Wq, L0_xattn_Wk, L0_xattn_Wv, L0_xattn_Wo)
    x = x + jnp.tanh(g_ffn[0]) * _L0_ffn_ref(_layernorm(x, axis=-1), L0_ffn_W_Q, L0_ffn_W_K, L0_ffn_W_O, L0_ffn_W_inv, L0_ffn_V_fwd, L0_ffn_W_fwd, L0_ffn_U_fwd, L0_ffn_b_fwd, L0_ffn_V_inv, L0_ffn_W_inv_exp, L0_ffn_U_inv, L0_ffn_b_inv, L0_ffn_router_w1, L0_ffn_router_b1, L0_ffn_router_w2, L0_ffn_router_b2, L0_ffn_alpha_bi, L0_ffn_expert_bias)
    x = x + jnp.tanh(g_xattn[1]) * _L1_xattn_ref(_layernorm(x, axis=-1), ctx_1024, mask_BxSxS2_bk0, L1_xattn_Wq, L1_xattn_Wkv, L1_xattn_Wo, L1_xattn_nbias)
    x = x + jnp.tanh(g_ffn[1]) * _L1_ffn_ref(_layernorm(x, axis=-1), L1_ffn_centroids, L1_ffn_gamma, L1_ffn_beta, L1_ffn_W1, L1_ffn_b1, L1_ffn_W2, L1_ffn_b2)
    x = x + jnp.tanh(g_xattn[2]) * _L2_xattn_ref(_layernorm(x, axis=-1), ctx_1024, ctx_1024)
    x = x + jnp.tanh(g_ffn[2]) * _L2_ffn_ref(_layernorm(x, axis=-1), L2_ffn_kernel, L2_ffn_bias, L2_ffn_a, L2_ffn_b)
    x = x + jnp.tanh(g_xattn[3]) * _L3_xattn_ref(_layernorm(x, axis=-1), ctx_1024, L3_xattn_ln_l_w, L3_xattn_ln_l_b, L3_xattn_ln_c_w, L3_xattn_ln_c_b, L3_xattn_Wq, L3_xattn_Wkv, L3_xattn_Wo, L3_xattn_bo)
    x = x + jnp.tanh(g_ffn[3]) * _L3_ffn_ref(_layernorm(x, axis=-1), L3_ffn_gate_w, L3_ffn_gate_k, L3_ffn_up_k, L3_ffn_down_k, L3_ffn_sh_gate, L3_ffn_sh_up, L3_ffn_sh_down)
    return x

_drawn_inputs = setup_inputs


def setup_inputs(seed=0):
    import zlib

    import numpy as np

    out = dict(_drawn_inputs(seed))
    spreads = {'L0_ffn_b_fwd': (0.0, 0.1),
     'L0_ffn_b_inv': (0.0, 0.1),
     'L0_ffn_router_b1': (0.0, 0.1),
     'L0_ffn_router_b2': (0.0, 0.1),
     'L0_ffn_expert_bias': (0.0, 0.1),
     'L1_ffn_gamma': (1.0, 0.2),
     'L1_ffn_beta': (0.0, 0.1),
     'L1_ffn_b1': (0.0, 0.1),
     'L1_ffn_b2': (0.0, 0.1),
     'L3_xattn_ln_l_w': (1.0, 0.2),
     'L3_xattn_ln_l_b': (0.0, 0.1),
     'L3_xattn_ln_c_w': (1.0, 0.2),
     'L3_xattn_ln_c_b': (0.0, 0.1),
     'L3_xattn_bo': (0.0, 0.1)}
    factors = {}
    for name, (base, spread) in spreads.items():
        noise = np.random.default_rng([zlib.crc32(name.encode()), seed]).standard_normal(out[name].shape)
        drawn = base * np.exp(spread * noise) if base else spread * noise
        out[name] = jnp.asarray(drawn.astype(out[name].dtype))
    for name, factor in factors.items():
        out[name] = (out[name] * factor).astype(out[name].dtype)
    return out
```

```python
from contextlib import ExitStack

import numpy as np

import concourse.bass as bass
from concourse import mybir

F32 = mybir.dt.float32
F32R = mybir.dt.float32r
U8 = mybir.dt.uint8
ALU = mybir.AluOpType
ACT = mybir.ActivationFunctionType
AX = mybir.AxisListType

P = 128
B, S, D = 4, 256, 128
T = B * S
NT = T // P
H = 16
HALF = 512
E = 8
BLK = 32
GH = P // BLK
NG = H // GH
DH8 = D // H
DH = 64
NQ = 4
QW = 4 * DH
NKT = 4
BIG = 3.0e38
EPS = 1e-5
IEPS = 1e-32
CLIP = 11.0
ROUND = 12582912.0

SMALL = {}
N_SMALL = 0
for _name, _width in (
    ("ident", P), ("spread", 2 * P), ("lo_q", 1), ("lo_k", 1), ("one_rows", 1), ("head", GH),
    ("inv_n", 2), ("iota", E), ("gates", 8), ("nbias", 1), ("alpha", 1), ("rb2", E), ("ebias", E),
    ("rb1", 1), ("gamma", E), ("beta", E), ("b1", 4 * E), ("b2", E), ("quant_bias", P),
    ("ln_l_w", 1), ("ln_l_b", 1), ("ln_c_w", 1), ("ln_c_b", 1), ("bo", P),
    ("centroids", E), ("gate_w", E), ("router_w2", E), ("b_experts", P),
    ("W_Q", P), ("W_K", P), ("W_inv", P), ("router_w1", P), ("W_O", P), ("wv0", P), ("wo0", P),
    ("quant_w", P), ("lora_a", P), ("lora_b", P), ("sel_e", E * P),
):
    SMALL[_name] = (N_SMALL, _width)
    N_SMALL += _width
W_A = 2 * P
W_F0 = 4 * P
W_B = 4 * QW
W_F1 = 1024
W_F3 = 1536
W_SH = 768
NF = 4


class Order:

    def __init__(self, eng, sem):
        self.eng, self.sem = eng, sem
        self.base, self.i, self.per, self.local = 0, None, 0, 0

    def loop(self, i, per):
        self.i, self.per, self.local = i, per, 0

    def end(self, passes):
        assert self.local == self.per, (self.local, self.per)
        self.base += passes * self.per
        self.i, self.per, self.local = None, 0, 0

    def done(self, ins):
        ins.then_inc(self.sem, 1)
        if self.i is None:
            self.base += 1
        else:
            self.local += 1
        return ins

    def wait(self):
        self.eng.wait_ge(self.sem, self.base if self.i is None else self.i * self.per + (self.base + self.local))

    def step(self, ins):
        self.done(ins)
        self.wait()


class Signal:

    def __init__(self, sem, per, passes):
        self.sem, self.per, self.passes = sem, per, passes

    def at(self, call, i, k):
        return i * self.per + (call * self.per * self.passes + k)


def build(nc, x, ctx_tok, ctx_t, mask, small, wa0, wf0, wb1, wf1, wa2, wb3, wf3, out):
    stack = ExitStack()
    with stack:
        def sb(name, shape, dt=F32):
            return stack.enter_context(nc.sbuf_tensor(name, shape, dt))

        def sem(name):
            return stack.enter_context(nc.semaphore(name))

        sm = sb("small_operands", [P, N_SMALL])
        res = sb("residual", [P, NT, D])
        xn = sb("normed_tokens", [P, NT, D])
        xf = sb("normed_t", [P, T])
        xh = sb("normed_t_high", [P, T], F32R)
        xl = sb("normed_t_low", [P, T], F32R)
        out_t = sb("sublayer_out_t", [P, T])
        ctok = sb("context_tokens", [P, NT, D])
        ch = sb("context_t_high", [P, T], F32R)
        cl = sb("context_t_low", [P, T], F32R)
        gate = sb("tanh_gates", [P, 8])
        mask_u8 = sb("mask_bytes", [P, 2 * T], U8)
        w_floor_t = sb("score_floor", [P, 1])
        w_floor = w_floor_t[:, :]
        stats = sb("ln_stats", [P, NT, 6])
        mv = sb("ln_mean_var", [P, NT, 2])
        ve = sb("ln_var_eps", [P, NT])
        mhalf = sb("minus_half", [P, NT])
        rs = sb("ln_rstd", [P, NT])
        rt = sb("ln_newton", [P, NT])
        raw_a = sb("raw_a", [P, E * W_F1])
        raw_b = sb("raw_b", [P, E * W_F3 + W_SH])
        RA0, RF0 = 0, NG * W_A
        RB3 = 0
        RB1, RA2, CAP = 0, NQ * W_B, NQ * W_B + NG * W_A
        cap = raw_b[:, CAP:CAP + B * 2 * S].rearrange("p (b k q) -> p b k q", b=B, k=2)
        NWF, NWR = 8192, 9472
        wf = sb("work", [P, NWF])
        wr = sb("work_split", [P, NWR], F32R)

        def col(name, a=0, n=None):
            at, width = SMALL[name]
            return sm[:, at + a:at + (width if n is None else a + n)]

        ident = col("ident")
        ps = stack.enter_context(nc.psum_tensor("banks", [P, 8, HALF], F32))

        def bank(i, n=1):
            return ps[:, i, :] if n == 1 else ps[:, i:i + n, :].rearrange("p a b -> p (a b)")

        def half(t, h):
            return t[:, h * HALF:(h + 1) * HALF]

        def mm3(o, w, m, start=True, stop=True):
            nc.tensor.matmul(o, w[0], m[0], start=start, stop=False)
            nc.tensor.matmul(o, w[0], m[1], start=False, stop=False)
            return nc.tensor.matmul(o, w[1], m[0], start=False, stop=stop)

        ld = {n: sem("loaded_" + n) for n in ("x", "ctx_t", "ctx_tok", "small", "mask", "a0", "f0", "b1", "f1", "a2", "b3", "f3")}
        s_dve = sem("vector_own_steps")
        s_act = sem("scalar_own_steps")
        s_init = sem("constants_ready")
        s_gate = sem("gates_ready")
        s_ctx = sem("context_split")
        s_ve = sem("ln_variance_ready")
        s_pow = sem("ln_power_ready")
        s_xn = sem("ln_tile_ready")
        s_xt = sem("ln_half_transposed")
        s_xf = sem("ln_half_copied")
        s_xs = sem("ln_half_split")
        s_rt = sem("out_half_back")
        s_vp = sem("values_tile_product")
        s_va = sem("values_ready")
        s_out = sem("stored")
        s_res = sem("residual_done")
        s_ot, s_oc = sem("heads_transposed"), sem("heads_copied")

        def signals(prefix, passes, **per):
            return {k: Signal(sem(f"{prefix}_{k}"), n, passes) for k, n in per.items()}

        def norm_dve_tokens(dve, order, n, src, dst):
            if src is xn:
                dve.wait_ge(s_xn, NT * n)
            for t in range(NT):
                order.done(nc.vector.bn_stats(stats[:, t, :], src[:, t, :]))
            order.wait()
            for t in range(NT):
                order.done(nc.vector.bn_aggr(mv[:, t, :], stats[:, t, :]))
            order.wait()
            nc.vector.tensor_scalar(ve[:, :], mv[:, :, 1], EPS, None, ALU.add).then_inc(s_ve, 1)
            dve.wait_ge(s_ve, n + 1)
            dve.wait_ge(s_pow, n + 1)
            order.step(nc.vector.tensor_tensor(rt[:, :], rs[:, :], rs[:, :], ALU.mult))
            order.step(nc.vector.tensor_tensor(rt[:, :], rt[:, :], ve[:, :], ALU.mult))
            order.step(nc.vector.tensor_scalar(rt[:, :], rt[:, :], -0.5, 1.5, ALU.mult, ALU.add))
            order.step(nc.vector.tensor_tensor(rs[:, :], rs[:, :], rt[:, :], ALU.mult))
            for t in range(NT):
                nc.vector.tensor_scalar(dst[:, t, :], src[:, t, :], mv[:, t, 0:1], rs[:, t:t + 1],
                                        ALU.subtract, ALU.mult).then_inc(s_xn, 1)

        def norm_pool(pool, n):
            pool.wait_ge(s_ve, n + 1)
            nc.gpsimd.tensor_tensor(rs[:, :], ve[:, :], mhalf[:, :], ALU.pow).then_inc(s_pow, 1)

        def norm_pe(pe, n, m):
            for h in range(2):
                for t in range(4 * h, 4 * h + 4):
                    pe.wait_ge(s_xn, NT * n + t + 1)
                    last = nc.tensor.transpose(ps[:, 6 + h, (t % 4) * P:(t % 4 + 1) * P], xn[:, t, :], ident)
                last.then_inc(s_xt, 1)

        def norm_act(act, m, w=None, b=None):
            for h in range(2):
                act.wait_ge(s_xt, 2 * m + h + 1)
                act.wait_ge(s_xs, 2 * m)
                if w is None:
                    ins = nc.scalar.activation(half(xf, h), bank(6 + h), ACT.Copy)
                else:
                    ins = nc.scalar.activation(half(xf, h), bank(6 + h), ACT.Identity, bias=b, scale=w)
                ins.then_inc(s_xf, 1)

        def norm_dve_split(dve, order, m, hi, lo):
            for h in range(2):
                dve.wait_ge(s_xf, 2 * m + h + 1)
                order.step(nc.vector.tensor_copy(half(hi, h), half(xf, h)))
                nc.vector.tensor_tensor(half(lo, h), half(xf, h), half(hi, h).bitcast(F32), ALU.subtract).then_inc(s_xs, 1)

        def back_pe(pe):
            for h in range(2):
                for t in range(4):
                    last = nc.tensor.transpose(ps[:, 6 + h, t * P:(t + 1) * P],
                                               out_t[:, (4 * h + t) * P:(4 * h + t + 1) * P], ident)
                last.then_inc(s_rt, 1)

        def tokens_pe(src, w):
            for h in range(2):
                for t in range(4):
                    last = nc.tensor.matmul(ps[:, 6 + h, t * P:(t + 1) * P],
                                            src[:, (4 * h + t) * P:(4 * h + t + 1) * P], w, start=True, stop=True)
                last.then_inc(s_rt, 1)

        def back_dve(dve, order, r, n, signal=None):
            for h in range(2):
                dve.wait_ge(s_rt, 2 * r + h + 1)
                t = res[:, 4 * h:4 * h + 4, :].rearrange("p t d -> p (t d)")
                ins = nc.vector.scalar_tensor_tensor(out=t, in0=bank(6 + h), scalar=gate[:, n:n + 1], in1=t,
                                                     op0=ALU.mult, op1=ALU.add)
                if signal is None:
                    order.done(ins)
                else:
                    ins.then_inc(signal, 1)
            if signal is None:
                order.wait()

        A = signals("a", NG, w=2, q=4, hi=4, y=4, km=4, v=1, mx=8, red=8, m2=2, mt=2, yf=2, s=8, p=8, pv=8,
                    raw=2, rt=2, att=2)
        s_ainit = sem("a_cleared")
        a_y, a_yf, a_ky = wr[:, 0:1024], wr[:, 1024:2048], wr[:, 2048:3072]
        a_km = [wr[:, 3072 + 1024 * j:4096 + 1024 * j] for j in range(GH)]
        a_hi = wr[:, 7168:8192]
        a_wh, a_wl = wr[:, 8192:8448], wr[:, 8448:8704]
        a_vall = wf[:, 0:1024]
        a_vg = wf[:, 1024:2048].rearrange("p (t j c) -> p t j c", t=NT, j=GH)
        a_p = [wf[:, 2048 + 1024 * k:3072 + 1024 * k] for k in range(2)]
        a_m2 = wf[:, 4096:5120].rearrange("p (t j c) -> p t j c", t=NT, j=GH)
        a_raw = wf[:, 5120:6144]
        a_nm = wf[:, 6144:6176].rearrange("p (t j) -> p t j", t=NT)
        a_rec = wf[:, 6176:6208].rearrange("p (t j) -> p t j", t=NT)
        a_att = wf[:, 7168:8192].rearrange("p (t d) -> p t d", t=NT)
        a_att_t = wf[:, 1024:2048]

        def small_pe(pe, c, m):
            pe.wait_ge(s_xs, 2 * m + 2)
            with pe.Fori(0, NG) as i:
                pe.wait_ge(A["w"].sem, A["w"].at(c, i, 2))
                pe.wait_ge(A["att"].sem, A["att"].at(c, i, 0))
                for n in range(4):
                    h, k = n % 2, n // 2
                    if k:
                        pe.wait_ge(A["y"].sem, A["y"].at(c, i, h + 1))
                    w = (a_wh[:, k * P:(k + 1) * P], a_wl[:, k * P:(k + 1) * P])
                    src = (half(ch, h), half(cl, h)) if k else (half(xh, h), half(xl, h))
                    mm3(bank(6 + h), w, src).then_inc(A["q"].sem, 1)
                pe.wait_ge(A["km"].sem, A["km"].at(c, i, 4))
                pe.wait_ge(A["p"].sem, A["p"].at(c, i, 0))
                for u in range(NT):
                    if u >= 2:
                        pe.wait_ge(A["red"].sem, A["red"].at(c, i, u - 1))
                    for j in range(GH):
                        last = nc.tensor.matmul(ps[:, 2 * (u % 2) + j // 2, (j % 2) * S:(j % 2 + 1) * S],
                                                a_y[:, u * P:(u + 1) * P], a_km[j][:, (u // 2) * S:(u // 2 + 1) * S],
                                                start=True, stop=True)
                    last.then_inc(A["mx"].sem, 1)
                for h in range(2):
                    pe.wait_ge(A["m2"].sem, A["m2"].at(c, i, h + 1))
                    for t in range(4):
                        last = nc.tensor.transpose(ps[:, 6 + h, t * P:(t + 1) * P],
                                                   a_m2[:, 4 * h + t, :, :].rearrange("p j c -> p (j c)"), ident)
                    last.then_inc(A["mt"].sem, 1)

                def scores(u):
                    b, kb = u // 2, u % 2
                    if b % 2 == 0 and kb == 0:
                        pe.wait_ge(A["yf"].sem, A["yf"].at(c, i, b // 2 + 1))
                    if u < 2:
                        pe.wait_ge(A["red"].sem, A["red"].at(c, i, 7 + u))
                    else:
                        pe.wait_ge(A["p"].sem, A["p"].at(c, i, u - 1))
                    for j in range(GH):
                        last = nc.tensor.matmul(ps[:, 2 * (u % 2) + j // 2, (j % 2) * S:(j % 2 + 1) * S],
                                                a_km[j][:, b * S + kb * P:b * S + (kb + 1) * P],
                                                a_yf[:, b * S:(b + 1) * S], start=True, stop=True)
                    last.then_inc(A["s"].sem, 1)

                def values(u):
                    b, kb = u // 2, u % 2
                    pe.wait_ge(A["p"].sem, A["p"].at(c, i, u + 1))
                    for j in range(GH):
                        last = nc.tensor.matmul(ps[BLK * j:BLK * (j + 1), 4 + b // 2, (b % 2) * S:(b % 2 + 1) * S],
                                                a_vg[:, u, j, :], a_p[u % 2][:, j * S:(j + 1) * S],
                                                start=kb == 0, stop=kb == 1)
                    last.then_inc(A["pv"].sem, 1)

                def sums_back(h):
                    pe.wait_ge(A["raw"].sem, A["raw"].at(c, i, h + 1))
                    for t in range(4 * h, 4 * h + 4):
                        last = nc.tensor.transpose(ps[:, 6 + h, (t % 4) * P:(t % 4 + 1) * P],
                                                   a_raw[:, t * P:(t + 1) * P], ident)
                    last.then_inc(A["rt"].sem, 1)

                pe.wait_ge(A["v"].sem, A["v"].at(c, i, 1))
                pe.wait_ge(A["raw"].sem, A["raw"].at(c, i, 0))
                pe.wait_ge(A["yf"].sem, A["yf"].at(c, i, 2))
                scores(0)
                scores(1)
                for u in range(8):
                    values(u)
                    if u + 2 < 8:
                        scores(u + 2)
                    if u == 5:
                        sums_back(0)
                sums_back(1)

        def small_act(act, c):
            act.wait_ge(s_ainit, c + 1)
            if c == 0:
                act.wait_ge(s_va, 1)
            else:
                act.wait_ge(ld["ctx_tok"], 16)
            vsrc = a_vall if c == 0 else ctok[:, :, :].rearrange("p t d -> p (t d)")
            vsrc = vsrc.rearrange("p (t d) -> p t d", t=NT)
            with act.Fori(0, NG) as i:
                act.wait_ge(A["pv"].sem, A["pv"].at(c, i, 0))
                nc.scalar.activation(a_vg[:, :, :, 0:DH8],
                                     vsrc[:, :, bass.ds(i * BLK, BLK)].rearrange("p t (j d) -> p t j d", j=GH),
                                     ACT.Copy).then_inc(A["v"].sem, 1)
                act.wait_ge(A["y"].sem, A["y"].at(c, i, 0))
                for n in range(4):
                    act.wait_ge(A["q"].sem, A["q"].at(c, i, n + 1))
                    if n >= 2:
                        act.wait_ge(A["y"].sem, A["y"].at(c, i, n - 1))
                    nc.scalar.activation(half(a_hi, n % 2), bank(6 + n % 2), ACT.Copy).then_inc(A["hi"].sem, 1)

                def sums(h):
                    act.wait_ge(A["pv"].sem, A["pv"].at(c, i, 4 * h + 4))
                    nc.scalar.activation(half(a_raw, h), bank(4 + h), ACT.Copy).then_inc(A["raw"].sem, 1)

                act.wait_ge(A["rt"].sem, A["rt"].at(c, i, 0))
                for u in range(8):
                    act.wait_ge(A["s"].sem, A["s"].at(c, i, u + 1))
                    if u >= 2:
                        act.wait_ge(A["pv"].sem, A["pv"].at(c, i, u - 1))
                    nc.scalar.activation(a_p[u % 2], bank(2 * (u % 2), 2), ACT.Exp,
                                         scale=float(1.0 / np.sqrt(np.float32(DH8)))).then_inc(A["p"].sem, 1)
                    if u == 5:
                        sums(0)
                sums(1)

        def small_dve(dve, order, c, raw, r0, loaded):
            for t in (a_m2, a_vg):
                order.done(nc.vector.memset(t, 0.0))
            order.wait()
            nc.vector.memset(a_vg[:, :, :, DH8:DH8 + 1], 1.0).then_inc(s_ainit, 1)
            dve.wait_ge(loaded, 16)
            with dve.Fori(0, NG) as i:
                order.loop(i, 4)
                dve.wait_ge(A["q"].sem, A["q"].at(c, i, 0))
                wqk = raw[:, bass.ds(i * W_A + r0, 2 * P)]
                nc.vector.tensor_copy(a_wh, wqk).then_inc(A["w"].sem, 1)
                dve.wait_ge(A["w"].sem, A["w"].at(c, i, 1))
                nc.vector.tensor_tensor(a_wl, wqk, a_wh.bitcast(F32), ALU.subtract).then_inc(A["w"].sem, 1)
                dve.wait_ge(A["mx"].sem, A["mx"].at(c, i, 0))
                for n in range(4):
                    dve.wait_ge(A["hi"].sem, A["hi"].at(c, i, n + 1))
                    dst = (a_y, a_ky)[n // 2]
                    nc.vector.scalar_tensor_tensor(out=half(dst, n % 2), in0=half(a_hi, n % 2).bitcast(F32),
                                                   scalar=col(("lo_q", "lo_k")[n // 2]), in1=bank(6 + n % 2),
                                                   op0=ALU.mult, op1=ALU.add).then_inc(A["y"].sem, 1)
                dve.wait_ge(A["y"].sem, A["y"].at(c, i, 4))
                dve.wait_ge(A["s"].sem, A["s"].at(c, i, 0))
                for j in range(GH):
                    nc.vector.tensor_scalar(a_km[j], a_ky.bitcast(F32), col("one_rows"), col("head", j, 1),
                                            ALU.add, ALU.mult).then_inc(A["km"].sem, 1)
                dve.wait_ge(A["mt"].sem, A["mt"].at(c, i, 0))
                for u in range(NT):
                    dve.wait_ge(A["mx"].sem, A["mx"].at(c, i, u + 1))
                    nc.vector.tensor_reduce(a_nm[:, u, :], bank(2 * (u % 2), 2).rearrange("p (j k) -> p j k", j=GH),
                                            AX.X, ALU.max, negate=True).then_inc(A["red"].sem, 1)
                    if u % 4 == 3:
                        h = u // 4
                        dve.wait_ge(A["red"].sem, A["red"].at(c, i, u + 1))
                        nm = a_nm[:, 4 * h:4 * h + 4, :]
                        hi = a_m2[:, 4 * h:4 * h + 4, :, 24]
                        lo = a_m2[:, 4 * h:4 * h + 4, :, 25]
                        order.step(nc.vector.tensor_copy(hi.bitcast(F32R), nm))
                        nc.vector.tensor_tensor(lo.bitcast(F32R), nm, hi, ALU.subtract).then_inc(A["m2"].sem, 1)
                for h in range(2):
                    dve.wait_ge(A["mt"].sem, A["mt"].at(c, i, h + 1))
                    nc.vector.tensor_tensor(half(a_yf, h), bank(6 + h), half(a_y, h).bitcast(F32), ALU.add)\
                        .then_inc(A["yf"].sem, 1)
                for h in range(2):
                    dve.wait_ge(A["rt"].sem, A["rt"].at(c, i, h + 1))
                    sums = bank(6 + h).rearrange("p (t j c) -> p t j c", t=4, j=GH)
                    rec = a_rec[:, 4 * h:4 * h + 4, :]
                    order.step(nc.vector.reciprocal(rec, sums[:, :, :, DH8]))
                    nc.vector.tensor_tensor(
                        a_att[:, 4 * h:4 * h + 4, bass.ds(i * BLK, BLK)].rearrange("p t (j d) -> p t j d", j=GH),
                        sums[:, :, :, 0:DH8], rec.unsqueeze(3).to_broadcast((P, 4, GH, DH8)), ALU.mult)\
                        .then_inc(A["att"].sem, 1)
            order.end(NG)

        def small_out_pe(pe):
            pe.wait_ge(A["att"].sem, A["att"].at(0, NG, 0))
            for h in range(2):
                for t in range(4 * h, 4 * h + 4):
                    last = nc.tensor.transpose(ps[:, h, (t % 4) * P:(t % 4 + 1) * P], a_att[:, t, :], ident)
                last.then_inc(s_ot, 1)
            pe.wait_ge(s_oc, 2)
            tokens_pe(a_att_t, col("wo0"))

        def small_out_act(act):
            for h in range(2):
                act.wait_ge(s_ot, h + 1)
                nc.scalar.activation(half(a_att_t, h), bank(h), ACT.Copy).then_inc(s_oc, 1)

        W = signals("w", NQ, w=3, qk=8, eh=12, el=12, vp=4, va=4, s=8, y=8, p=8, ps=8, pv=8, pvc=4, dn=4,
                    rec=4, rb=4, at=4, o=4, acc=4)
        s_winit = sem("w_cleared")
        w_q = (wr[:, 0:1024], wr[:, 1024:2048])
        w_k = [(wr[:, 2048 + 2048 * h:3072 + 2048 * h], wr[:, 3072 + 2048 * h:4096 + 2048 * h]) for h in range(2)]
        w_w = (wr[:, 6144:6912], wr[:, 6912:7680])
        w_v = wf[:, 0:2048].rearrange("p (t c) -> p t c", t=NT)
        w_p = [wf[:, 2048 + 1024 * k:3072 + 1024 * k] for k in range(3)]
        w_ps = [wf[:, 5120 + 512 * k:5632 + 512 * k] for k in range(2)]
        w_pv, w_at, w_rec, w_wo = wf[:, 6144:6656], wf[:, 6656:7168], wf[:, 7168:7424], wf[:, 7424:7680]
        w_den, w_ones = wf[:, 7680:7936], wf[:, 7936:7968]

        def wide_pe(pe, c, m):
            pe.wait_ge(s_xs, 2 * m + 2)
            pe.wait_ge(s_winit, c + 1)
            with pe.Fori(0, NQ) as i:
                def at(name, k):
                    pe.wait_ge(W[name].sem, W[name].at(c, i, k))

                def project(k):
                    p, h = k // 2, k % 2
                    for n in range(2):
                        at("el", 3 * (k - 1) + (1, 3)[n] if k else 0)
                        w = [t[:, n * QW + p * P:n * QW + (p + 1) * P] for t in w_w]
                        src = (half(ch, h), half(cl, h)) if n else (half(xh, h), half(xl, h))
                        if k == 1:
                            at("va", 3 + n)
                        mm3(bank(6 + n), w, src).then_inc(W["qk"].sem, 1)

                def scores(g):
                    b = g % 4
                    if b % 2 == 0:
                        at("el", 3 * (g // 2) + 3)
                    if g < 2:
                        at("y", 0)
                    else:
                        at("y", g - 1)
                    for h in range(2):
                        for kb in range(2):
                            keys = slice(b * S + kb * P, b * S + (kb + 1) * P)
                            last = mm3(ps[:, 2 * (g % 2) + h, kb * S:(kb + 1) * S], [t[:, keys] for t in w_k[h]],
                                       [t[:, b * S:(b + 1) * S] for t in w_q])
                    last.then_inc(W["s"].sem, 1)

                def values(g):
                    b, p = g % 4, g // 4
                    at("p", g + 1)
                    if g % 2 == 0:
                        at("pvc", g // 2)
                    for kb in range(2):
                        for h in range(2):
                            last = nc.tensor.matmul(ps[DH * h:DH * (h + 1), 4, (b % 2) * S:(b % 2 + 1) * S],
                                                    w_v[:, 2 * b + kb, (2 * p + h) * DH:(2 * p + h + 1) * DH],
                                                    w_p[g % 3][:, (2 * h + kb) * S:(2 * h + kb + 1) * S],
                                                    start=kb == 0, stop=kb == 1)
                    last.then_inc(W["pv"].sem, 1)

                def denominators(k):
                    at("at", k)
                    at("ps", 2 * k + 2)
                    for h in range(2):
                        for b in range(2):
                            r = BLK * (2 * h + b)
                            last = nc.tensor.matmul(ps[r:r + BLK, 5, 0:S], w_ones, w_ps[b][:, h * S:(h + 1) * S],
                                                    start=True, stop=True)
                    last.then_inc(W["dn"].sem, 1)

                def spread(k):
                    at("rec", k + 1)
                    for b in range(2):
                        last = nc.tensor.matmul(ps[:, 5, b * S:(b + 1) * S], col("spread", b * P, P), w_rec,
                                                start=True, stop=True)
                    last.then_inc(W["rb"].sem, 1)

                def output(k):
                    at("at", k + 1)
                    at("el", 10)
                    at("acc", k)
                    for t in range(4):
                        last = nc.tensor.matmul(ps[:, 6, t * P:(t + 1) * P], w_at[:, t * P:(t + 1) * P],
                                                w_wo[:, (k // 2) * P:(k // 2 + 1) * P], start=True, stop=True)
                    last.then_inc(W["o"].sem, 1)

                at("w", 3)
                at("acc", 0)
                project(0)
                for n in range(4):
                    if n < 2:
                        at("el", (1, 3)[n])
                    else:
                        at("va", n - 1)
                    for t in range(2):
                        tile = slice((2 * n + t) * P, (2 * n + t + 1) * P)
                        last = mm3(ps[:, 6 + n % 2, t * QW:(t + 1) * QW], (ch[:, tile], cl[:, tile]),
                                   [v[:, 2 * QW:3 * QW] for v in w_w])
                    last.then_inc(W["vp"].sem, 1)
                project(1)
                scores(0)
                scores(1)
                for g in range(8):
                    k = g // 2
                    if g % 2 == 0 and k + 2 < 4:
                        project(k + 2)
                    if g == 0:
                        at("va", 4)
                    values(g)
                    if g % 2 == 0 and k >= 1:
                        spread(k - 1)
                    if g + 2 < 8:
                        scores(g + 2)
                    if g % 2 == 1:
                        denominators(k)
                        if k >= 1:
                            output(k - 1)
                spread(3)
                output(3)

        def wide_act(act, c, func, bias):
            with act.Fori(0, NQ) as i:
                def at(name, k):
                    act.wait_ge(W[name].sem, W[name].at(c, i, k))

                def high(k):
                    p, h = k // 2, k % 2
                    at("s", max(0, 2 * k - 2))
                    at("qk", 2 * k + 1)
                    nc.scalar.activation(half(w_q[0], h), bank(6), ACT.Copy).then_inc(W["eh"].sem, 1)
                    at("qk", 2 * k + 2)
                    for j in range(2):
                        rows = slice(DH * j, DH * (j + 1))
                        nc.scalar.activation(half(w_k[j][0], h)[rows, :], ps[rows, 7, :], ACT.Copy)\
                            .then_inc(W["eh"].sem, 1)

                def sums(k):
                    at("pv", 2 * k + 2)
                    at("at", k)
                    nc.scalar.activation(w_pv, bank(4), ACT.Copy).then_inc(W["pvc"].sem, 1)

                high(0)
                at("pv", 0)
                for n in range(4):
                    at("vp", n + 1)
                    nc.scalar.activation(w_v[:, 2 * n:2 * n + 2, :].rearrange("p t c -> p (t c)"),
                                         bank(6 + n % 2), ACT.Copy).then_inc(W["va"].sem, 1)
                high(1)
                for g in range(8):
                    k = g // 2
                    at("y", g + 1)
                    nc.scalar.activation(w_p[g % 3], w_p[g % 3], func, bias=bias, scale=0.125)\
                        .then_inc(W["p"].sem, 1)
                    if g % 2 == 0 and k + 2 < 4:
                        high(k + 2)
                    if g % 2 == 0 and k >= 1:
                        sums(k - 1)
                sums(3)

        def wide_pool(pool, c):
            with pool.Fori(0, NQ) as i:
                for g in range(8):
                    pool.wait_ge(W["p"].sem, W["p"].at(c, i, g + 1))
                    pool.wait_ge(W["dn"].sem, W["dn"].at(c, i, g // 2))
                    v = w_p[g % 3].rearrange("p (h k q) -> p h k q", h=2, k=2)
                    nc.gpsimd.tensor_tensor(w_ps[g % 2].rearrange("p (h q) -> p h q", h=2), v[:, :, 0, :],
                                            v[:, :, 1, :], ALU.add).then_inc(W["ps"].sem, 1)

        def wide_dve(dve, order, c, raw, r0, loaded):
            for j in range(2):
                rows = slice(DH * (1 - j), DH * (2 - j))
                for t in w_k[j]:
                    nc.vector.memset(t[rows, :].bitcast(F32), 0.0)
            nc.vector.memset(w_ones, 1.0).then_inc(s_winit, 1)
            dve.wait_ge(s_winit, c + 1)
            dve.wait_ge(loaded, 16)
            with dve.Fori(0, NQ) as i:
                order.loop(i, 4 if c == 0 else 0)

                def at(name, k):
                    dve.wait_ge(W[name].sem, W[name].at(c, i, k))

                def low(k):
                    h = k % 2
                    at("eh", 3 * k + 1)
                    nc.vector.tensor_tensor(half(w_q[1], h), bank(6), half(w_q[0], h).bitcast(F32), ALU.subtract)\
                        .then_inc(W["el"].sem, 1)
                    at("eh", 3 * k + 3)
                    for j in range(2):
                        rows = slice(DH * j, DH * (j + 1))
                        nc.vector.tensor_tensor(half(w_k[j][1], h)[rows, :], ps[rows, 7, :],
                                                half(w_k[j][0], h)[rows, :].bitcast(F32), ALU.subtract)\
                            .then_inc(W["el"].sem, 1)

                def bound(g):
                    at("s", g + 1)
                    if g < 3:
                        at("pv", 0)
                        at("ps", 0)
                    else:
                        at("pv", g - 2)
                        at("ps", g - 2)
                    v = w_p[g % 3].rearrange("p (h c) -> p h c", h=2)
                    s = ps[:, 2 * (g % 2):2 * (g % 2) + 2, :]
                    if c == 0:
                        ins = nc.vector.scalar_tensor_tensor(
                            out=v, in0=s, scalar=w_floor, op0=ALU.max, op1=ALU.min,
                            in1=cap[:, g % 4, :, :].rearrange("p k q -> p (k q)").unsqueeze(1).to_broadcast((P, 2, HALF)))
                    else:
                        ins = nc.vector.tensor_scalar(v, s, -8.0 * CLIP, 8.0 * CLIP, ALU.max, ALU.min)
                    ins.then_inc(W["y"].sem, 1)

                def reciprocal(k):
                    at("dn", k + 1)
                    at("rb", k)
                    if c == 0:
                        order.step(nc.vector.tensor_scalar(w_den, ps[:, 5, 0:S], IEPS, None, ALU.add))
                        nc.vector.reciprocal(w_rec, w_den).then_inc(W["rec"].sem, 1)
                    else:
                        nc.vector.reciprocal(w_rec, ps[:, 5, 0:S]).then_inc(W["rec"].sem, 1)

                def normalise(k):
                    at("rb", k + 1)
                    at("pvc", k + 1)
                    at("o", k)
                    nc.vector.tensor_tensor(w_at, w_pv, bank(5), ALU.mult).then_inc(W["at"].sem, 1)

                def add(k):
                    at("o", k + 1)
                    h = k % 2
                    at("acc", max(0, k - 1))
                    r = xn[:, 4 * h:4 * h + 4, :].rearrange("p t d -> p (t d)")
                    nc.vector.tensor_tensor(r, r, bank(6), ALU.add).then_inc(W["acc"].sem, 1)

                at("vp", 0)
                at("qk", 0)
                at("o", 0)
                qkv = raw[:, bass.ds(i * W_B + r0, 3 * QW)]
                nc.vector.tensor_copy(w_w[0], qkv).then_inc(W["w"].sem, 1)
                nc.vector.tensor_copy(w_wo, raw[:, bass.ds(i * W_B + (r0 + 3 * QW), QW)]).then_inc(W["w"].sem, 1)
                at("w", 1)
                nc.vector.tensor_tensor(w_w[1], qkv, w_w[0].bitcast(F32), ALU.subtract).then_inc(W["w"].sem, 1)
                at("s", 0)
                low(0)
                low(1)
                bound(0)
                bound(1)
                low(2)
                bound(2)
                bound(3)
                reciprocal(0)
                low(3)
                for k in range(4):
                    if 2 * k + 4 < 8:
                        bound(2 * k + 4)
                    normalise(k)
                    if 2 * k + 5 < 8:
                        bound(2 * k + 5)
                    if k < 3:
                        reciprocal(k + 1)
                    add(k)
            order.end(NQ)

        def tokens_in(dve, order, n, src):
            for h in range(2):
                r = res[:, 4 * h:4 * h + 4, :].rearrange("p t d -> p (t d)")
                s = src[:, 4 * h:4 * h + 4, :].rearrange("p t d -> p (t d)")
                order.done(nc.vector.scalar_tensor_tensor(out=r, in0=s, scalar=gate[:, n:n + 1], in1=r,
                                                          op0=ALU.mult, op1=ALU.add))
            order.wait()

        def pick_max(order, oh, s, t1, m):
            order.step(nc.vector.tensor_reduce(m, s, AX.X, ALU.max))
            mb = m.unsqueeze(2).to_broadcast((P, NT, E))
            order.step(nc.vector.tensor_tensor(t1, s, mb, ALU.is_equal))
            iota = col("iota").unsqueeze(1).to_broadcast((P, NT, E))
            order.step(nc.vector.tensor_scalar(t1, t1, -float(E), None, ALU.mult))
            order.step(nc.vector.tensor_tensor(t1, t1, iota, ALU.add))
            order.step(nc.vector.tensor_reduce(m2col, t1, AX.X, ALU.min))
            order.step(nc.vector.tensor_tensor(oh, t1, m2col.unsqueeze(2).to_broadcast((P, NT, E)), ALU.is_equal))

        def split_stack(order, w, at, last=False):
            hi, lo = stk[:, :, at:at + E], stk[:, :, at + E:at + 2 * E]
            order.step(nc.vector.tensor_copy(hi.bitcast(F32R), w))
            ins = nc.vector.tensor_tensor(lo.bitcast(F32R), w, hi, ALU.subtract)
            if last:
                ins.then_inc(s_st, 1)
            else:
                order.step(ins)

        sp_ = [sb(f"router_{k}", [P, NT, E]) for k in range(5)]
        lg, ex, t1, oh, oh2 = [t[:, :, :] for t in sp_]
        mcol_t, m2col_t, rcol_t = sb("router_max", [P, NT]), sb("router_first", [P, NT]), sb("router_sum", [P, NT])
        mcol, m2col, rcol = mcol_t[:, :], m2col_t[:, :], rcol_t[:, :]
        stk_t = sb("router_stack", [P, NT, BLK])
        stk = stk_t[:, :, :]
        s_lg, s_lx, s_le, s_st, s_sk, s_wt = [sem(n) for n in (
            "logits_product", "logits_less_max", "logits_exponentials", "stack_ready", "stack_transposed", "stack_copied")]

        def softmax_dve(dve, order, n):
            order.step(nc.vector.tensor_reduce(mcol, lg, AX.X, ALU.max))
            nc.vector.tensor_tensor(lg, lg, mcol.unsqueeze(2).to_broadcast((P, NT, E)), ALU.subtract).then_inc(s_lx, 1)
            dve.wait_ge(s_le, n + 1)
            order.step(nc.vector.tensor_reduce(rcol, ex, AX.X, ALU.add))
            order.step(nc.vector.reciprocal(rcol, rcol))
            order.step(nc.vector.tensor_tensor(ex, ex, rcol.unsqueeze(2).to_broadcast((P, NT, E)), ALU.mult))

        def softmax_act(act, n, scale=1.0):
            act.wait_ge(s_lx, n + 1)
            nc.scalar.activation(ex, lg, ACT.Exp, scale=scale).then_inc(s_le, 1)

        def logits_pe(src, w, k):
            for t in range(NT):
                last = nc.tensor.matmul(ps[:, k, t * E:(t + 1) * E], src[:, t * P:(t + 1) * P], w, start=True, stop=True)
            last.then_inc(s_lg, 1)

        def stack_pe(pe, n):
            pe.wait_ge(s_st, n + 1)
            for t in range(NT):
                last = nc.tensor.transpose(ps[0:BLK, 6 + t // 4, (t % 4) * P:(t % 4 + 1) * P], stk[:, t, :], ident)
            last.then_inc(s_sk, 1)

        def stack_act(act, n, wt):
            act.wait_ge(s_sk, n + 1)
            nc.scalar.activation(wt[0:BLK, :], ps[0:BLK, 6:8, :].rearrange("p a b -> p (a b)"), ACT.Copy).then_inc(s_wt, 1)

        F = signals("f0", NKT, w=8, x=4, yw=4, xs=4, z=4, u=4, acc=4)
        s_fp, s_fh, s_fl, s_fc, s_fb, s_fo = [sem("f0_" + n) for n in ("product", "high", "low", "sums_split", "bias", "whole")]
        f_slots = [(wr[:, 1024 * 2 * k:1024 * (2 * k + 1)], wr[:, 1024 * (2 * k + 1):1024 * (2 * k + 2)]) for k in range(3)]
        f_q, f_k, f_ik = f_slots
        f_iq = (xh[:, :], xl[:, :])
        f_wt = wr[:, 6144:7168]
        f_w = (wr[:, 7168:7680], wr[:, 7680:8192])
        f_vw = [(wr[:, 8192 + 640 * b:8448 + 640 * b], wr[:, 8448 + 640 * b:8704 + 640 * b]) for b in range(2)]
        f_sel = [wr[:, 8704 + 640 * b:8832 + 640 * b] for b in range(2)]
        f_cum = wf[:, 0:1024]
        f_xs = [wf[:, 1024 + 512 * k:1536 + 512 * k] for k in range(2)]
        f_z = [wf[:, 2048 + 512 * k:2560 + 512 * k] for k in range(2)]
        f_u = [wf[:, 3072 + 128 * k:3200 + 128 * k] for k in range(2)]
        f_ones = wf[:, 3328:3584]
        f_h = [wf[:, 4096 + 1024 * k:5120 + 1024 * k] for k in range(2)]
        f_zz = [wf[:, 6144 + 512 * k:6656 + 512 * k] for k in range(2)]
        f_steps = ((0, "x", f_q), (1, "cum", f_k), (2, "q", f_iq), (2, "k", f_ik), (3, "q", None), (3, "iq", None))

        def f0_pe(pe, m):
            pe.wait_ge(s_xs, 2 * m + 2)
            pe.wait_ge(s_fc, 1)
            src = {"x": (xh[:, :], xl[:, :]), "cum": f_ik, "q": f_q, "k": f_k, "iq": f_iq}
            low = {2: 1, 3: 2, 4: 1, 5: 3}
            for j, (w, s, _) in enumerate(f_steps):
                if j in low:
                    pe.wait_ge(s_fl, low[j])
                if j >= 3:
                    pe.wait_ge(s_fl, j - 2)
                for h in range(2):
                    last = mm3(bank(2 * (j % 3) + h), [v[:, w * P:(w + 1) * P] for v in f_w],
                               [half(v, h) for v in src[s]])
                last.then_inc(s_fp, 1)
            for br in range(2):
                pe.wait_ge(s_fh, 5 + br)
                logits_pe(f_h[br], col("router_w2"), 6 + br)
            stack_pe(pe, 0)
            pe.wait_ge(s_wt, 1)
            pe.wait_ge(s_fl, 4)
            with pe.Fori(0, NKT) as i:
                def at(name, k):
                    pe.wait_ge(F[name].sem, F[name].at(0, i, k))

                def products(n):
                    br, h = n // 2, n % 2
                    if h == 0:
                        at("w", 4 * br + 4)
                    at("xs", max(0, n - 1))
                    at("z", max(0, n - 1))
                    q, k = ((f_q, f_k), (f_iq, f_ik))[br]
                    mm3(bank(h), [v[:, 0:P] for v in f_vw[br]], [half(v, h) for v in q]).then_inc(F["x"].sem, 1)
                    mm3(bank(2 + h), [v[:, P:2 * P] for v in f_vw[br]], [half(v, h) for v in k])
                    nc.tensor.matmul(bank(4 + h), f_sel[br], half(f_wt, h), start=True, stop=True)\
                        .then_inc(F["yw"].sem, 1)

                def out(n):
                    br, h = n // 2, n % 2
                    at("z", n + 1)
                    at("acc", max(0, n - 1))
                    nc.tensor.matmul(bank(6 + h), f_u[br], f_zz[h], start=True, stop=True).then_inc(F["u"].sem, 1)

                products(0)
                products(1)
                for n in range(4):
                    out(n)
                    if n + 2 < 4:
                        products(n + 2)
            pe.wait_ge(F["acc"].sem, F["acc"].at(0, NKT, 0))
            for h in range(2):
                last = nc.tensor.matmul(bank(6 + h), col("b_experts"), half(f_wt, h).bitcast(F32), start=True, stop=True)
            last.then_inc(s_fb, 1)
            pe.wait_ge(s_fo, 1)
            tokens_pe(out_t, col("W_O"))

        def f0_act(act):
            for j, (_, _, dst) in enumerate(f_steps):
                act.wait_ge(s_fp, j + 1)
                if dst is None:
                    ins = nc.scalar.activation(f_h[j - 4], bank(2 * (j % 3), 2), ACT.Gelu, bias=col("rb1"))
                else:
                    ins = nc.scalar.activation(dst[0], bank(2 * (j % 3), 2), ACT.Copy)
                ins.then_inc(s_fh, 1)
            for br in range(2):
                softmax_act(act, br)
            stack_act(act, 0, f_wt)
            with act.Fori(0, NKT) as i:
                for n in range(4):
                    act.wait_ge(F["x"].sem, F["x"].at(0, i, n + 1))
                    act.wait_ge(F["z"].sem, F["z"].at(0, i, max(0, n - 1)))
                    nc.scalar.activation(f_xs[n % 2], bank(n % 2), ACT.Copy).then_inc(F["xs"].sem, 1)

        def f0_dve(dve, order):
            order.done(nc.vector.memset(f_ones, 1.0))
            order.done(nc.vector.memset(out_t[:, :], 0.0))
            order.done(nc.vector.memset(f_wt.bitcast(F32), 0.0))
            order.done(nc.vector.memset(stk, 0.0))
            order.step(nc.vector.tensor_copy(f_w[0], col("W_Q", 0, 4 * P)))
            for b in range(B):
                order.done(nc.vector.tensor_tensor_scan(f_cum[:, b * S:(b + 1) * S], f_ones, xf[:, b * S:(b + 1) * S],
                                                        0.0, ALU.mult, ALU.add))
            order.step(nc.vector.tensor_tensor(f_w[1], col("W_Q", 0, 4 * P), f_w[0].bitcast(F32), ALU.subtract))
            order.step(nc.vector.tensor_copy(f_ik[0], f_cum))
            nc.vector.tensor_tensor(f_ik[1], f_cum, f_ik[0].bitcast(F32), ALU.subtract).then_inc(s_fc, 1)
            for j in range(4):
                dve.wait_ge(s_fh, j + 1)
                dst = f_steps[j][2]
                nc.vector.tensor_tensor(dst[1], bank(2 * (j % 3), 2), dst[0].bitcast(F32), ALU.subtract).then_inc(s_fl, 1)
            for br in range(2):
                dve.wait_ge(s_lg, br + 1)
                src = ps[:, 6 + br, 0:NT * E].rearrange("p (t e) -> p t e", t=NT)
                order.step(nc.vector.tensor_tensor(lg, src, col("rb2").unsqueeze(1).to_broadcast((P, NT, E)), ALU.add))
                order.step(nc.vector.tensor_tensor(lg, lg, col("ebias").unsqueeze(1).to_broadcast((P, NT, E)), ALU.add))
                softmax_dve(dve, order, br)
                e2 = ex.rearrange("p (b q) e -> p b q e", b=B)
                for q in range(2):
                    order.done(nc.vector.tensor_scalar(e2[:, :, q, :], e2[:, :, q, :], col("inv_n", q, 1), None, ALU.mult))
                order.wait()
                if br:
                    order.step(nc.vector.tensor_scalar(ex, ex, col("alpha"), None, ALU.mult))
                split_stack(order, ex, 2 * E * br, br == 1)
            dve.wait_ge(ld["f0"], 16)
            dve.wait_ge(s_wt, 1)
            with dve.Fori(0, NKT) as i:
                order.loop(i, 4)

                def at(name, k):
                    dve.wait_ge(F[name].sem, F[name].at(0, i, k))

                def weights(br):
                    at("yw", 0)
                    at("u", 0)
                    base = i * (2 * W_F0) + (RF0 + br * W_F0)
                    vw = raw_a[:, bass.ds(base, 2 * P)]
                    nc.vector.tensor_copy(f_vw[br][0], vw).then_inc(F["w"].sem, 1)
                    nc.vector.tensor_copy(f_u[br], raw_a[:, bass.ds(base + 2 * P, P)]).then_inc(F["w"].sem, 1)
                    nc.vector.tensor_copy(f_sel[br], raw_a[:, bass.ds(base + 3 * P, P)]).then_inc(F["w"].sem, 1)
                    at("w", 4 * br + 1)
                    nc.vector.tensor_tensor(f_vw[br][1], vw, f_vw[br][0].bitcast(F32), ALU.subtract)\
                        .then_inc(F["w"].sem, 1)

                def weigh(n):
                    h = n % 2
                    at("xs", n + 1)
                    at("yw", n + 1)
                    order.step(nc.vector.tensor_tensor(f_z[h], f_xs[h], bank(2 + h), ALU.mult))
                    at("u", max(0, n - 1))
                    nc.vector.tensor_tensor(f_zz[h], f_z[h], bank(4 + h), ALU.mult).then_inc(F["z"].sem, 1)

                def add(n):
                    h = n % 2
                    at("u", n + 1)
                    at("acc", max(0, n - 1))
                    nc.vector.tensor_tensor(half(out_t, h), half(out_t, h), bank(6 + h), ALU.add)\
                        .then_inc(F["acc"].sem, 1)

                weights(0)
                weights(1)
                weigh(0)
                weigh(1)
                for n in range(4):
                    add(n)
                    if n + 2 < 4:
                        weigh(n + 2)
            order.end(NKT)
            dve.wait_ge(F["acc"].sem, F["acc"].at(0, NKT, 0))
            dve.wait_ge(s_fb, 1)
            nc.vector.tensor_tensor(out_t[:, :], out_t[:, :], bank(6, 2), ALU.add).then_inc(s_fo, 1)

        G = signals("f1", E // 2, w=10, up=16, a=16, al=16, dn=16, cb=2, cc=2, t=4, acc=4)
        s_gb, s_gi = sem("f1_bias_product"), sem("f1_ready")
        g_w = [(wr[:, 2048 * s:2048 * s + 1024], wr[:, 2048 * s + 1024:2048 * s + 2048]) for s in range(2)]
        g_a = [(wr[:, 4096 + 1024 * k:4608 + 1024 * k], wr[:, 4608 + 1024 * k:5120 + 1024 * k]) for k in range(4)]
        g_wt = wr[:, 8192:9216]
        g_sel = [wr[:, 9216 + 128 * k:9344 + 128 * k] for k in range(2)]
        g_af = [wf[:, 4096 + 512 * k:4608 + 512 * k] for k in range(4)]
        g_cw = wf[:, 1024:2048]
        g_t = [wf[:, 2048 + 512 * k:2560 + 512 * k] for k in range(2)]
        g_shift = wf[:, 3072:3072 + E * NF]
        g_b1 = [wf[:, 3104 + NF * k:3104 + NF * (k + 1)] for k in range(2)]
        PASSES = E // 2

        def passes(eng, body):
            with eng.Fori(0, PASSES - 1) as i:
                body(i, False)
            body(PASSES - 1, True)

        def f1_pe(pe, m):
            pe.wait_ge(s_xf, 2 * m + 2)
            logits_pe(xf, col("centroids"), 5)
            pe.wait_ge(ld["f1"], 16)
            for e in range(E):
                for f in range(NF):
                    last = nc.tensor.matmul(ps[:, 4, e * NF + f:e * NF + f + 1],
                                            raw_a[:, e * W_F1 + f * P:e * W_F1 + (f + 1) * P], col("beta", e, 1),
                                            start=True, stop=True)
            last.then_inc(s_gb, 1)
            stack_pe(pe, 1)
            pe.wait_ge(s_wt, 2)
            pe.wait_ge(s_gi, 1)
            pe.wait_ge(s_xs, 2 * m + 2)

            def up(i, n):
                s, h, f = n // 8, n // 4 % 2, n % 4
                if n % 8 == 0:
                    pe.wait_ge(G["w"].sem, G["w"].at(0, i, 5 * s + 5))
                pe.wait_ge(G["a"].sem, G["a"].at(0, i, max(0, n - 2)))
                mm3(ps[:, (0, 1, 2, 7)[n % 4], :], [v[:, f * P:(f + 1) * P] for v in g_w[s % 2]],
                    (half(xh, h), half(xl, h))).then_inc(G["up"].sem, 1)

            def body(i, last_pass):
                def at(name, k):
                    pe.wait_ge(G[name].sem, G[name].at(0, i, k))

                def down(n):
                    s, h, f = n // 8, n // 4 % 2, n % 4
                    at("al", n + 1)
                    if f == 0:
                        at("t", max(0, 2 * (s - 1) + h + 1) if s else 0)
                    last = mm3(bank(3 + h), [v[:, 512 + f * P:512 + (f + 1) * P] for v in g_w[s]], g_a[n % 4],
                               start=f == 0, stop=f == NF - 1)
                    last.then_inc(G["dn"].sem, 1)

                for n in range(16):
                    if n + 2 < 16 or not last_pass:
                        up(i, n + 2)
                    if n % 8 == 3:
                        s = n // 8
                        at("cc", s)
                        for h in range(2):
                            last = nc.tensor.matmul(bank(5 + h), g_sel[s], half(g_wt, h), start=True, stop=True)
                        last.then_inc(G["cb"].sem, 1)
                    down(n)

            up(0, 0)
            up(0, 1)
            passes(pe, body)
            pe.wait_ge(G["acc"].sem, G["acc"].at(0, PASSES, 0))
            back_pe(pe)

        def f1_act(act):
            softmax_act(act, 2, scale=-1.0)
            stack_act(act, 1, g_wt)
            act.wait_ge(s_gi, 1)

            def body(i, last_pass):
                def at(name, k):
                    act.wait_ge(G[name].sem, G[name].at(0, i, k))

                for n in range(16):
                    s, f = n // 8, n % 4
                    at("up", n + 1)
                    at("al", max(0, n - 3))
                    at("dn", max(0, n - 3))
                    b, hidden = g_b1[s][:, f:f + 1], bank((0, 1, 2, 7)[n % 4])
                    nc.scalar.activation(g_af[n % 4], hidden, ACT.Relu, bias=b).then_inc(s_act, 1)
                    nc.scalar.activation(g_a[n % 4][0], hidden, ACT.Relu, bias=b).then_inc(G["a"].sem, 1)
                    if n % 8 == 3:
                        at("cb", s + 1)
                        at("t", 2 * s)
                        nc.scalar.activation(g_cw, bank(5, 2), ACT.Copy).then_inc(G["cc"].sem, 1)

            passes(act, body)

        def f1_pool(pool):
            pool.wait_ge(s_gi, 1)

            def body(i, last_pass):
                for n in range(4):
                    h = n % 2
                    pool.wait_ge(G["t"].sem, G["t"].at(0, i, n + 1))
                    pool.wait_ge(G["acc"].sem, G["acc"].at(0, i, max(0, n - 1)))
                    nc.gpsimd.tensor_tensor(half(out_t, h), half(out_t, h), g_t[h], ALU.add).then_inc(G["acc"].sem, 1)

            passes(pool, body)

        def f1_dve(dve, order):
            dve.wait_ge(s_lg, 3)
            order.step(nc.vector.tensor_copy(lg, ps[:, 5, 0:NT * E].rearrange("p (t e) -> p t e", t=NT)))
            pick_max(order, oh, lg, t1, mcol)
            nc.vector.tensor_copy(lg, mcol.unsqueeze(2).to_broadcast((P, NT, E))).then_inc(s_lx, 1)
            dve.wait_ge(s_le, 3)
            order.step(nc.vector.tensor_scalar(ex, ex, 1.0, None, ALU.add))
            order.step(nc.vector.reciprocal(ex, ex))
            order.step(nc.vector.tensor_tensor(ex, ex, oh, ALU.mult))
            order.step(nc.vector.memset(stk, 0.0))
            order.step(nc.vector.memset(g_wt.bitcast(F32), 0.0))
            split_stack(order, ex, 0, True)
            dve.wait_ge(s_gb, 1)
            order.step(nc.vector.tensor_copy(g_shift, ps[:, 4, 0:E * NF]))
            nc.vector.memset(out_t[:, :], 0.0).then_inc(s_gi, 1)

            def piece(i, s, k):
                def expert(base, n):
                    return sm[:, bass.ds(i * (2 * n) + (s * n + SMALL[base][0]), n)]

                w1 = raw_a[:, bass.ds(i * (2 * W_F1) + s * W_F1, 512)]
                w2 = raw_a[:, bass.ds(i * (2 * W_F1) + (s * W_F1 + 512), 512)]
                (hi, lo), gam = g_w[s], expert("gamma", 1)
                if k == 0:
                    ins = nc.vector.tensor_scalar(hi[:, 0:512], w1, gam, None, ALU.mult)
                elif k == 1:
                    ins = nc.vector.tensor_copy(hi[:, 512:1024], w2)
                elif k == 2:
                    dve.wait_ge(G["w"].sem, G["w"].at(0, i, 5 * s + 1))
                    ins = nc.vector.scalar_tensor_tensor(out=lo[:, 0:512], in0=w1, scalar=gam,
                                                         in1=hi[:, 0:512].bitcast(F32), op0=ALU.mult, op1=ALU.subtract)
                elif k == 3:
                    dve.wait_ge(G["w"].sem, G["w"].at(0, i, 5 * s + 2))
                    ins = nc.vector.tensor_tensor(lo[:, 512:1024], w2, hi[:, 512:1024].bitcast(F32), ALU.subtract)
                else:
                    nc.vector.tensor_tensor(g_b1[s], g_shift[:, bass.ds(i * (2 * NF) + s * NF, NF)], expert("b1", NF), ALU.add)
                    ins = nc.vector.tensor_copy(g_sel[s], expert("sel_e", P))
                ins.then_inc(G["w"].sem, 1)

            for k in range(5):
                piece(0, 0, k)

            def body(i, last_pass):
                def at(name, k):
                    dve.wait_ge(G[name].sem, G[name].at(0, i, k))

                for n in range(16):
                    s, h, f = n // 8, n // 4 % 2, n % 4
                    at("a", n + 1)
                    at("dn", max(0, n - 3))
                    nc.vector.tensor_tensor(g_a[n % 4][1], g_af[n % 4], g_a[n % 4][0].bitcast(F32), ALU.subtract)\
                        .then_inc(G["al"].sem, 1)
                    if n % 8 == 1 or (n % 8 == 5):
                        q = (n - 5) // 4
                        if n > 1:
                            weigh(dve, i, q)
                    if 2 <= n % 8 <= 6 and not (s == 1 and last_pass):
                        k = n % 8 - 2
                        if k == 0:
                            at("dn", 8 * s)
                            at("cb", s)
                        if s == 0:
                            piece(i, 1, k)
                        else:
                            piece(i + 1, 0, k)
                weigh(dve, i, 3)

            def weigh(dve, i, q):
                s, h = q // 2, q % 2
                dve.wait_ge(G["dn"].sem, G["dn"].at(0, i, 4 * q + 4))
                dve.wait_ge(G["cc"].sem, G["cc"].at(0, i, s + 1))
                dve.wait_ge(G["acc"].sem, G["acc"].at(0, i, max(0, q - 1)))
                b2 = sm[:, bass.ds(i * 2 + (s + SMALL["b2"][0]), 1)]
                nc.vector.scalar_tensor_tensor(out=g_t[h], in0=bank(3 + h), scalar=b2, in1=half(g_cw, h),
                                               op0=ALU.add, op1=ALU.mult).then_inc(G["t"].sem, 1)

            passes(dve, body)

        q_s = [sb(f"quant_{n}", [P, 1]) for n in ("max", "all", "scale", "inverse")]
        q_w = sb("quant_weights", [P, D])
        s_qm, s_qa, s_ql, s_qw = [sem("quant_" + n) for n in ("row_max", "all_max", "low_rank", "ready")]

        def quant_pool(pool):
            pool.wait_ge(s_qm, 1)
            nc.gpsimd.partition_all_reduce(q_s[1][:, :], q_s[0][:, :], P, bass.bass_isa.ReduceOp.max).then_inc(s_qa, 1)

        def quant_pe(pe):
            nc.tensor.matmul(ps[:, 4, 0:D], col("lora_a"), col("lora_b"), start=True, stop=True).then_inc(s_ql, 1)

        def quant_dve_max(dve):
            nc.vector.tensor_reduce(q_s[0][:, :], col("quant_w"), AX.X, ALU.max, apply_absolute_value=True).then_inc(s_qm, 1)

        def quant_dve(dve, order):
            dve.wait_ge(s_qa, 1)
            dve.wait_ge(s_ql, 1)
            scale, inv, w = q_s[2][:, :], q_s[3][:, :], q_w[:, :]
            order.step(nc.vector.tensor_scalar(scale, q_s[1][:, :], 1.0 / 7.0, None, ALU.mult))
            order.step(nc.vector.reciprocal(inv, scale))
            order.step(nc.vector.tensor_scalar(w, col("quant_w"), inv, None, ALU.mult))
            order.step(nc.vector.tensor_scalar(w, w, ROUND, None, ALU.add))
            order.step(nc.vector.tensor_scalar(w, w, -ROUND, 7.0, ALU.add, ALU.min))
            order.step(nc.vector.tensor_scalar(w, w, -8.0, scale, ALU.max, ALU.mult))
            nc.vector.tensor_tensor(w, w, ps[:, 4, 0:D], ALU.add).then_inc(s_qw, 1)

        K = signals("f3", E // 2, w=10, gu=16, sg=16, a=16, ah=16, al=16, dn=16, cb=2, cc=2, t=4, acc=4)
        s_kw = sem("f3_shared_weights")
        k_w = [(wr[:, 3072 * s:3072 * s + 1536], wr[:, 3072 * s + 1536:3072 * s + 3072]) for s in range(2)]
        k_a = [(wr[:, 6144 + 512 * k:6656 + 512 * k], wr[:, 7168 + 512 * k:7680 + 512 * k]) for k in range(2)]
        k_wt = wr[:, 8192:9216]
        k_sel = [wr[:, 9216 + 128 * k:9344 + 128 * k] for k in range(2)]
        k_sg = [wf[:, 512 * k:512 * (k + 1)] for k in range(2)]
        k_af = [wf[:, 1024 + 512 * k:1536 + 512 * k] for k in range(2)]
        k_cw = wf[:, 2048:3072]
        k_t = [wf[:, 3072 + 512 * k:3584 + 512 * k] for k in range(2)]
        FULL = [(s, h, f, NF) for s in range(2) for h in range(2) for f in range(NF)]
        SHARED = [(0, h, f, 2) for h in range(2) for f in range(2)]

        def f3_pe(pe, m):
            pe.wait_ge(s_xf, 2 * m + 2)
            logits_pe(xf, col("gate_w"), 5)
            stack_pe(pe, 2)
            pe.wait_ge(s_wt, 3)
            pe.wait_ge(s_xs, 2 * m + 2)

            def up(i, n, shared=False):
                s, h, f, nf = (SHARED if shared else FULL)[n % 16]
                if h == 0 and f == 0:
                    if shared:
                        pe.wait_ge(s_kw, 2)
                    else:
                        pe.wait_ge(K["w"].sem, K["w"].at(0, i, 5 * (n // 8) + 5))
                pe.wait_ge(K["a"].sem, K["a"].at(0, i, max(0, n - 1)))
                for k in range(2):
                    c0 = (k * nf + f) * P
                    last = mm3(bank(2 * k + n % 2), [v[:, c0:c0 + P] for v in k_w[s]], (half(xh, h), half(xl, h)))
                last.then_inc(K["gu"].sem, 1)

            def body(i, last_pass, shared):
                steps = SHARED if shared else FULL

                def at(name, k):
                    pe.wait_ge(K[name].sem, K[name].at(0, i, k))

                def down(n):
                    s, h, f, nf = steps[n]
                    at("al", n + 1)
                    if f == 0:
                        at("t", 2 * (s - 1) + h + 1 if s else 0)
                    c0 = (2 * nf + f) * P
                    mm3(bank(4 + h), [v[:, c0:c0 + P] for v in k_w[s]], k_a[n % 2], start=f == 0, stop=f == nf - 1)\
                        .then_inc(K["dn"].sem, 1)

                for n in range(len(steps)):
                    if n + 2 < len(steps) or not shared:
                        up(i, n + 2, shared or (last_pass and n + 2 >= 16))
                    if n % 8 == 3 and not shared:
                        s = n // 8
                        at("cc", s)
                        for h in range(2):
                            last = nc.tensor.matmul(bank(6 + h), k_sel[s], half(k_wt, h), start=True, stop=True)
                        last.then_inc(K["cb"].sem, 1)
                    down(n)

            up(0, 0)
            up(0, 1)
            with pe.Fori(0, PASSES - 1) as i:
                body(i, False, False)
            body(PASSES - 1, True, False)
            body(PASSES, True, True)
            pe.wait_ge(K["acc"].sem, K["acc"].at(0, PASSES, 2))
            back_pe(pe)

        def f3_act(act):
            softmax_act(act, 3)
            stack_act(act, 2, k_wt)

            def body(i, shared):
                steps = SHARED if shared else FULL

                def at(name, k):
                    act.wait_ge(K[name].sem, K[name].at(0, i, k))

                def high(n):
                    at("a", n + 1)
                    at("dn", max(0, n - 1))
                    nc.scalar.activation(k_a[n % 2][0], k_af[n % 2], ACT.Copy).then_inc(K["ah"].sem, 1)

                for n in range(len(steps)):
                    at("gu", n + 1)
                    at("a", max(0, n - 1))
                    nc.scalar.activation(k_sg[n % 2], bank(n % 2), ACT.Silu).then_inc(K["sg"].sem, 1)
                    if n >= 1:
                        high(n - 1)
                    if n % 8 == 4 and not shared:
                        s = n // 8
                        at("cb", s + 1)
                        at("t", 2 * s)
                        nc.scalar.activation(k_cw, bank(6, 2), ACT.Copy).then_inc(K["cc"].sem, 1)
                high(len(steps) - 1)

            with act.Fori(0, PASSES - 1) as i:
                body(i, False)
            body(PASSES - 1, False)
            body(PASSES, True)

        def f3_pool(pool):
            pool.wait_ge(s_wt, 3)

            def body(i, count):
                for n in range(count):
                    h = n % 2
                    pool.wait_ge(K["t"].sem, K["t"].at(0, i, n + 1))
                    pool.wait_ge(K["acc"].sem, K["acc"].at(0, i, max(0, n - 1)))
                    nc.gpsimd.tensor_tensor(half(out_t, h), half(out_t, h), k_t[h], ALU.add).then_inc(K["acc"].sem, 1)

            with pool.Fori(0, PASSES) as i:
                body(i, 4)
            body(PASSES, 2)

        def f3_dve(dve, order):
            dve.wait_ge(s_lg, 4)
            order.step(nc.vector.tensor_copy(lg, ps[:, 5, 0:NT * E].rearrange("p (t e) -> p t e", t=NT)))
            softmax_dve(dve, order, 3)
            pick_max(order, oh, ex, t1, mcol)
            order.step(nc.vector.scalar_tensor_tensor(out=lg.rearrange("p t e -> p (t e)"), in0=oh.rearrange("p t e -> p (t e)"),
                                                      scalar=-2.0, in1=ex.rearrange("p t e -> p (t e)"),
                                                      op0=ALU.mult, op1=ALU.add))
            pick_max(order, oh2, lg, t1, mcol)
            order.step(nc.vector.tensor_tensor(oh, oh, oh2, ALU.add))
            order.step(nc.vector.tensor_tensor(ex, ex, oh, ALU.mult))
            order.done(nc.vector.memset(k_wt.bitcast(F32), 0.0))
            order.step(nc.vector.memset(out_t[:, :], 0.0))
            split_stack(order, ex, 0, True)
            dve.wait_ge(ld["f3"], 16)

            def piece(i, s, k):
                w = raw_b[:, bass.ds(i * (2 * W_F3) + s * W_F3, W_F3)]
                hi, lo = k_w[s]
                c = slice(768 * (k % 2), 768 * (k % 2 + 1))
                if k < 2:
                    ins = nc.vector.tensor_copy(hi[:, c], w[:, c])
                elif k < 4:
                    dve.wait_ge(K["w"].sem, K["w"].at(0, i, 5 * s + k - 1))
                    ins = nc.vector.tensor_tensor(lo[:, c], w[:, c], hi[:, c].bitcast(F32), ALU.subtract)
                else:
                    ins = nc.vector.tensor_copy(k_sel[s], sm[:, bass.ds(i * (2 * P) + (s * P + SMALL["sel_e"][0]), P)])
                ins.then_inc(K["w"].sem, 1)

            for k in range(5):
                piece(0, 0, k)

            def body(i, last_pass, shared):
                steps = SHARED if shared else FULL

                def at(name, k):
                    dve.wait_ge(K[name].sem, K[name].at(0, i, k))

                def low(n):
                    at("ah", n + 1)
                    at("dn", max(0, n - 1))
                    nc.vector.tensor_tensor(k_a[n % 2][1], k_af[n % 2], k_a[n % 2][0].bitcast(F32), ALU.subtract)\
                        .then_inc(K["al"].sem, 1)

                def weigh(q):
                    h = q % 2
                    at("dn", (2 if shared else 4) * (q + 1))
                    at("acc", max(0, q - 1))
                    if shared:
                        ins = nc.vector.tensor_copy(k_t[h], bank(4 + h))
                    else:
                        at("cc", q // 2 + 1)
                        ins = nc.vector.tensor_tensor(k_t[h], bank(4 + h), half(k_cw, h), ALU.mult)
                    ins.then_inc(K["t"].sem, 1)

                for n in range(len(steps)):
                    at("sg", n + 1)
                    at("al", max(0, n - 1))
                    at("ah", max(0, n - 1))
                    nc.vector.tensor_tensor(k_af[n % 2], k_sg[n % 2], bank(2 + n % 2), ALU.mult).then_inc(K["a"].sem, 1)
                    if n >= 1:
                        low(n - 1)
                    if not shared:
                        s = n // 8
                        if n % 4 == 2 and n > 2:
                            weigh((n - 6) // 4)
                        if 2 <= n % 8 <= 6:
                            k = n % 8 - 2
                            if k == 0:
                                at("dn", 8 * s)
                                at("cb", s)
                            if s == 0:
                                piece(i, 1, k)
                            elif not last_pass:
                                piece(i + 1, 0, k)
                            elif k < 2:
                                w = raw_b[:, E * W_F3:E * W_F3 + W_SH]
                                hi, lo = k_w[0][0][:, 0:W_SH], k_w[0][1][:, 0:W_SH]
                                if k == 0:
                                    ins = nc.vector.tensor_copy(hi, w)
                                else:
                                    dve.wait_ge(s_kw, 1)
                                    ins = nc.vector.tensor_tensor(lo, w, hi.bitcast(F32), ALU.subtract)
                                ins.then_inc(s_kw, 1)
                    elif n == 3:
                        weigh(0)
                low(len(steps) - 1)
                weigh(1 if shared else 3)

            with dve.Fori(0, PASSES - 1) as i:
                body(i, False, False)
            body(PASSES - 1, True, False)
            body(PASSES, True, True)

        def split_ctx(dve, order):
            dve.wait_ge(ld["ctx_t"], 16)
            order.step(nc.vector.tensor_copy(ch[:, :], out_t[:, :]))
            nc.vector.tensor_tensor(cl[:, :], out_t[:, :], ch[:, :].bitcast(F32), ALU.subtract).then_inc(s_ctx, 1)

        block = stack.enter_context(nc.Block())

        @block.sync
        def _(sp):
            def load(dst, src, name):
                sp.dma_start(dst, src).then_inc(ld[name], 16)

            load(res[:, :, :], x, "x")
            load(sm[:, :], small, "small")
            load(out_t[:, :], ctx_t, "ctx_t")
            load(raw_a[:, RA0:RA0 + NG * W_A], wa0, "a0")
            load(raw_a[:, RF0:RF0 + 2 * NKT * W_F0], wf0, "f0")
            load(mask_u8[:, :], mask, "mask")
            load(raw_b[:, RB1:RB1 + NQ * W_B], wb1, "b1")
            load(ctok[:, :, :], ctx_tok, "ctx_tok")
            load(raw_b[:, RA2:RA2 + NG * W_A], wa2, "a2")
            sp.wait_ge(A["w"].sem, A["w"].at(0, NG, 0))
            sp.wait_ge(F["w"].sem, F["w"].at(0, NKT, 0))
            load(raw_a[:, :], wf1, "f1")
            sp.wait_ge(G["w"].sem, G["w"].at(0, PASSES, 0))
            load(raw_a[:, RB3:RB3 + NQ * W_B], wb3, "b3")
            sp.wait_ge(W["w"].sem, W["w"].at(0, NQ, 0))
            sp.wait_ge(W["y"].sem, W["y"].at(0, NQ, 0))
            sp.wait_ge(A["w"].sem, A["w"].at(1, NG, 0))
            load(raw_b[:, :], wf3, "f3")
            sp.wait_ge(s_res, 2)
            sp.dma_start(out, res[:, :, :]).then_inc(s_out, 16)
            sp.wait_ge(s_out, 16)

        @block.gpsimd
        def _(pool):
            nc.gpsimd.memset(mhalf[:, :], -0.5).then_inc(s_init, 1)
            pool.wait_ge(s_init, 1)
            quant_pool(pool)
            norm_pool(pool, 0)
            norm_pool(pool, 1)
            norm_pool(pool, 2)
            wide_pool(pool, 0)
            norm_pool(pool, 3)
            f1_pool(pool)
            norm_pool(pool, 4)
            norm_pool(pool, 5)
            norm_pool(pool, 6)
            norm_pool(pool, 7)
            norm_pool(pool, 8)
            wide_pool(pool, 1)
            norm_pool(pool, 9)
            f3_pool(pool)

        @block.scalar
        def _(act):
            act.wait_ge(ld["small"], 16)
            nc.scalar.activation(gate[:, :], col("gates"), ACT.Tanh).then_inc(s_gate, 1)
            norm_act(act, 0)
            act.wait_ge(s_vp, 1)
            nc.scalar.activation(a_vall, bank(0, 2), ACT.Copy).then_inc(s_va, 1)
            small_act(act, 0)
            small_out_act(act)
            norm_act(act, 1)
            f0_act(act)
            norm_act(act, 2)
            wide_act(act, 0, ACT.Square, col("nbias"))
            norm_act(act, 3)
            f1_act(act)
            norm_act(act, 4)
            small_act(act, 1)
            norm_act(act, 5)
            norm_act(act, 6, col("ln_c_w"), col("ln_c_b"))
            norm_act(act, 7, col("ln_l_w"), col("ln_l_b"))
            wide_act(act, 1, ACT.Exp, 0.0)
            norm_act(act, 8)
            f3_act(act)

        @block.vector
        def _(dve):
            order = Order(dve, s_dve)
            dve.wait_ge(ld["small"], 16)
            quant_dve_max(dve)
            dve.wait_ge(ld["x"], 16)
            norm_dve_tokens(dve, order, 0, res, xn)
            norm_dve_split(dve, order, 0, xh, xl)
            split_ctx(dve, order)
            dve.wait_ge(s_gate, 1)
            small_dve(dve, order, 0, raw_a, RA0, ld["a0"])
            back_dve(dve, order, 0, 0)
            norm_dve_tokens(dve, order, 1, res, xn)
            norm_dve_split(dve, order, 1, xh, xl)
            f0_dve(dve, order)
            back_dve(dve, order, 1, 1)
            norm_dve_tokens(dve, order, 2, res, xn)
            norm_dve_split(dve, order, 2, xh, xl)
            dve.wait_ge(ld["mask"], 16)
            order.step(nc.vector.tensor_scalar(w_floor, col("nbias"), -8.0, None, ALU.mult))
            flat_cap = raw_b[:, CAP:CAP + 2 * T]
            order.step(nc.vector.tensor_scalar(flat_cap, mask_u8[:, :], -BIG, BIG, ALU.mult, ALU.add))
            order.step(nc.vector.tensor_scalar(flat_cap, flat_cap, w_floor, None, ALU.add))
            order.step(nc.vector.memset(xn[:, :, :], 0.0))
            wide_dve(dve, order, 0, raw_b, RB1, ld["b1"])
            dve.wait_ge(W["acc"].sem, W["acc"].at(0, NQ, 0))
            tokens_in(dve, order, 2, xn)
            norm_dve_tokens(dve, order, 3, res, xn)
            norm_dve_split(dve, order, 3, xh, xl)
            f1_dve(dve, order)
            tokens_in(dve, order, 3, xn)
            back_dve(dve, order, 2, 3)
            norm_dve_tokens(dve, order, 4, res, xn)
            norm_dve_split(dve, order, 4, xh, xl)
            small_dve(dve, order, 1, raw_b, RA2, ld["a2"])
            dve.wait_ge(A["att"].sem, A["att"].at(1, NG, 0))
            tokens_in(dve, order, 4, a_att)
            norm_dve_tokens(dve, order, 5, res, xn)
            norm_dve_split(dve, order, 5, xh, xl)
            quant_dve(dve, order)
            for h in range(2):
                dve.wait_ge(s_rt, 2 * 3 + h + 1)
                r = xn[:, 4 * h:4 * h + 4, :]
                order.done(nc.vector.tensor_tensor(r, bank(6 + h).rearrange("p (t d) -> p t d", t=4),
                                                   col("quant_bias").unsqueeze(1).to_broadcast((P, 4, D)), ALU.add))
            order.wait()
            tokens_in(dve, order, 5, xn)
            norm_dve_tokens(dve, order, 6, ctok, xn)
            norm_dve_split(dve, order, 6, ch, cl)
            norm_dve_tokens(dve, order, 7, res, xn)
            norm_dve_tokens(dve, order, 8, xn, xn)
            norm_dve_split(dve, order, 7, xh, xl)
            order.step(nc.vector.tensor_copy(xn[:, :, :], col("bo").unsqueeze(1).to_broadcast((P, NT, D))))
            wide_dve(dve, order, 1, raw_a, RB3, ld["b3"])
            dve.wait_ge(W["acc"].sem, W["acc"].at(1, NQ, 0))
            tokens_in(dve, order, 6, xn)
            norm_dve_tokens(dve, order, 9, res, xn)
            norm_dve_split(dve, order, 8, xh, xl)
            f3_dve(dve, order)
            back_dve(dve, order, 4, 7, s_res)

        @block.tensor
        def _(pe):
            pe.wait_ge(ld["small"], 16)
            norm_pe(pe, 0, 0)
            pe.wait_ge(ld["ctx_t"], 16)
            for t in range(NT):
                last = nc.tensor.matmul(ps[:, t // 4, (t % 4) * P:(t % 4 + 1) * P], out_t[:, t * P:(t + 1) * P],
                                        col("wv0"), start=True, stop=True)
            last.then_inc(s_vp, 1)
            pe.wait_ge(s_va, 1)
            pe.wait_ge(s_ctx, 1)
            small_pe(pe, 0, 0)
            small_out_pe(pe)
            norm_pe(pe, 1, 1)
            f0_pe(pe, 1)
            norm_pe(pe, 2, 2)
            wide_pe(pe, 0, 2)
            norm_pe(pe, 3, 3)
            f1_pe(pe, 3)
            norm_pe(pe, 4, 4)
            small_pe(pe, 1, 4)
            norm_pe(pe, 5, 5)
            quant_pe(pe)
            pe.wait_ge(s_xf, 2 * 5 + 2)
            pe.wait_ge(s_qw, 1)
            tokens_pe(xf, q_w[:, :])
            norm_pe(pe, 6, 6)
            norm_pe(pe, 8, 7)
            wide_pe(pe, 1, 7)
            norm_pe(pe, 9, 8)
            f3_pe(pe, 8)

def tokens_first(a):
    return np.ascontiguousarray(a.reshape(NT, P, D).transpose(1, 0, 2))


def small_heads(wq, wk):
    a = np.zeros((P, NG, W_A), np.float32)
    for g in range(NG):
        for j in range(GH):
            r = (g * GH + j) * DH8
            for rep in range(3):
                at = BLK * j + DH8 * rep
                a[:, g, at:at + DH8] = wq[r:r + DH8, :].T
                a[:, g, P + at:P + at + DH8] = wk[r:r + DH8, :].T
    return a.reshape(P, NG * W_A)


def kernel(**inputs):
    import concourse.bacc as _bacc
    from concourse.bass_utils import run_bass_kernel_spmd as _run
    arrays = layout({k: np.asarray(v) for k, v in inputs.items()})
    nc = _bacc.Bacc("TRN2", target_bir_lowering=False, num_devices=1)
    aps = {n: nc.dram_tensor("in_" + n, a.shape, mybir.dt.from_np(a.dtype), kind="ExternalInput").ap()
           for n, a in arrays.items()}
    out = nc.dram_tensor("out_tokens", (P, NT, D), F32, kind="ExternalOutput").ap()
    build(nc, out=out, **aps)
    r = _run(nc, [{"in_" + n: a for n, a in arrays.items()}], core_ids=[0])
    got = np.asarray(r.results[0]["out_tokens"])
    return np.ascontiguousarray(got.transpose(1, 0, 2)).reshape(B, S, D)


def layout(v):
    f = np.float32
    sm = np.zeros((P, N_SMALL), f)

    def put(name, a, rows=slice(None)):
        at, width = SMALL[name]
        sm[rows, at:at + width] = a

    r = np.arange(P)
    put("ident", np.eye(P, dtype=f))
    c = np.arange(2 * P)
    put("spread", (r[:, None] == BLK * (2 * (c[None, :] % P // DH) + c[None, :] // P)).astype(f))
    put("lo_q", -((r % BLK) // DH8 == 2).astype(f)[:, None])
    put("lo_k", -((r % BLK) // DH8 == 1).astype(f)[:, None])
    put("one_rows", ((r % BLK == 24) | (r % BLK == 25)).astype(f)[:, None])
    put("head", (r[:, None] // BLK == np.arange(GH)[None, :]).astype(f))
    put("inv_n", np.stack([f(1) / (r + 1).astype(f), f(1) / (P + r + 1).astype(f)], 1))
    put("iota", np.arange(E, dtype=f)[None, :])
    put("gates", np.stack([v["g_xattn"], v["g_ffn"]], 1).reshape(1, 8))
    put("nbias", v["L1_xattn_nbias"].reshape(1, 1))
    put("alpha", v["L0_ffn_alpha_bi"].reshape(1, 1))
    put("rb2", v["L0_ffn_router_b2"][None, :])
    put("ebias", v["L0_ffn_expert_bias"][None, :])
    put("rb1", v["L0_ffn_router_b1"][:, None])
    put("gamma", v["L1_ffn_gamma"].T)
    put("beta", v["L1_ffn_beta"].T)
    put("b1", v["L1_ffn_b1"].reshape(E, NF, P).transpose(2, 0, 1).reshape(P, E * NF))
    put("b2", v["L1_ffn_b2"].T)
    put("quant_bias", v["L2_ffn_bias"][None, :])
    put("bo", v["L3_xattn_bo"][None, :])
    for n in ("ln_l_w", "ln_l_b", "ln_c_w", "ln_c_b"):
        put(n, v["L3_xattn_" + n][:, None])
    put("centroids", v["L1_ffn_centroids"].T)
    put("gate_w", v["L3_ffn_gate_w"].T)
    put("router_w2", v["L0_ffn_router_w2"].T)
    for k, n in enumerate(("b_fwd", "b_fwd", "b_inv", "b_inv")):
        put("b_experts", v["L0_ffn_" + n], slice(E * k, E * (k + 1)))
    for n in ("W_Q", "W_K", "W_inv", "W_O", "router_w1"):
        put(n, v["L0_ffn_" + n].T)
    put("wv0", v["L0_xattn_Wv"].T)
    put("wo0", v["L0_xattn_Wo"].T)
    put("quant_w", v["L2_ffn_kernel"])
    put("lora_a", v["L2_ffn_a"].T, slice(0, 16))
    put("lora_b", v["L2_ffn_b"], slice(0, 16))
    e = np.arange(E)
    sel_e = ((r[:, None] % E == e[None, :]) & (r[:, None] < 2 * E)).astype(f)
    put("sel_e", np.repeat(sel_e, P, axis=1))

    wf0 = np.zeros((P, NKT, 2, W_F0), f)
    for br, (nv, nw, nu) in enumerate((("V_fwd", "W_fwd", "U_fwd"), ("W_inv_exp", "V_inv", "U_inv"))):
        for k in range(NKT):
            two = slice(2 * k, 2 * k + 2)
            wf0[:, k, br, 0:P] = v["L0_ffn_" + nv][two].transpose(1, 0, 2).reshape(D, P)
            wf0[:, k, br, P:2 * P] = v["L0_ffn_" + nw][two].transpose(1, 0, 2).reshape(D, P)
            wf0[:, k, br, 2 * P:3 * P] = v["L0_ffn_" + nu][two].transpose(0, 2, 1).reshape(P, D)
            expert = 2 * k + r[None, :] // 64
            wf0[:, k, br, 3 * P:] = ((r[:, None] // (2 * E) == br) & (r[:, None] % E == expert)).astype(f)

    def wide(wq_t, wk_t, wv_t, wo):
        a = np.zeros((P, NQ, W_B), f)
        for q in range(NQ):
            s = slice(q * QW, (q + 1) * QW)
            a[:, q, 0:QW], a[:, q, QW:2 * QW], a[:, q, 2 * QW:3 * QW] = wq_t[:, s], wk_t[:, s], wv_t[:, s]
            a[:, q, 3 * QW:] = wo[s, :].reshape(2, P, D).transpose(1, 0, 2).reshape(P, 2 * D)
        return a.reshape(P, NQ * W_B)

    w = NQ * QW
    kv1, kv3 = v["L1_xattn_Wkv"], v["L3_xattn_Wkv"]
    wf1 = np.zeros((P, E, W_F1), f)
    wf1[:, :, :512] = v["L1_ffn_W1"].transpose(2, 0, 1)
    wf1[:, :, 512:] = v["L1_ffn_W2"].reshape(E, D, NF, P).transpose(3, 0, 2, 1).reshape(P, E, NF * D)
    wf3 = np.zeros((P, E * W_F3 + W_SH), f)
    a = wf3[:, :E * W_F3].reshape(P, E, W_F3)
    a[:, :, 0:512] = v["L3_ffn_gate_k"].transpose(1, 0, 2)
    a[:, :, 512:1024] = v["L3_ffn_up_k"].transpose(1, 0, 2)
    a[:, :, 1024:] = v["L3_ffn_down_k"].reshape(E, NF, P, D).transpose(2, 0, 1, 3).reshape(P, E, NF * D)
    wf3[:, :E * W_F3] = a.reshape(P, E * W_F3)
    sh = wf3[:, E * W_F3:]
    sh[:, 0:256], sh[:, 256:512] = v["L3_ffn_sh_gate"], v["L3_ffn_sh_up"]
    sh[:, 512:] = v["L3_ffn_sh_down"].reshape(2, P, D).transpose(1, 0, 2).reshape(P, 2 * D)
    eye = np.eye(D, dtype=f)
    c = v["ctx_1024"]
    arrays = dict(
        x=tokens_first(v["x"]), ctx_tok=tokens_first(c), ctx_t=np.ascontiguousarray(c.reshape(T, D).T),
        mask=np.ascontiguousarray(v["mask_BxSxS2_bk0"].reshape(B, S, 2, P).transpose(3, 0, 2, 1)).reshape(P, 2 * T),
        small=sm,
        wa0=small_heads(v["L0_xattn_Wq"], v["L0_xattn_Wk"]),
        wa2=small_heads(eye, eye),
        wf0=wf0.reshape(P, 2 * NKT * W_F0),
        wb1=wide(v["L1_xattn_Wq"].T, kv1[:w].T, kv1[w:].T, v["L1_xattn_Wo"].T),
        wf1=wf1.reshape(P, E * W_F1),
        wb3=wide(v["L3_xattn_Wq"], kv3[:, :w], kv3[:, w:], v["L3_xattn_Wo"]),
        wf3=wf3,
    )
    return arrays
```

```python
from contextlib import ExitStack

import numpy as np

import concourse.bass as bass
from concourse import mybir

F32 = mybir.dt.float32
F32R = mybir.dt.float32r
U8 = mybir.dt.uint8
ALU = mybir.AluOpType
ACT = mybir.ActivationFunctionType
AX = mybir.AxisListType

P = 128
B, S, D = 4, 256, 128
T = B * S
NT = T // P
H = 16
HALF = 512
E = 8
BLK = 32
GH = P // BLK
NG = H // GH
DH8 = D // H
DH = 64
NQ = 4
QW = 4 * DH
NKT = 4
BIG = 3.0e38
EPS = 1e-5
IEPS = 1e-32
CLIP = 11.0
ROUND = 12582912.0

SMALL = {}
N_SMALL = 0
for _name, _width in (
    ("ident", P), ("spread", 2 * P), ("lo_q", 1), ("lo_k", 1), ("one_rows", 1), ("head", GH),
    ("inv_n", 2), ("iota", E), ("gates", 8), ("nbias", 1), ("alpha", 1), ("rb2", E), ("ebias", E),
    ("rb1", 1), ("gamma", E), ("beta", E), ("b1", 4 * E), ("b2", E), ("quant_bias", P),
    ("ln_l_w", 1), ("ln_l_b", 1), ("ln_c_w", 1), ("ln_c_b", 1), ("bo", P),
    ("centroids", E), ("gate_w", E), ("router_w2", E), ("b_experts", P),
    ("W_Q", P), ("W_K", P), ("W_inv", P), ("router_w1", P), ("W_O", P), ("wv0", P), ("wo0", P),
    ("quant_w", P), ("lora_a", P), ("lora_b", P), ("sel_e", E * P),
):
    SMALL[_name] = (N_SMALL, _width)
    N_SMALL += _width
W_A = 2 * P
W_F0 = 4 * P
W_B = 4 * QW
W_F1 = 1024
W_F3 = 1536
W_SH = 768
NF = 4


class Order:

    def __init__(self, eng, sem):
        self.eng, self.sem = eng, sem
        self.base, self.i, self.per, self.local = 0, None, 0, 0

    def loop(self, i, per):
        self.i, self.per, self.local = i, per, 0

    def end(self, passes):
        assert self.local == self.per, (self.local, self.per)
        self.base += passes * self.per
        self.i, self.per, self.local = None, 0, 0

    def done(self, ins):
        ins.then_inc(self.sem, 1)
        if self.i is None:
            self.base += 1
        else:
            self.local += 1
        return ins

    def wait(self):
        self.eng.wait_ge(self.sem, self.base if self.i is None else self.i * self.per + (self.base + self.local))

    def step(self, ins):
        self.done(ins)
        self.wait()


class Signal:

    def __init__(self, sem, per, passes):
        self.sem, self.per, self.passes = sem, per, passes

    def at(self, call, i, k):
        return i * self.per + (call * self.per * self.passes + k)


def build(nc, x, ctx_tok, ctx_t, mask, small, wa0, wf0, wb1, wf1, wa2, wb3, wf3, out):
    stack = ExitStack()
    with stack:
        def sb(name, shape, dt=F32):
            return stack.enter_context(nc.sbuf_tensor(name, shape, dt))

        def sem(name):
            return stack.enter_context(nc.semaphore(name))

        sm = sb("small_operands", [P, N_SMALL])
        res = sb("residual", [P, NT, D])
        xn = sb("normed_tokens", [P, NT, D])
        xf = sb("normed_t", [P, T])
        xh = sb("normed_t_high", [P, T], F32R)
        xl = sb("normed_t_low", [P, T], F32R)
        out_t = sb("sublayer_out_t", [P, T])
        ctok = sb("context_tokens", [P, NT, D])
        ch = sb("context_t_high", [P, T], F32R)
        cl = sb("context_t_low", [P, T], F32R)
        gate = sb("tanh_gates", [P, 8])
        mask_u8 = sb("mask_bytes", [P, 2 * T], U8)
        w_floor_t = sb("score_floor", [P, 1])
        w_floor = w_floor_t[:, :]
        stats = sb("ln_stats", [P, NT, 6])
        mv = sb("ln_mean_var", [P, NT, 2])
        ve = sb("ln_var_eps", [P, NT])
        mhalf = sb("minus_half", [P, NT])
        rs = sb("ln_rstd", [P, NT])
        rt = sb("ln_newton", [P, NT])
        raw_a = sb("raw_a", [P, E * W_F1])
        raw_b = sb("raw_b", [P, E * W_F3 + W_SH])
        RA0, RF0 = 0, NG * W_A
        RB3 = 0
        RB1, RA2, CAP = 0, NQ * W_B, NQ * W_B + NG * W_A
        cap = raw_b[:, CAP:CAP + B * 2 * S].rearrange("p (b k q) -> p b k q", b=B, k=2)
        NWF, NWR = 8192, 9472
        wf = sb("work", [P, NWF])
        wr = sb("work_split", [P, NWR], F32R)

        def col(name, a=0, n=None):
            at, width = SMALL[name]
            return sm[:, at + a:at + (width if n is None else a + n)]

        ident = col("ident")
        ps = stack.enter_context(nc.psum_tensor("banks", [P, 8, HALF], F32))

        def bank(i, n=1):
            return ps[:, i, :] if n == 1 else ps[:, i:i + n, :].rearrange("p a b -> p (a b)")

        def half(t, h):
            return t[:, h * HALF:(h + 1) * HALF]

        def mm3(o, w, m, start=True, stop=True):
            nc.tensor.matmul(o, w[0], m[0], start=start, stop=False)
            nc.tensor.matmul(o, w[0], m[1], start=False, stop=False)
            return nc.tensor.matmul(o, w[1], m[0], start=False, stop=stop)

        ld = {n: sem("loaded_" + n) for n in ("x", "ctx_t", "ctx_tok", "small", "mask", "a0", "f0", "b1", "f1", "a2", "b3", "f3")}
        s_dve = sem("vector_own_steps")
        s_act = sem("scalar_own_steps")
        s_init = sem("constants_ready")
        s_gate = sem("gates_ready")
        s_ctx = sem("context_split")
        s_ve = sem("ln_variance_ready")
        s_pow = sem("ln_power_ready")
        s_xn = sem("ln_tile_ready")
        s_xt = sem("ln_half_transposed")
        s_xf = sem("ln_half_copied")
        s_xs = sem("ln_half_split")
        s_rt = sem("out_half_back")
        s_vp = sem("values_tile_product")
        s_va = sem("values_ready")
        s_out = sem("stored")
        s_pcl, s_clear = sem("parts_cleared"), sem("feed_forward_cleared")
        s_res = sem("residual_done")
        s_ot, s_oc = sem("heads_transposed"), sem("heads_copied")

        def signals(prefix, passes, **per):
            return {k: Signal(sem(f"{prefix}_{k}"), n, passes) for k, n in per.items()}

        def splits(m):
            return m - (m > 6)

        def norm_dve_tokens(dve, order, n, src, dst, meanwhile=None):
            if src is xn:
                dve.wait_ge(s_xn, NT * n)
            for t in range(NT):
                order.done(nc.vector.bn_stats(stats[:, t, :], src[:, t, :]))
            order.wait()
            for t in range(NT):
                order.done(nc.vector.bn_aggr(mv[:, t, :], stats[:, t, :]))
            order.wait()
            nc.vector.tensor_scalar(ve[:, :], mv[:, :, 1], EPS, None, ALU.add).then_inc(s_ve, 1)
            dve.wait_ge(s_ve, n + 1)
            if meanwhile is not None:
                meanwhile()
            dve.wait_ge(s_pow, n + 1)
            order.step(nc.vector.tensor_tensor(rt[:, :], rs[:, :], rs[:, :], ALU.mult))
            order.step(nc.vector.tensor_tensor(rt[:, :], rt[:, :], ve[:, :], ALU.mult))
            order.step(nc.vector.tensor_scalar(rt[:, :], rt[:, :], -0.5, 1.5, ALU.mult, ALU.add))
            order.step(nc.vector.tensor_tensor(rs[:, :], rs[:, :], rt[:, :], ALU.mult))
            for t in range(NT):
                nc.vector.tensor_scalar(dst[:, t, :], src[:, t, :], mv[:, t, 0:1], rs[:, t:t + 1],
                                        ALU.subtract, ALU.mult).then_inc(s_xn, 1)

        def norm_pool(pool, n):
            pool.wait_ge(s_ve, n + 1)
            nc.gpsimd.tensor_tensor(rs[:, :], ve[:, :], mhalf[:, :], ALU.pow).then_inc(s_pow, 1)

        def norm_pe(pe, n, m, src=xn):
            for h in range(2):
                for t in range(4 * h, 4 * h + 4):
                    pe.wait_ge(s_xn, NT * n + t + 1)
                    last = nc.tensor.transpose(ps[:, 6 + h, (t % 4) * P:(t % 4 + 1) * P], src[:, t, :], ident)
                last.then_inc(s_xt, 1)

        def norm_act(act, m, f32=True, high=None, w=None, b=None):
            for h in range(2):
                act.wait_ge(s_xt, 2 * m + h + 1)
                act.wait_ge(s_xs, 2 * splits(m))
                if f32 and w is None:
                    ins = nc.scalar.activation(half(xf, h), bank(6 + h), ACT.Copy)
                elif f32:
                    ins = nc.scalar.activation(half(xf, h), bank(6 + h), ACT.Identity, bias=b, scale=w)
                if high is not None:
                    ins = nc.scalar.activation(half(high, h), bank(6 + h), ACT.Copy)
                ins.then_inc(s_xf, 1)

        def norm_dve_split(dve, order, m, hi, lo, from_bank=True):
            for h in range(2):
                dve.wait_ge(s_xf, 2 * m + h + 1)
                src = bank(6 + h) if from_bank else half(xf, h)
                if not from_bank:
                    order.step(nc.vector.tensor_copy(half(hi, h), src))
                nc.vector.tensor_tensor(half(lo, h), src, half(hi, h).bitcast(F32), ALU.subtract).then_inc(s_xs, 1)

        def back_pe(pe):
            for h in range(2):
                for t in range(4):
                    last = nc.tensor.transpose(ps[:, 6 + h, t * P:(t + 1) * P],
                                               out_t[:, (4 * h + t) * P:(4 * h + t + 1) * P], ident)
                last.then_inc(s_rt, 1)

        def tokens_pe(src, w):
            for h in range(2):
                for t in range(4):
                    last = nc.tensor.matmul(ps[:, 6 + h, t * P:(t + 1) * P],
                                            src[:, (4 * h + t) * P:(4 * h + t + 1) * P], w, start=True, stop=True)
                last.then_inc(s_rt, 1)

        def back_dve(dve, order, r, n, signal=None):
            for h in range(2):
                dve.wait_ge(s_rt, 2 * r + h + 1)
                t = res[:, 4 * h:4 * h + 4, :].rearrange("p t d -> p (t d)")
                ins = nc.vector.scalar_tensor_tensor(out=t, in0=bank(6 + h), scalar=gate[:, n:n + 1], in1=t,
                                                     op0=ALU.mult, op1=ALU.add)
                if signal is None:
                    order.done(ins)
                else:
                    ins.then_inc(signal, 1)
            if signal is None:
                order.wait()

        A = signals("a", NG, w=2, q=4, hi=4, y=4, km=8, v=2, mx=16, red=16, m2=2, mt=2, yf=2, s=8, p=8, pv=8,
                    raw=2, rt=2, att=2)
        s_acl = sem("a_tile_cleared")
        s_ainit = sem("a_cleared")
        a_y, a_yf, a_ky = wr[:, 0:1024], wr[:, 1024:2048], wr[:, 2048:3072]
        a_km = [wr[:, 3072 + 1024 * j:4096 + 1024 * j] for j in range(GH)]
        a_hi = wr[:, 7168:8192]
        a_wh, a_wl = wr[:, 8192:8448], wr[:, 8448:8704]
        a_vall = wf[:, 0:1024]
        a_vg = wf[:, 1024:2048].rearrange("p (t j c) -> p t j c", t=NT, j=GH)
        a_p = [wf[:, 2048 + 1024 * k:3072 + 1024 * k] for k in range(2)]
        a_m2 = wf[:, 4096:5120].rearrange("p (t j c) -> p t j c", t=NT, j=GH)
        a_raw = wf[:, 5120:6144]
        a_nm = wf[:, 6144:6176].rearrange("p (t j) -> p t j", t=NT)
        a_rec = wf[:, 6176:6208].rearrange("p (t j) -> p t j", t=NT)
        a_att = wf[:, 7168:8192].rearrange("p (t d) -> p t d", t=NT)
        a_att_t = wf[:, 1024:2048]

        def small_passes(eng, slot):
            with eng.Fori(0, NG - 1) as i:
                slot(i, 0, True, True)
                slot(i, 1, True, True)
            slot(NG - 1, 0, False, True)
            slot(NG - 1, 1, False, False)

        def small_pe(pe, c, m):
            def at(i, name, k):
                pe.wait_ge(A[name].sem, A[name].at(c, i, k))

            def project(i, x, k):
                h = x % 2
                at(i, "w", 2 * (x // 2) + 2)
                if k:
                    at(i, "y", 2 * x + 1)
                src = (half(ch, h), half(cl, h)) if k else (half(xh, h), half(xl, h))
                mm3(bank(5), (a_wh[:, k * P:(k + 1) * P], a_wl[:, k * P:(k + 1) * P]), src).then_inc(A["q"].sem, 1)

            def maxima(i, x, n):
                t, j0 = 4 * (x % 2) + n // 2, 2 * (n % 2)
                if n == 0:
                    at(i, "km", 4 * x + 4)
                if n >= 2:
                    at(i, "red", 8 * x + n - 1)
                for j in range(j0, j0 + 2):
                    last = nc.tensor.matmul(ps[:, 6 + n % 2, (j % 2) * S:(j % 2 + 1) * S],
                                            a_y[:, t * P:(t + 1) * P], a_km[j][:, (t // 2) * S:(t // 2 + 1) * S],
                                            start=True, stop=True)
                last.then_inc(A["mx"].sem, 1)

            def maxima_back(i, x):
                at(i, "m2", x + 1)
                for t in range(4):
                    last = nc.tensor.transpose(ps[:, 5, t * P:(t + 1) * P],
                                               a_m2[:, 4 * (x % 2) + t, :, :].rearrange("p j c -> p (j c)"), ident)
                last.then_inc(A["mt"].sem, 1)

            def scores(x, u):
                b, kb = 2 * (x % 2) + u // 2, u % 2
                for j in range(GH):
                    last = nc.tensor.matmul(ps[:, 2 * (u % 2) + j // 2, (j % 2) * S:(j % 2 + 1) * S],
                                            a_km[j][:, b * S + kb * P:b * S + (kb + 1) * P],
                                            a_yf[:, b * S:(b + 1) * S], start=True, stop=True)
                last.then_inc(A["s"].sem, 1)

            def values(i, x, u):
                if u == 0:
                    at(i, "v", x + 1)
                at(i, "p", 4 * x + u + 1)
                for j in range(GH):
                    last = nc.tensor.matmul(ps[BLK * j:BLK * (j + 1), 4, (u // 2) * S:(u // 2 + 1) * S],
                                            a_vg[:, 4 * (x % 2) + u, j, :], a_p[u % 2][:, j * S:(j + 1) * S],
                                            start=u % 2 == 0, stop=u % 2 == 1)
                last.then_inc(A["pv"].sem, 1)

            def sums_back(i, x):
                at(i, "raw", x + 1)
                for t in range(4 * (x % 2), 4 * (x % 2) + 4):
                    last = nc.tensor.transpose(ps[:, 5, (t % 4) * P:(t % 4 + 1) * P],
                                               a_raw[:, t * P:(t + 1) * P], ident)
                last.then_inc(A["rt"].sem, 1)

            def slot(i, x, projecting, maxing):
                def more(*tiles):
                    for n in tiles if maxing else ():
                        maxima(i, x + 1, n)

                at(i, "yf", x + 1)
                scores(x, 0)
                more(0, 1)
                if projecting:
                    project(i, x + 2, 0)
                scores(x, 1)
                values(i, x, 0)
                scores(x, 2)
                more(2, 3)
                if projecting:
                    project(i, x + 2, 1)
                values(i, x, 1)
                scores(x, 3)
                more(4, 5)
                values(i, x, 2)
                more(6)
                values(i, x, 3)
                more(7)
                if projecting:
                    at(i, "y", 2 * (x + 2) + 2)
                sums_back(i, x)
                if maxing:
                    at(i, "att", x + 1)
                    maxima_back(i, x + 1)

            for x in range(2):
                pe.wait_ge(s_xs, 2 * splits(m) + x + 1)
                if x:
                    at(0, "y", 2)
                project(0, x, 0)
                project(0, x, 1)
            for n in range(8):
                maxima(0, 0, n)
            at(0, "y", 4)
            maxima_back(0, 0)
            small_passes(pe, slot)

        def small_act(act, c):
            if c == 0:
                act.wait_ge(s_va, 1)
            else:
                act.wait_ge(ld["ctx_tok"], 16)
            vsrc = a_vall if c == 0 else ctok[:, :, :].rearrange("p t d -> p (t d)")
            vsrc = vsrc.rearrange("p (t d) -> p t d", t=NT)

            def at(i, name, k):
                act.wait_ge(A[name].sem, A[name].at(c, i, k))

            def high(i, x, k, used=True):
                at(i, "q", 2 * x + k + 1)
                if used:
                    at(i, "y", 2 * (x - 1) + k + 1)
                nc.scalar.activation(half(a_hi, k), bank(5), ACT.Copy).then_inc(A["hi"].sem, 1)

            def value_tiles(i, x):
                t = slice(4 * (x % 2), 4 * (x % 2) + 4)
                nc.scalar.activation(a_vg[:, t, :, 0:DH8],
                                     vsrc[:, t, bass.ds((i + x // 2) * BLK, BLK)].rearrange("p t (j d) -> p t j d", j=GH),
                                     ACT.Copy).then_inc(A["v"].sem, 1)

            def slot(i, x, projecting, maxing):
                for u in range(4):
                    if projecting and u in (1, 3):
                        high(i, x + 2, u // 2)
                    at(i, "s", 4 * x + u + 1)
                    if u >= 2:
                        at(i, "pv", 4 * x + u - 1)
                    nc.scalar.activation(a_p[u % 2], bank(2 * (u % 2), 2), ACT.Exp,
                                         scale=float(1.0 / np.sqrt(np.float32(DH8)))).then_inc(A["p"].sem, 1)
                at(i, "pv", 4 * x + 4)
                nc.scalar.activation(half(a_raw, x % 2), bank(4), ACT.Copy).then_inc(A["raw"].sem, 1)
                if projecting:
                    value_tiles(i, x + 2)

            act.wait_ge(s_ainit, c + 1)
            for x in range(2):
                value_tiles(0, x)
            for x in range(2):
                for k in range(2):
                    high(0, x, k, used=x == 1)
            small_passes(act, slot)

        def small_pool(pool, c):
            for t in (a_m2, a_vg):
                nc.gpsimd.memset(t, 0.0).then_inc(s_acl, 1)
            pool.wait_ge(s_acl, 2 * (c + 1))
            nc.gpsimd.memset(a_vg[:, :, :, DH8:DH8 + 1], 1.0).then_inc(s_ainit, 1)

        def small_weights(dve, c, i, raw, r0, loaded=None):
            if loaded is not None:
                dve.wait_ge(loaded, 16)
            wqk = raw[:, bass.ds(i * W_A + r0, 2 * P)]
            nc.vector.tensor_copy(a_wh, wqk).then_inc(A["w"].sem, 1)
            dve.wait_ge(A["w"].sem, A["w"].at(c, i, 1))
            nc.vector.tensor_tensor(a_wl, wqk, a_wh.bitcast(F32), ALU.subtract).then_inc(A["w"].sem, 1)

        def small_dve(dve, order, c, raw, r0, before_last=None):
            def at(i, name, k):
                dve.wait_ge(A[name].sem, A[name].at(c, i, k))

            def stack(i, x, k):
                at(i, "hi", 2 * x + k + 1)
                nc.vector.scalar_tensor_tensor(out=half((a_y, a_ky)[k], x % 2), in0=half(a_hi, k).bitcast(F32),
                                               scalar=col(("lo_q", "lo_k")[k]), in1=bank(5),
                                               op0=ALU.mult, op1=ALU.add).then_inc(A["y"].sem, 1)

            def masked_keys(i, x, heads=range(GH)):
                at(i, "y", 2 * x + 2)
                for j in heads:
                    nc.vector.tensor_scalar(half(a_km[j], x % 2), half(a_ky, x % 2).bitcast(F32), col("one_rows"),
                                            col("head", j, 1), ALU.add, ALU.mult).then_inc(A["km"].sem, 1)

            def largest(i, x, n):
                t, j0 = 4 * (x % 2) + n // 2, 2 * (n % 2)
                at(i, "mx", 8 * x + n + 1)
                nc.vector.tensor_reduce(a_nm[:, t, j0:j0 + 2], bank(6 + n % 2).rearrange("p (j k) -> p j k", j=2),
                                        AX.X, ALU.max, negate=True).then_inc(A["red"].sem, 1)

            def minus(i, x):
                h = x % 2
                at(i, "red", 8 * x + 8)
                nm = a_nm[:, 4 * h:4 * h + 4, :]
                hi = a_m2[:, 4 * h:4 * h + 4, :, 24]
                lo = a_m2[:, 4 * h:4 * h + 4, :, 25]
                order.step(nc.vector.tensor_copy(hi.bitcast(F32R), nm))
                nc.vector.tensor_tensor(lo.bitcast(F32R), nm, hi, ALU.subtract).then_inc(A["m2"].sem, 1)

            def queries(i, x):
                at(i, "mt", x + 1)
                nc.vector.tensor_tensor(half(a_yf, x % 2), bank(5), half(a_y, x % 2).bitcast(F32), ALU.add)\
                    .then_inc(A["yf"].sem, 1)

            def normalise(i, x):
                at(i, "rt", x + 1)
                h = x % 2
                sums = bank(5).rearrange("p (t j c) -> p t j c", t=4, j=GH)
                rec = a_rec[:, 4 * h:4 * h + 4, :]
                order.step(nc.vector.reciprocal(rec, sums[:, :, :, DH8]))
                nc.vector.tensor_tensor(
                    a_att[:, 4 * h:4 * h + 4, bass.ds(i * BLK, BLK)].rearrange("p t (j d) -> p t j d", j=GH),
                    sums[:, :, :, 0:DH8], rec.unsqueeze(3).to_broadcast((P, 4, GH, DH8)), ALU.mult)\
                    .then_inc(A["att"].sem, 1)

            def slot(i, x, projecting, maxing):
                if projecting and x == 0:
                    at(i, "q", 4)
                    small_weights(dve, c, i + 1, raw, r0)
                def more(*tiles):
                    for n in tiles if maxing else ():
                        largest(i, x + 1, n)

                more(0, 1)
                if projecting:
                    stack(i, x + 2, 0)
                more(2, 3)
                if projecting:
                    stack(i, x + 2, 1)
                more(4, 5, 6)
                normalise(i, x)
                more(7)
                if maxing:
                    minus(i, x + 1)
                if projecting:
                    at(i, "s", 4 * x + 4)
                    masked_keys(i, x + 2, (0, 1, 2))
                if maxing:
                    queries(i, x + 1)
                if projecting:
                    masked_keys(i, x + 2, (3,))

            for x in range(2):
                stack(0, x, 0)
                stack(0, x, 1)
                masked_keys(0, x)
            for n in range(8):
                largest(0, 0, n)
            dve.wait_ge(s_ainit, c + 1)
            minus(0, 0)
            queries(0, 0)
            with dve.Fori(0, NG - 1) as i:
                order.loop(i, 4)
                slot(i, 0, True, True)
                slot(i, 1, True, True)
            order.end(NG - 1)
            slot(NG - 1, 0, False, True)
            if before_last is not None:
                before_last()
            slot(NG - 1, 1, False, False)

        def small_out_pe(pe):
            pe.wait_ge(A["att"].sem, A["att"].at(0, NG, 0))
            for h in range(2):
                for t in range(4 * h, 4 * h + 4):
                    last = nc.tensor.transpose(ps[:, h, (t % 4) * P:(t % 4 + 1) * P], a_att[:, t, :], ident)
                last.then_inc(s_ot, 1)
            pe.wait_ge(s_oc, 2)
            tokens_pe(a_att_t, col("wo0"))

        def small_out_act(act):
            for h in range(2):
                act.wait_ge(s_ot, h + 1)
                nc.scalar.activation(half(a_att_t, h), bank(h), ACT.Copy).then_inc(s_oc, 1)

        W = signals("w", NQ, w=2, qk=8, eh=12, el=12, vp=4, va=4, s=8, y=8, p=8, ps=8, pv=8, pvc=4, dn=4,
                    rec=4, rb=4, at=4, o=4, acc=4)
        s_wcl, s_winit = sem("w_keys_cleared"), sem("w_cleared")
        w_q = (wr[:, 0:1024], wr[:, 1024:2048])
        w_k = [(wr[:, 2048 + 2048 * h:3072 + 2048 * h], wr[:, 3072 + 2048 * h:4096 + 2048 * h]) for h in range(2)]
        w_w = (wr[:, 6144:6912], wr[:, 6912:7680])
        w_v = wf[:, 0:2048].rearrange("p (t c) -> p t c", t=NT)
        w_p = [wf[:, 2048 + 1024 * k:3072 + 1024 * k] for k in range(3)]
        w_ps = [wf[:, 5120 + 512 * k:5632 + 512 * k] for k in range(2)]
        w_pv, w_at, w_rec = wf[:, 6144:6656], wf[:, 6656:7168], wf[:, 7168:7424]
        w_den, w_ones = wf[:, 7680:7936], wf[:, 7936:7968]

        def wide_passes(eng, body):
            with eng.Fori(0, NQ - 1) as i:
                body(i, True)
            body(NQ - 1, False)

        def wide_pe(pe, c, m, raw, r0):
            def at(i, name, k):
                pe.wait_ge(W[name].sem, W[name].at(c, i, k))

            def project(i, k):
                p, h = k // 2 % 2, k % 2
                at(i, "w", 2 * (k // 4) + 2)
                for n in range(2):
                    w = [t[:, n * QW + p * P:n * QW + (p + 1) * P] for t in w_w]
                    src = (half(ch, h), half(cl, h)) if n else (half(xh, h), half(xl, h))
                    if n == 1 and k in (3, 4, 5):
                        at(i, "el", 3 * k)
                    mm3(bank(6 + n), w, src).then_inc(W["qk"].sem, 1)

            def value_tiles(n):
                for t in range(2):
                    tile = slice((2 * (n % 4) + t) * P, (2 * (n % 4) + t + 1) * P)
                    last = mm3(ps[:, 6 + n % 2, t * QW:(t + 1) * QW], (ch[:, tile], cl[:, tile]),
                               [v[:, 2 * QW:3 * QW] for v in w_w])
                last.then_inc(W["vp"].sem, 1)

            def scores(i, g):
                b = g % 4
                if b % 2 == 0:
                    at(i, "el", 3 * (g // 2) + 3)
                if g >= 2:
                    at(i, "y", g - 1)
                for h in range(2):
                    for kb in range(2):
                        keys = slice(b * S + kb * P, b * S + (kb + 1) * P)
                        last = mm3(ps[:, 2 * (g % 2) + h, kb * S:(kb + 1) * S], [t[:, keys] for t in w_k[h]],
                                   [t[:, b * S:(b + 1) * S] for t in w_q])
                last.then_inc(W["s"].sem, 1)

            def values(i, g):
                b, p = g % 4, g // 4
                at(i, "p", g + 1)
                if g == 0:
                    at(i, "va", 4)
                elif g % 2 == 0:
                    at(i, "pvc", g // 2)
                for kb in range(2):
                    for h in range(2):
                        last = nc.tensor.matmul(ps[DH * h:DH * (h + 1), 4, (b % 2) * S:(b % 2 + 1) * S],
                                                w_v[:, 2 * b + kb, (2 * p + h) * DH:(2 * p + h + 1) * DH],
                                                w_p[g % 3][:, (2 * h + kb) * S:(2 * h + kb + 1) * S],
                                                start=kb == 0, stop=kb == 1)
                last.then_inc(W["pv"].sem, 1)

            def denominators(i, k):
                if k:
                    at(i, "at", k)
                at(i, "ps", 2 * k + 2)
                for h in range(2):
                    for b in range(2):
                        r = BLK * (2 * h + b)
                        last = nc.tensor.matmul(ps[r:r + BLK, 5, 0:S], w_ones, w_ps[b][:, h * S:(h + 1) * S],
                                                start=True, stop=True)
                last.then_inc(W["dn"].sem, 1)

            def spread(i, k):
                at(i, "rec", k + 1)
                for b in range(2):
                    last = nc.tensor.matmul(ps[:, 5, b * S:(b + 1) * S], col("spread", b * P, P), w_rec,
                                            start=True, stop=True)
                last.then_inc(W["rb"].sem, 1)

            def output(i, k):
                at(i, "at", k + 1)
                wo = raw[:, bass.ds(i * W_B + (r0 + 3 * QW + (k // 2) * P), P)]
                for t in range(4):
                    last = nc.tensor.matmul(ps[:, 6, t * P:(t + 1) * P], w_at[:, t * P:(t + 1) * P], wo,
                                            start=True, stop=True)
                last.then_inc(W["o"].sem, 1)

            def body(i, ahead):
                for g in range(8):
                    k = g // 2
                    values(i, g)
                    if g + 2 < 8 or ahead:
                        scores(i, g + 2)
                    if g % 2 == 0:
                        if k >= 1:
                            spread(i, k - 1)
                        if k < 2 or ahead:
                            at(i, "acc", (0, 0, 1, 2)[k])
                            if k == 0:
                                at(i, "va", 4)
                            if k == 1:
                                at(i, "el", 7)
                            project(i, k + 2)
                        if g == 6 and ahead:
                            at(i, "el", 16)
                            value_tiles(4)
                    else:
                        denominators(i, k)
                        if k == 3 and ahead:
                            at(i, "el", 18)
                            value_tiles(5)
                        if k == 1:
                            at(i, "el", 10)
                        elif k == 2:
                            at(i, "acc", 1)
                            if ahead:
                                at(i, "el", 13)
                        elif k == 3:
                            at(i, "acc", 2)
                            if ahead:
                                at(i, "va", 5)
                        if k >= 1:
                            output(i, k - 1)
                at(i, "acc", 3)
                if ahead:
                    value_tiles(6)
                spread(i, 3)
                if ahead:
                    at(i, "va", 6)
                    value_tiles(7)
                    at(i, "va", 7)
                output(i, 3)

            pe.wait_ge(s_xs, 2 * splits(m) + 2)
            project(0, 0)
            for n in range(4):
                if n < 2:
                    at(0, "el", (1, 3)[n])
                else:
                    at(0, "va", n - 1)
                value_tiles(n)
            at(0, "va", 4)
            project(0, 1)
            pe.wait_ge(s_winit, c + 1)
            scores(0, 0)
            scores(0, 1)
            at(0, "el", 6)
            wide_passes(pe, body)

        def wide_act(act, c, func, bias):
            def at(i, name, k):
                act.wait_ge(W[name].sem, W[name].at(c, i, k))

            def high(i, k):
                h = k % 2
                if k >= 2:
                    at(i, "s", 2 * k - 2)
                at(i, "qk", 2 * k + 1)
                nc.scalar.activation(half(w_q[0], h), bank(6), ACT.Copy).then_inc(W["eh"].sem, 1)
                at(i, "qk", 2 * k + 2)
                for j in range(2):
                    rows = slice(DH * j, DH * (j + 1))
                    nc.scalar.activation(half(w_k[j][0], h)[rows, :], ps[rows, 7, :], ACT.Copy)\
                        .then_inc(W["eh"].sem, 1)

            def sums(i, k):
                at(i, "pv", 2 * k + 2)
                if k:
                    at(i, "at", k)
                nc.scalar.activation(w_pv, bank(4), ACT.Copy).then_inc(W["pvc"].sem, 1)

            def value_tiles(i, n):
                if n >= 4:
                    at(i, "pv", 6 if n < 6 else 8)
                at(i, "vp", n + 1)
                m = n % 4
                nc.scalar.activation(w_v[:, 2 * m:2 * m + 2, :].rearrange("p t c -> p (t c)"),
                                     bank(6 + n % 2), ACT.Copy).then_inc(W["va"].sem, 1)

            def weights(i, g):
                at(i, "y", g + 1)
                p = w_p[g % 8 % 3]
                nc.scalar.activation(p, p, func, bias=bias, scale=0.125).then_inc(W["p"].sem, 1)

            def body(i, ahead):
                high(i, 2)
                for g in range(2, 8):
                    k = g // 2
                    weights(i, g)
                    if g % 2 == 0:
                        sums(i, k - 1)
                    elif k < 2 or ahead:
                        high(i, k + 2)
                if ahead:
                    value_tiles(i, 4)
                sums(i, 3)
                if ahead:
                    weights(i, 8)
                    value_tiles(i, 5)
                    weights(i, 9)
                    value_tiles(i, 6)
                    value_tiles(i, 7)

            high(0, 0)
            for n in range(4):
                value_tiles(0, n)
            high(0, 1)
            weights(0, 0)
            weights(0, 1)
            wide_passes(act, body)

        def wide_pool_init(pool, c, n):
            pool.wait_ge(s_pow, n + 1)
            for j in range(2):
                rows = slice(DH * (1 - j), DH * (2 - j))
                for t in w_k[j]:
                    nc.gpsimd.memset(t[rows, :].bitcast(F32), 0.0).then_inc(s_wcl, 1)
                pool.wait_ge(s_wcl, 4 * c + 2 * (j + 1))
            nc.gpsimd.memset(w_ones, 1.0).then_inc(s_winit, 1)
            pool.wait_ge(s_winit, c + 1)

        def wide_pool(pool, c):
            def add(i, g):
                pool.wait_ge(W["p"].sem, W["p"].at(c, i, g + 1))
                if g >= 2:
                    pool.wait_ge(W["dn"].sem, W["dn"].at(c, i, g // 2))
                v = w_p[g % 8 % 3].rearrange("p (h k q) -> p h k q", h=2, k=2)
                nc.gpsimd.tensor_tensor(w_ps[g % 2].rearrange("p (h q) -> p h q", h=2), v[:, :, 0, :],
                                        v[:, :, 1, :], ALU.add).then_inc(W["ps"].sem, 1)

            def body(i, ahead):
                for g in range(2, 10 if ahead else 8):
                    add(i, g)

            add(0, 0)
            add(0, 1)
            wide_passes(pool, body)

        def wide_weights(dve, c, i, raw, r0, loaded=None):
            if loaded is not None:
                dve.wait_ge(loaded, 16)
            qkv = raw[:, bass.ds(i * W_B + r0, 3 * QW)]
            nc.vector.tensor_copy(w_w[0], qkv).then_inc(W["w"].sem, 1)
            dve.wait_ge(W["w"].sem, W["w"].at(c, i, 1))
            nc.vector.tensor_tensor(w_w[1], qkv, w_w[0].bitcast(F32), ALU.subtract).then_inc(W["w"].sem, 1)

        def wide_dve(dve, order, c, raw, r0):
            def at(i, name, k):
                dve.wait_ge(W[name].sem, W[name].at(c, i, k))

            def low(i, k):
                h = k % 2
                at(i, "eh", 3 * k + 1)
                nc.vector.tensor_tensor(half(w_q[1], h), bank(6), half(w_q[0], h).bitcast(F32), ALU.subtract)\
                    .then_inc(W["el"].sem, 1)
                at(i, "eh", 3 * k + 3)
                for j in range(2):
                    rows = slice(DH * j, DH * (j + 1))
                    nc.vector.tensor_tensor(half(w_k[j][1], h)[rows, :], ps[rows, 7, :],
                                            half(w_k[j][0], h)[rows, :].bitcast(F32), ALU.subtract)\
                        .then_inc(W["el"].sem, 1)

            def bound(i, g):
                at(i, "s", g + 1)
                if g >= 3:
                    at(i, "ps", g - 2 if g < 8 else g - 1)
                v = w_p[g % 8 % 3].rearrange("p (h c) -> p h c", h=2)
                s = ps[:, 2 * (g % 2):2 * (g % 2) + 2, :]
                if c == 0:
                    ins = nc.vector.scalar_tensor_tensor(
                        out=v, in0=s, scalar=w_floor, op0=ALU.max, op1=ALU.min,
                        in1=cap[:, g % 4, :, :].rearrange("p k q -> p (k q)").unsqueeze(1).to_broadcast((P, 2, HALF)))
                else:
                    ins = nc.vector.tensor_scalar(v, s, -8.0 * CLIP, 8.0 * CLIP, ALU.max, ALU.min)
                ins.then_inc(W["y"].sem, 1)

            def reciprocal(i, k):
                at(i, "dn", k + 1)
                if c == 0:
                    order.step(nc.vector.tensor_scalar(w_den, ps[:, 5, 0:S], IEPS, None, ALU.add))
                    nc.vector.reciprocal(w_rec, w_den).then_inc(W["rec"].sem, 1)
                else:
                    nc.vector.reciprocal(w_rec, ps[:, 5, 0:S]).then_inc(W["rec"].sem, 1)

            def normalise(i, k):
                at(i, "rb", k + 1)
                at(i, "pvc", k + 1)
                nc.vector.tensor_tensor(w_at, w_pv, bank(5), ALU.mult).then_inc(W["at"].sem, 1)

            def add(i, k):
                at(i, "o", k + 1)
                at(i, "acc", k)
                h = k % 2
                r = xn[:, 4 * h:4 * h + 4, :].rearrange("p t d -> p (t d)")
                nc.vector.tensor_tensor(r, r, bank(6), ALU.add).then_inc(W["acc"].sem, 1)

            def body(i, ahead):
                for k in range(4):
                    if k < 3 or ahead:
                        bound(i, 2 * k + 2)
                    if k:
                        normalise(i, k - 1)
                    if k < 2 or ahead:
                        low(i, k + 2)
                    if k < 3 or ahead:
                        bound(i, 2 * k + 3)
                    if k == 1 and ahead:
                        at(i, "qk", 8)
                        wide_weights(dve, c, i + 1, raw, r0)
                    reciprocal(i, k)
                    if k:
                        add(i, k - 1)
                normalise(i, 3)
                add(i, 3)

            low(0, 0)
            low(0, 1)
            bound(0, 0)
            bound(0, 1)
            per = 4 if c == 0 else 0
            with dve.Fori(0, NQ - 1) as i:
                order.loop(i, per)
                body(i, True)
            order.end(NQ - 1)
            body(NQ - 1, False)

        def tokens_in(dve, order, n, src):
            for h in range(2):
                r = res[:, 4 * h:4 * h + 4, :].rearrange("p t d -> p (t d)")
                s = src[:, 4 * h:4 * h + 4, :].rearrange("p t d -> p (t d)")
                order.done(nc.vector.scalar_tensor_tensor(out=r, in0=s, scalar=gate[:, n:n + 1], in1=r,
                                                          op0=ALU.mult, op1=ALU.add))
            order.wait()

        def pick_max(order, oh, s, t1, m):
            order.step(nc.vector.tensor_reduce(m, s, AX.X, ALU.max))
            mb = m.unsqueeze(2).to_broadcast((P, NT, E))
            order.step(nc.vector.tensor_tensor(t1, s, mb, ALU.is_equal))
            iota = col("iota").unsqueeze(1).to_broadcast((P, NT, E))
            order.step(nc.vector.tensor_scalar(t1, t1, -float(E), None, ALU.mult))
            order.step(nc.vector.tensor_tensor(t1, t1, iota, ALU.add))
            order.step(nc.vector.tensor_reduce(m2col, t1, AX.X, ALU.min))
            order.step(nc.vector.tensor_tensor(oh, t1, m2col.unsqueeze(2).to_broadcast((P, NT, E)), ALU.is_equal))

        def split_stack(order, w, at, last=False):
            hi, lo = stk[:, :, at:at + E], stk[:, :, at + E:at + 2 * E]
            order.step(nc.vector.tensor_copy(hi.bitcast(F32R), w))
            ins = nc.vector.tensor_tensor(lo.bitcast(F32R), w, hi, ALU.subtract)
            if last:
                ins.then_inc(s_st, 1)
            else:
                order.step(ins)

        sp_ = [sb(f"router_{k}", [P, NT, E]) for k in range(5)]
        lg, ex, t1, oh, oh2 = [t[:, :, :] for t in sp_]
        mcol_t, m2col_t, rcol_t = sb("router_max", [P, NT]), sb("router_first", [P, NT]), sb("router_sum", [P, NT])
        mcol, m2col, rcol = mcol_t[:, :], m2col_t[:, :], rcol_t[:, :]
        stk_t = sb("router_stack", [P, NT, BLK])
        stk = stk_t[:, :, :]
        s_lg, s_lx, s_le, s_st, s_sk, s_wt = [sem(n) for n in (
            "logits_product", "logits_less_max", "logits_exponentials", "stack_ready", "stack_transposed", "stack_copied")]

        def softmax_dve(dve, order, n):
            order.step(nc.vector.tensor_reduce(mcol, lg, AX.X, ALU.max))
            nc.vector.tensor_tensor(lg, lg, mcol.unsqueeze(2).to_broadcast((P, NT, E)), ALU.subtract).then_inc(s_lx, 1)
            dve.wait_ge(s_le, n + 1)
            order.step(nc.vector.tensor_reduce(rcol, ex, AX.X, ALU.add))
            order.step(nc.vector.reciprocal(rcol, rcol))
            order.step(nc.vector.tensor_tensor(ex, ex, rcol.unsqueeze(2).to_broadcast((P, NT, E)), ALU.mult))

        def softmax_act(act, n, scale=1.0):
            act.wait_ge(s_lx, n + 1)
            nc.scalar.activation(ex, lg, ACT.Exp, scale=scale).then_inc(s_le, 1)

        def logits_pe(src, w, k):
            for t in range(NT):
                last = nc.tensor.matmul(ps[:, k, t * E:(t + 1) * E], src[:, t * P:(t + 1) * P], w, start=True, stop=True)
            last.then_inc(s_lg, 1)

        def stack_pe(pe, n):
            pe.wait_ge(s_st, n + 1)
            for t in range(NT):
                last = nc.tensor.transpose(ps[0:BLK, 6 + t // 4, (t % 4) * P:(t % 4 + 1) * P], stk[:, t, :], ident)
            last.then_inc(s_sk, 1)

        def stack_act(act, n, wt):
            act.wait_ge(s_sk, n + 1)
            nc.scalar.activation(wt[0:BLK, :], ps[0:BLK, 6:8, :].rearrange("p a b -> p (a b)"), ACT.Copy).then_inc(s_wt, 1)

        F = signals("f0", NKT, w=8, x=4, yw=4, xs=4, z=4, u=4, acc=4)
        s_fp, s_fh, s_fl, s_fc, s_fb, s_fo = [sem("f0_" + n) for n in ("product", "high", "low", "sums_split", "bias", "whole")]
        f_slots = [(wr[:, 1024 * 2 * k:1024 * (2 * k + 1)], wr[:, 1024 * (2 * k + 1):1024 * (2 * k + 2)]) for k in range(3)]
        f_q, f_k, f_ik = f_slots
        f_iq = (xh[:, :], xl[:, :])
        f_wt = wr[:, 6144:7168]
        f_w = (wr[:, 7168:7680], wr[:, 7680:8192])
        f_vw = [(wr[:, 8192 + 640 * b:8448 + 640 * b], wr[:, 8448 + 640 * b:8704 + 640 * b]) for b in range(2)]
        f_sel = [wr[:, 8704 + 640 * b:8832 + 640 * b] for b in range(2)]
        f_cum = wf[:, 0:1024]
        f_xs = [wf[:, 1024 + 512 * k:1536 + 512 * k] for k in range(2)]
        f_z = [wf[:, 2048 + 512 * k:2560 + 512 * k] for k in range(2)]
        f_u = [wf[:, 3072 + 128 * k:3200 + 128 * k] for k in range(2)]
        f_ones = wf[:, 3328:3584]
        f_h = [wf[:, 4096 + 1024 * k:5120 + 1024 * k] for k in range(2)]
        f_zz = [wf[:, 6144 + 512 * k:6656 + 512 * k] for k in range(2)]
        f_steps = ((0, "x", f_q), (1, "cum", f_k), (2, "q", f_iq), (2, "k", f_ik), (3, "q", None), (3, "iq", None))

        def f0_pe(pe, m):
            pe.wait_ge(s_xs, 2 * splits(m) + 2)
            pe.wait_ge(s_fc, 1)
            src = {"x": (xh[:, :], xl[:, :]), "cum": f_ik, "q": f_q, "k": f_k, "iq": f_iq}
            low = {2: 1, 3: 2, 4: 1, 5: 3}
            for j, (w, s, _) in enumerate(f_steps):
                if j in low:
                    pe.wait_ge(s_fl, low[j])
                if j >= 3:
                    pe.wait_ge(s_fl, j - 2)
                for h in range(2):
                    last = mm3(bank(2 * (j % 3) + h), [v[:, w * P:(w + 1) * P] for v in f_w],
                               [half(v, h) for v in src[s]])
                last.then_inc(s_fp, 1)
            for br in range(2):
                pe.wait_ge(s_fh, 5 + br)
                logits_pe(f_h[br], col("router_w2"), 6 + br)
            stack_pe(pe, 0)
            pe.wait_ge(s_wt, 1)
            pe.wait_ge(s_fl, 4)
            with pe.Fori(0, NKT) as i:
                def at(name, k):
                    pe.wait_ge(F[name].sem, F[name].at(0, i, k))

                def products(n):
                    br, h = n // 2, n % 2
                    if h == 0:
                        at("w", 4 * br + 4)
                    at("xs", max(0, n - 1))
                    at("z", max(0, n - 1))
                    q, k = ((f_q, f_k), (f_iq, f_ik))[br]
                    mm3(bank(h), [v[:, 0:P] for v in f_vw[br]], [half(v, h) for v in q]).then_inc(F["x"].sem, 1)
                    mm3(bank(2 + h), [v[:, P:2 * P] for v in f_vw[br]], [half(v, h) for v in k])
                    nc.tensor.matmul(bank(4 + h), f_sel[br], half(f_wt, h), start=True, stop=True)\
                        .then_inc(F["yw"].sem, 1)

                def out(n):
                    br, h = n // 2, n % 2
                    at("z", n + 1)
                    at("acc", max(0, n - 1))
                    nc.tensor.matmul(bank(6 + h), f_u[br], f_zz[h], start=True, stop=True).then_inc(F["u"].sem, 1)

                products(0)
                products(1)
                for n in range(4):
                    out(n)
                    if n + 2 < 4:
                        products(n + 2)
            pe.wait_ge(F["acc"].sem, F["acc"].at(0, NKT, 0))
            for h in range(2):
                last = nc.tensor.matmul(bank(6 + h), col("b_experts"), half(f_wt, h).bitcast(F32), start=True, stop=True)
            last.then_inc(s_fb, 1)
            pe.wait_ge(s_fo, 1)
            tokens_pe(out_t, col("W_O"))

        def f0_act(act):
            for j, (_, _, dst) in enumerate(f_steps):
                act.wait_ge(s_fp, j + 1)
                if dst is None:
                    ins = nc.scalar.activation(f_h[j - 4], bank(2 * (j % 3), 2), ACT.Gelu, bias=col("rb1"))
                else:
                    ins = nc.scalar.activation(dst[0], bank(2 * (j % 3), 2), ACT.Copy)
                ins.then_inc(s_fh, 1)
            for br in range(2):
                softmax_act(act, br)
            stack_act(act, 0, f_wt)
            with act.Fori(0, NKT) as i:
                for n in range(4):
                    act.wait_ge(F["x"].sem, F["x"].at(0, i, n + 1))
                    act.wait_ge(F["z"].sem, F["z"].at(0, i, max(0, n - 1)))
                    nc.scalar.activation(f_xs[n % 2], bank(n % 2), ACT.Copy).then_inc(F["xs"].sem, 1)

        def f0_weights(dve, order):
            order.step(nc.vector.tensor_copy(f_w[0], col("W_Q", 0, 4 * P)))
            order.done(nc.vector.tensor_tensor(f_w[1], col("W_Q", 0, 4 * P), f_w[0].bitcast(F32), ALU.subtract))

        def clear_pool(pool, n, t, *values):
            for v, x in values:
                nc.gpsimd.memset(v, x).then_inc(s_pcl, 1)
            pool.wait_ge(s_pcl, t)
            nc.gpsimd.memset(out_t[:, :], 0.0).then_inc(s_clear, 1)
            pool.wait_ge(s_clear, n + 1)

        def f0_dve(dve, order):
            dve.wait_ge(s_clear, 1)
            for b in range(B):
                order.done(nc.vector.tensor_tensor_scan(f_cum[:, b * S:(b + 1) * S], f_ones, xf[:, b * S:(b + 1) * S],
                                                        0.0, ALU.mult, ALU.add))
            order.wait()
            order.step(nc.vector.tensor_copy(f_ik[0], f_cum))
            nc.vector.tensor_tensor(f_ik[1], f_cum, f_ik[0].bitcast(F32), ALU.subtract).then_inc(s_fc, 1)
            for j in range(4):
                dve.wait_ge(s_fh, j + 1)
                dst = f_steps[j][2]
                nc.vector.tensor_tensor(dst[1], bank(2 * (j % 3), 2), dst[0].bitcast(F32), ALU.subtract).then_inc(s_fl, 1)
            for br in range(2):
                dve.wait_ge(s_lg, br + 1)
                src = ps[:, 6 + br, 0:NT * E].rearrange("p (t e) -> p t e", t=NT)
                order.step(nc.vector.tensor_tensor(lg, src, col("rb2").unsqueeze(1).to_broadcast((P, NT, E)), ALU.add))
                order.step(nc.vector.tensor_tensor(lg, lg, col("ebias").unsqueeze(1).to_broadcast((P, NT, E)), ALU.add))
                softmax_dve(dve, order, br)
                e2 = ex.rearrange("p (b q) e -> p b q e", b=B)
                for q in range(2):
                    order.done(nc.vector.tensor_scalar(e2[:, :, q, :], e2[:, :, q, :], col("inv_n", q, 1), None, ALU.mult))
                order.wait()
                if br:
                    order.step(nc.vector.tensor_scalar(ex, ex, col("alpha"), None, ALU.mult))
                split_stack(order, ex, 2 * E * br, br == 1)
            dve.wait_ge(ld["f0"], 16)
            dve.wait_ge(s_wt, 1)
            with dve.Fori(0, NKT) as i:
                order.loop(i, 4)

                def at(name, k):
                    dve.wait_ge(F[name].sem, F[name].at(0, i, k))

                def weights(br):
                    at("yw", 0)
                    at("u", 0)
                    base = i * (2 * W_F0) + (RF0 + br * W_F0)
                    vw = raw_a[:, bass.ds(base, 2 * P)]
                    nc.vector.tensor_copy(f_vw[br][0], vw).then_inc(F["w"].sem, 1)
                    nc.vector.tensor_copy(f_u[br], raw_a[:, bass.ds(base + 2 * P, P)]).then_inc(F["w"].sem, 1)
                    nc.vector.tensor_copy(f_sel[br], raw_a[:, bass.ds(base + 3 * P, P)]).then_inc(F["w"].sem, 1)
                    at("w", 4 * br + 1)
                    nc.vector.tensor_tensor(f_vw[br][1], vw, f_vw[br][0].bitcast(F32), ALU.subtract)\
                        .then_inc(F["w"].sem, 1)

                def weigh(n):
                    h = n % 2
                    at("xs", n + 1)
                    at("yw", n + 1)
                    order.step(nc.vector.tensor_tensor(f_z[h], f_xs[h], bank(2 + h), ALU.mult))
                    at("u", max(0, n - 1))
                    nc.vector.tensor_tensor(f_zz[h], f_z[h], bank(4 + h), ALU.mult).then_inc(F["z"].sem, 1)

                def add(n):
                    h = n % 2
                    at("u", n + 1)
                    at("acc", max(0, n - 1))
                    nc.vector.tensor_tensor(half(out_t, h), half(out_t, h), bank(6 + h), ALU.add)\
                        .then_inc(F["acc"].sem, 1)

                weights(0)
                weights(1)
                weigh(0)
                weigh(1)
                for n in range(4):
                    add(n)
                    if n + 2 < 4:
                        weigh(n + 2)
            order.end(NKT)
            dve.wait_ge(F["acc"].sem, F["acc"].at(0, NKT, 0))
            dve.wait_ge(s_fb, 1)
            nc.vector.tensor_tensor(out_t[:, :], out_t[:, :], bank(6, 2), ALU.add).then_inc(s_fo, 1)

        G = signals("f1", E // 2, w=10, up=16, a=16, al=16, dn=16, cb=2, cc=2, t=4, acc=4)
        s_gb = sem("f1_bias_product")
        g_w = [(wr[:, 2048 * s:2048 * s + 1024], wr[:, 2048 * s + 1024:2048 * s + 2048]) for s in range(2)]
        g_a = [(wr[:, 4096 + 1024 * k:4608 + 1024 * k], wr[:, 4608 + 1024 * k:5120 + 1024 * k]) for k in range(4)]
        g_wt = wr[:, 8192:9216]
        g_sel = [wr[:, 9216 + 128 * k:9344 + 128 * k] for k in range(2)]
        g_af = [wf[:, 4096 + 512 * k:4608 + 512 * k] for k in range(4)]
        g_cw = wf[:, 1024:2048]
        g_t = [wf[:, 2048 + 512 * k:2560 + 512 * k] for k in range(2)]
        g_shift = wf[:, 3072:3072 + E * NF]
        g_b1 = [wf[:, 3104 + NF * k:3104 + NF * (k + 1)] for k in range(2)]
        PASSES = E // 2

        def passes(eng, body):
            with eng.Fori(0, PASSES - 1) as i:
                body(i, False)
            body(PASSES - 1, True)

        def f1_shifts_pe(pe):
            pe.wait_ge(ld["f1"], 16)
            for e in range(E):
                for f in range(NF):
                    last = nc.tensor.matmul(ps[:, 4, e * NF + f:e * NF + f + 1],
                                            raw_a[:, e * W_F1 + f * P:e * W_F1 + (f + 1) * P], col("beta", e, 1),
                                            start=True, stop=True)
            last.then_inc(s_gb, 1)

        def f1_pe(pe, m):
            pe.wait_ge(s_xf, 2 * m + 2)
            logits_pe(xf, col("centroids"), 5)
            def up(i, n):
                s, h, f = n // 8, n // 4 % 2, n % 4
                if n % 8 == 0:
                    pe.wait_ge(G["w"].sem, G["w"].at(0, i, 5 * s + 5))
                pe.wait_ge(G["a"].sem, G["a"].at(0, i, max(0, n - 2)))
                mm3(ps[:, (0, 1, 2, 7)[n % 4], :], [v[:, f * P:(f + 1) * P] for v in g_w[s % 2]],
                    (half(xh, h), half(xl, h))).then_inc(G["up"].sem, 1)

            def body(i, last_pass):
                def at(name, k):
                    pe.wait_ge(G[name].sem, G[name].at(0, i, k))

                def down(n):
                    s, h, f = n // 8, n // 4 % 2, n % 4
                    at("al", n + 1)
                    if f == 0:
                        at("t", max(0, 2 * (s - 1) + h + 1) if s else 0)
                    last = mm3(bank(3 + h), [v[:, 512 + f * P:512 + (f + 1) * P] for v in g_w[s]], g_a[n % 4],
                               start=f == 0, stop=f == NF - 1)
                    last.then_inc(G["dn"].sem, 1)

                for n in range(16):
                    if n + 2 < 16 or not last_pass:
                        up(i, n + 2)
                    if n % 8 == 2:
                        s = n // 8
                        at("cc", s)
                        for h in range(2):
                            last = nc.tensor.matmul(bank(5 + h), g_sel[s], half(g_wt, h), start=True, stop=True)
                        last.then_inc(G["cb"].sem, 1)
                    down(n)

            pe.wait_ge(s_xs, 2 * splits(m) + 2)
            up(0, 0)
            up(0, 1)
            stack_pe(pe, 1)
            pe.wait_ge(s_wt, 2)
            passes(pe, body)
            pe.wait_ge(G["acc"].sem, G["acc"].at(0, PASSES, 0))
            back_pe(pe)

        def f1_act(act):
            softmax_act(act, 2, scale=-1.0)
            stack_act(act, 1, g_wt)

            def body(i, last_pass):
                def at(name, k):
                    act.wait_ge(G[name].sem, G[name].at(0, i, k))

                for n in range(16):
                    s, f = n // 8, n % 4
                    at("up", n + 1)
                    at("al", max(0, n - 3))
                    at("dn", max(0, n - 3))
                    b, hidden = g_b1[s][:, f:f + 1], bank((0, 1, 2, 7)[n % 4])
                    nc.scalar.activation(g_af[n % 4], hidden, ACT.Relu, bias=b).then_inc(s_act, 1)
                    nc.scalar.activation(g_a[n % 4][0], hidden, ACT.Relu, bias=b).then_inc(G["a"].sem, 1)
                    if n % 8 == 4:
                        at("cb", s + 1)
                        at("t", 2 * s)
                        nc.scalar.activation(g_cw, bank(5, 2), ACT.Copy).then_inc(G["cc"].sem, 1)

            passes(act, body)

        def f1_pool(pool):

            def body(i, last_pass):
                for n in range(4):
                    h = n % 2
                    pool.wait_ge(G["t"].sem, G["t"].at(0, i, n + 1))
                    pool.wait_ge(G["acc"].sem, G["acc"].at(0, i, max(0, n - 1)))
                    nc.gpsimd.tensor_tensor(half(out_t, h), half(out_t, h), g_t[h], ALU.add).then_inc(G["acc"].sem, 1)

            passes(pool, body)

        def f1_piece(dve, i, s, k):
            def expert(base, n):
                return sm[:, bass.ds(i * (2 * n) + (s * n + SMALL[base][0]), n)]

            w1 = raw_a[:, bass.ds(i * (2 * W_F1) + s * W_F1, 512)]
            w2 = raw_a[:, bass.ds(i * (2 * W_F1) + (s * W_F1 + 512), 512)]
            (hi, lo), gam = g_w[s], expert("gamma", 1)
            if k == 0:
                ins = nc.vector.tensor_scalar(hi[:, 0:512], w1, gam, None, ALU.mult)
            elif k == 1:
                ins = nc.vector.tensor_copy(hi[:, 512:1024], w2)
            elif k == 2:
                dve.wait_ge(G["w"].sem, G["w"].at(0, i, 5 * s + 1))
                ins = nc.vector.scalar_tensor_tensor(out=lo[:, 0:512], in0=w1, scalar=gam,
                                                     in1=hi[:, 0:512].bitcast(F32), op0=ALU.mult, op1=ALU.subtract)
            elif k == 3:
                dve.wait_ge(G["w"].sem, G["w"].at(0, i, 5 * s + 2))
                ins = nc.vector.tensor_tensor(lo[:, 512:1024], w2, hi[:, 512:1024].bitcast(F32), ALU.subtract)
            else:
                nc.vector.tensor_tensor(g_b1[s], g_shift[:, bass.ds(i * (2 * NF) + s * NF, NF)], expert("b1", NF), ALU.add)
                ins = nc.vector.tensor_copy(g_sel[s], expert("sel_e", P))
            ins.then_inc(G["w"].sem, 1)

        def f1_first(dve):
            dve.wait_ge(ld["f1"], 16)
            for k in range(4):
                f1_piece(dve, 0, 0, k)

        def f1_shifts_dve(dve, order):
            dve.wait_ge(s_gb, 1)
            order.step(nc.vector.tensor_copy(g_shift, ps[:, 4, 0:E * NF]))
            f1_piece(dve, 0, 0, 4)

        def f1_dve(dve, order):
            dve.wait_ge(s_lg, 3)
            order.step(nc.vector.tensor_copy(lg, ps[:, 5, 0:NT * E].rearrange("p (t e) -> p t e", t=NT)))
            pick_max(order, oh, lg, t1, mcol)
            nc.vector.tensor_copy(lg, mcol.unsqueeze(2).to_broadcast((P, NT, E))).then_inc(s_lx, 1)
            dve.wait_ge(s_le, 3)
            order.step(nc.vector.tensor_scalar(ex, ex, 1.0, None, ALU.add))
            order.step(nc.vector.reciprocal(ex, ex))
            order.step(nc.vector.tensor_tensor(ex, ex, oh, ALU.mult))
            dve.wait_ge(s_clear, 2)
            split_stack(order, ex, 0, True)

            def body(i, last_pass):
                def at(name, k):
                    dve.wait_ge(G[name].sem, G[name].at(0, i, k))

                for n in range(16):
                    s, h, f = n // 8, n // 4 % 2, n % 4
                    at("a", n + 1)
                    at("dn", max(0, n - 3))
                    nc.vector.tensor_tensor(g_a[n % 4][1], g_af[n % 4], g_a[n % 4][0].bitcast(F32), ALU.subtract)\
                        .then_inc(G["al"].sem, 1)
                    if n % 8 == 1 or (n % 8 == 5):
                        q = (n - 5) // 4
                        if n > 1:
                            weigh(dve, i, q)
                    if 2 <= n % 8 <= 6 and not (s == 1 and last_pass):
                        k = n % 8 - 2
                        if k == 0:
                            at("dn", 8 * s)
                            at("cb", s)
                        if s == 0:
                            f1_piece(dve, i, 1, k)
                        else:
                            f1_piece(dve, i + 1, 0, k)
                weigh(dve, i, 3)

            def weigh(dve, i, q):
                s, h = q // 2, q % 2
                dve.wait_ge(G["dn"].sem, G["dn"].at(0, i, 4 * q + 4))
                dve.wait_ge(G["cc"].sem, G["cc"].at(0, i, s + 1))
                dve.wait_ge(G["acc"].sem, G["acc"].at(0, i, max(0, q - 1)))
                b2 = sm[:, bass.ds(i * 2 + (s + SMALL["b2"][0]), 1)]
                nc.vector.scalar_tensor_tensor(out=g_t[h], in0=bank(3 + h), scalar=b2, in1=half(g_cw, h),
                                               op0=ALU.add, op1=ALU.mult).then_inc(G["t"].sem, 1)

            passes(dve, body)

        q_s = [sb(f"quant_{n}", [P, 1]) for n in ("max", "all", "scale", "inverse")]
        q_w = sb("quant_weights", [P, D])
        s_qm, s_qa, s_ql, s_qw = [sem("quant_" + n) for n in ("row_max", "all_max", "low_rank", "ready")]

        def quant_pool(pool):
            pool.wait_ge(s_qm, 1)
            nc.gpsimd.partition_all_reduce(q_s[1][:, :], q_s[0][:, :], P, bass.bass_isa.ReduceOp.max).then_inc(s_qa, 1)

        def quant_pe(pe):
            nc.tensor.matmul(ps[:, 4, 0:D], col("lora_a"), col("lora_b"), start=True, stop=True).then_inc(s_ql, 1)

        def quant_dve_max(dve):
            nc.vector.tensor_reduce(q_s[0][:, :], col("quant_w"), AX.X, ALU.max, apply_absolute_value=True).then_inc(s_qm, 1)

        def quant_dve(dve, order):
            dve.wait_ge(s_qa, 1)
            dve.wait_ge(s_ql, 1)
            scale, inv, w = q_s[2][:, :], q_s[3][:, :], q_w[:, :]
            order.step(nc.vector.tensor_scalar(scale, q_s[1][:, :], 1.0 / 7.0, None, ALU.mult))
            order.step(nc.vector.reciprocal(inv, scale))
            order.step(nc.vector.tensor_scalar(w, col("quant_w"), inv, None, ALU.mult))
            order.step(nc.vector.tensor_scalar(w, w, ROUND, None, ALU.add))
            order.step(nc.vector.tensor_scalar(w, w, -ROUND, 7.0, ALU.add, ALU.min))
            order.step(nc.vector.tensor_scalar(w, w, -8.0, scale, ALU.max, ALU.mult))
            nc.vector.tensor_tensor(w, w, ps[:, 4, 0:D], ALU.add).then_inc(s_qw, 1)

        K = signals("f3", E // 2, w=10, gu=16, sg=16, a=16, ah=16, al=16, dn=16, cb=2, cc=2, t=4, acc=4)
        s_kw = sem("f3_shared_weights")
        k_w = [(wr[:, 3072 * s:3072 * s + 1536], wr[:, 3072 * s + 1536:3072 * s + 3072]) for s in range(2)]
        k_a = [(wr[:, 6144 + 512 * k:6656 + 512 * k], wr[:, 7168 + 512 * k:7680 + 512 * k]) for k in range(2)]
        k_wt = wr[:, 8192:9216]
        k_sel = [wr[:, 9216 + 128 * k:9344 + 128 * k] for k in range(2)]
        k_sg = [wf[:, 512 * k:512 * (k + 1)] for k in range(2)]
        k_af = [wf[:, 1024 + 512 * k:1536 + 512 * k] for k in range(2)]
        k_cw = wf[:, 2048:3072]
        k_t = [wf[:, 3072 + 512 * k:3584 + 512 * k] for k in range(2)]
        FULL = [(s, h, f, NF) for s in range(2) for h in range(2) for f in range(NF)]
        SHARED = [(0, h, f, 2) for h in range(2) for f in range(2)]

        def f3_pe(pe, m):
            pe.wait_ge(s_xf, 2 * m + 2)
            logits_pe(xf, col("gate_w"), 5)
            pe.wait_ge(s_xs, 2 * splits(m) + 2)

            def up(i, n, shared=False):
                s, h, f, nf = (SHARED if shared else FULL)[n % 16]
                if h == 0 and f == 0:
                    if shared:
                        pe.wait_ge(s_kw, 2)
                    else:
                        pe.wait_ge(K["w"].sem, K["w"].at(0, i, 5 * (n // 8) + 5))
                pe.wait_ge(K["a"].sem, K["a"].at(0, i, max(0, n - 1)))
                for k in range(2):
                    c0 = (k * nf + f) * P
                    last = mm3(bank(2 * k + n % 2), [v[:, c0:c0 + P] for v in k_w[s]], (half(xh, h), half(xl, h)))
                last.then_inc(K["gu"].sem, 1)

            def body(i, last_pass, shared):
                steps = SHARED if shared else FULL

                def at(name, k):
                    pe.wait_ge(K[name].sem, K[name].at(0, i, k))

                def down(n):
                    s, h, f, nf = steps[n]
                    at("al", n + 1)
                    if f == 0:
                        at("t", 2 * (s - 1) + h + 1 if s else 0)
                    c0 = (2 * nf + f) * P
                    mm3(bank(4 + h), [v[:, c0:c0 + P] for v in k_w[s]], k_a[n % 2], start=f == 0, stop=f == nf - 1)\
                        .then_inc(K["dn"].sem, 1)

                for n in range(len(steps)):
                    if n + 2 < len(steps) or not shared:
                        up(i, n + 2, shared or (last_pass and n + 2 >= 16))
                    if n % 8 == 3 and not shared:
                        s = n // 8
                        at("cc", s)
                        for h in range(2):
                            last = nc.tensor.matmul(bank(6 + h), k_sel[s], half(k_wt, h), start=True, stop=True)
                        last.then_inc(K["cb"].sem, 1)
                    down(n)

            up(0, 0)
            up(0, 1)
            stack_pe(pe, 2)
            pe.wait_ge(s_wt, 3)
            with pe.Fori(0, PASSES - 1) as i:
                body(i, False, False)
            body(PASSES - 1, True, False)
            body(PASSES, True, True)
            pe.wait_ge(K["acc"].sem, K["acc"].at(0, PASSES, 2))
            back_pe(pe)

        def f3_act(act):
            softmax_act(act, 3)
            stack_act(act, 2, k_wt)

            def body(i, shared):
                steps = SHARED if shared else FULL

                def at(name, k):
                    act.wait_ge(K[name].sem, K[name].at(0, i, k))

                def high(n):
                    at("a", n + 1)
                    at("dn", max(0, n - 1))
                    nc.scalar.activation(k_a[n % 2][0], k_af[n % 2], ACT.Copy).then_inc(K["ah"].sem, 1)

                for n in range(len(steps)):
                    at("gu", n + 1)
                    at("a", max(0, n - 1))
                    nc.scalar.activation(k_sg[n % 2], bank(n % 2), ACT.Silu).then_inc(K["sg"].sem, 1)
                    if n >= 1:
                        high(n - 1)
                    if n % 8 == 5 and not shared:
                        s = n // 8
                        at("cb", s + 1)
                        at("t", 2 * s)
                        nc.scalar.activation(k_cw, bank(6, 2), ACT.Copy).then_inc(K["cc"].sem, 1)
                high(len(steps) - 1)

            with act.Fori(0, PASSES - 1) as i:
                body(i, False)
            body(PASSES - 1, False)
            body(PASSES, True)

        def f3_pool(pool):
            def body(i, count):
                for n in range(count):
                    h = n % 2
                    pool.wait_ge(K["t"].sem, K["t"].at(0, i, n + 1))
                    pool.wait_ge(K["acc"].sem, K["acc"].at(0, i, max(0, n - 1)))
                    nc.gpsimd.tensor_tensor(half(out_t, h), half(out_t, h), k_t[h], ALU.add).then_inc(K["acc"].sem, 1)

            with pool.Fori(0, PASSES) as i:
                body(i, 4)
            body(PASSES, 2)

        def f3_piece(dve, i, s, k):
            w = raw_b[:, bass.ds(i * (2 * W_F3) + s * W_F3, W_F3)]
            hi, lo = k_w[s]
            c = slice(768 * (k % 2), 768 * (k % 2 + 1))
            if k < 2:
                ins = nc.vector.tensor_copy(hi[:, c], w[:, c])
            elif k < 4:
                dve.wait_ge(K["w"].sem, K["w"].at(0, i, 5 * s + k - 1))
                ins = nc.vector.tensor_tensor(lo[:, c], w[:, c], hi[:, c].bitcast(F32), ALU.subtract)
            else:
                ins = nc.vector.tensor_copy(k_sel[s], sm[:, bass.ds(i * (2 * P) + (s * P + SMALL["sel_e"][0]), P)])
            ins.then_inc(K["w"].sem, 1)

        def f3_first(dve):
            dve.wait_ge(ld["f3"], 16)
            for k in range(5):
                f3_piece(dve, 0, 0, k)

        def f3_dve(dve, order):
            dve.wait_ge(s_lg, 4)
            order.step(nc.vector.tensor_copy(lg, ps[:, 5, 0:NT * E].rearrange("p (t e) -> p t e", t=NT)))
            softmax_dve(dve, order, 3)
            pick_max(order, oh, ex, t1, mcol)
            order.step(nc.vector.scalar_tensor_tensor(out=lg.rearrange("p t e -> p (t e)"), in0=oh.rearrange("p t e -> p (t e)"),
                                                      scalar=-2.0, in1=ex.rearrange("p t e -> p (t e)"),
                                                      op0=ALU.mult, op1=ALU.add))
            pick_max(order, oh2, lg, t1, mcol)
            order.step(nc.vector.tensor_tensor(oh, oh, oh2, ALU.add))
            order.step(nc.vector.tensor_tensor(ex, ex, oh, ALU.mult))
            dve.wait_ge(s_clear, 3)
            split_stack(order, ex, 0, True)

            def body(i, last_pass, shared):
                steps = SHARED if shared else FULL

                def at(name, k):
                    dve.wait_ge(K[name].sem, K[name].at(0, i, k))

                def low(n):
                    at("ah", n + 1)
                    at("dn", max(0, n - 1))
                    nc.vector.tensor_tensor(k_a[n % 2][1], k_af[n % 2], k_a[n % 2][0].bitcast(F32), ALU.subtract)\
                        .then_inc(K["al"].sem, 1)

                def weigh(q):
                    h = q % 2
                    at("dn", (2 if shared else 4) * (q + 1))
                    at("acc", max(0, q - 1))
                    if shared:
                        ins = nc.vector.tensor_copy(k_t[h], bank(4 + h))
                    else:
                        at("cc", q // 2 + 1)
                        ins = nc.vector.tensor_tensor(k_t[h], bank(4 + h), half(k_cw, h), ALU.mult)
                    ins.then_inc(K["t"].sem, 1)

                for n in range(len(steps)):
                    at("sg", n + 1)
                    at("al", max(0, n - 1))
                    at("ah", max(0, n - 1))
                    nc.vector.tensor_tensor(k_af[n % 2], k_sg[n % 2], bank(2 + n % 2), ALU.mult).then_inc(K["a"].sem, 1)
                    if n >= 1:
                        low(n - 1)
                    if not shared:
                        s = n // 8
                        if n % 4 == 2 and n > 2:
                            weigh((n - 6) // 4)
                        if 2 <= n % 8 <= 6:
                            k = n % 8 - 2
                            if k == 0:
                                at("dn", 8 * s)
                                at("cb", s)
                            if s == 0:
                                f3_piece(dve, i, 1, k)
                            elif not last_pass:
                                f3_piece(dve, i + 1, 0, k)
                            elif k < 2:
                                w = raw_b[:, E * W_F3:E * W_F3 + W_SH]
                                hi, lo = k_w[0][0][:, 0:W_SH], k_w[0][1][:, 0:W_SH]
                                if k == 0:
                                    ins = nc.vector.tensor_copy(hi, w)
                                else:
                                    dve.wait_ge(s_kw, 1)
                                    ins = nc.vector.tensor_tensor(lo, w, hi.bitcast(F32), ALU.subtract)
                                ins.then_inc(s_kw, 1)
                    elif n == 3:
                        weigh(0)
                low(len(steps) - 1)
                weigh(1 if shared else 3)

            with dve.Fori(0, PASSES - 1) as i:
                body(i, False, False)
            body(PASSES - 1, True, False)
            body(PASSES, True, True)

        def split_ctx(dve, order):
            dve.wait_ge(ld["ctx_t"], 16)
            order.step(nc.vector.tensor_copy(ch[:, :], out_t[:, :]))
            nc.vector.tensor_tensor(cl[:, :], out_t[:, :], ch[:, :].bitcast(F32), ALU.subtract).then_inc(s_ctx, 1)

        def mask_cap(dve, order):
            dve.wait_ge(ld["mask"], 16)
            order.step(nc.vector.tensor_scalar(w_floor, col("nbias"), -8.0, None, ALU.mult))
            flat_cap = raw_b[:, CAP:CAP + 2 * T]
            order.step(nc.vector.tensor_scalar(flat_cap, mask_u8[:, :], -BIG, BIG, ALU.mult, ALU.add))
            order.step(nc.vector.tensor_scalar(flat_cap, flat_cap, w_floor, None, ALU.add))

        block = stack.enter_context(nc.Block())

        @block.sync
        def _(sp):
            def load(dst, src, name):
                sp.dma_start(dst, src).then_inc(ld[name], 16)

            load(res[:, :, :], x, "x")
            load(sm[:, :], small, "small")
            load(out_t[:, :], ctx_t, "ctx_t")
            load(raw_a[:, RA0:RA0 + NG * W_A], wa0, "a0")
            load(raw_a[:, RF0:RF0 + 2 * NKT * W_F0], wf0, "f0")
            load(mask_u8[:, :], mask, "mask")
            load(raw_b[:, RB1:RB1 + NQ * W_B], wb1, "b1")
            load(ctok[:, :, :], ctx_tok, "ctx_tok")
            load(raw_b[:, RA2:RA2 + NG * W_A], wa2, "a2")
            sp.wait_ge(A["w"].sem, A["w"].at(0, NG, 0))
            sp.wait_ge(F["w"].sem, F["w"].at(0, NKT, 0))
            load(raw_a[:, :], wf1, "f1")
            sp.wait_ge(G["w"].sem, G["w"].at(0, PASSES, 0))
            load(raw_a[:, RB3:RB3 + NQ * W_B], wb3, "b3")
            sp.wait_ge(W["acc"].sem, W["acc"].at(0, NQ, 0))
            sp.wait_ge(A["w"].sem, A["w"].at(1, NG, 0))
            load(raw_b[:, :], wf3, "f3")
            sp.wait_ge(s_res, 2)
            sp.dma_start(out, res[:, :, :]).then_inc(s_out, 16)
            sp.wait_ge(s_out, 16)

        @block.gpsimd
        def _(pool):
            nc.gpsimd.memset(mhalf[:, :], -0.5).then_inc(s_init, 1)
            pool.wait_ge(s_init, 1)
            norm_pool(pool, 0)
            small_pool(pool, 0)
            quant_pool(pool)
            norm_pool(pool, 1)
            clear_pool(pool, 0, 3, (f_ones, 1.0), (f_wt.bitcast(F32), 0.0), (stk, 0.0))
            norm_pool(pool, 2)
            wide_pool_init(pool, 0, 2)
            wide_pool(pool, 0)
            norm_pool(pool, 3)
            clear_pool(pool, 1, 5, (g_wt.bitcast(F32), 0.0), (stk, 0.0))
            f1_pool(pool)
            small_pool(pool, 1)
            norm_pool(pool, 4)
            norm_pool(pool, 5)
            norm_pool(pool, 6)
            norm_pool(pool, 7)
            norm_pool(pool, 8)
            wide_pool_init(pool, 1, 8)
            wide_pool(pool, 1)
            norm_pool(pool, 9)
            clear_pool(pool, 2, 6, (k_wt.bitcast(F32), 0.0))
            f3_pool(pool)

        @block.scalar
        def _(act):
            act.wait_ge(ld["small"], 16)
            nc.scalar.activation(gate[:, :], col("gates"), ACT.Tanh).then_inc(s_gate, 1)
            norm_act(act, 0, f32=False, high=xh)
            act.wait_ge(s_vp, 1)
            nc.scalar.activation(a_vall, bank(0, 2), ACT.Copy).then_inc(s_va, 1)
            small_act(act, 0)
            small_out_act(act)
            norm_act(act, 1, high=xh)
            f0_act(act)
            norm_act(act, 2, f32=False, high=xh)
            wide_act(act, 0, ACT.Square, col("nbias"))
            norm_act(act, 3, high=xh)
            f1_act(act)
            norm_act(act, 4, f32=False, high=xh)
            small_act(act, 1)
            norm_act(act, 5, w=col("ln_c_w"), b=col("ln_c_b"))
            norm_act(act, 6)
            norm_act(act, 7, w=col("ln_l_w"), b=col("ln_l_b"))
            wide_act(act, 1, ACT.Exp, 0.0)
            norm_act(act, 8, high=xh)
            f3_act(act)

        @block.vector
        def _(dve):
            order = Order(dve, s_dve)
            dve.wait_ge(ld["small"], 16)
            quant_dve_max(dve)
            dve.wait_ge(ld["x"], 16)
            norm_dve_tokens(dve, order, 0, res, xn, lambda: small_weights(dve, 0, 0, raw_a, RA0, ld["a0"]))
            norm_dve_split(dve, order, 0, xh, xl)
            split_ctx(dve, order)
            dve.wait_ge(s_gate, 1)
            small_dve(dve, order, 0, raw_a, RA0, lambda: (f0_weights(dve, order), mask_cap(dve, order)))
            quant_dve(dve, order)
            back_dve(dve, order, 0, 0)
            norm_dve_tokens(dve, order, 1, res, xn)
            norm_dve_split(dve, order, 1, xh, xl)
            f0_dve(dve, order)
            back_dve(dve, order, 1, 1)
            norm_dve_tokens(dve, order, 2, res, xn, lambda: wide_weights(dve, 0, 0, raw_b, RB1, ld["b1"]))
            norm_dve_split(dve, order, 2, xh, xl)
            order.step(nc.vector.memset(xn[:, :, :], 0.0))
            wide_dve(dve, order, 0, raw_b, RB1)
            dve.wait_ge(W["acc"].sem, W["acc"].at(0, NQ, 0))
            tokens_in(dve, order, 2, xn)
            norm_dve_tokens(dve, order, 3, res, xn, lambda: f1_first(dve))
            norm_dve_split(dve, order, 3, xh, xl)
            f1_shifts_dve(dve, order)
            f1_dve(dve, order)
            tokens_in(dve, order, 3, xn)
            back_dve(dve, order, 2, 3)
            norm_dve_tokens(dve, order, 4, res, xn, lambda: small_weights(dve, 1, 0, raw_b, RA2, ld["a2"]))
            norm_dve_split(dve, order, 4, xh, xl)
            small_dve(dve, order, 1, raw_b, RA2, lambda: norm_dve_tokens(dve, order, 5, ctok, ctok))
            dve.wait_ge(A["att"].sem, A["att"].at(1, NG, 0))
            tokens_in(dve, order, 4, a_att)
            norm_dve_tokens(dve, order, 6, res, xn, lambda: norm_dve_split(dve, order, 5, ch, cl, False))
            for h in range(2):
                dve.wait_ge(s_rt, 2 * 3 + h + 1)
                r = xn[:, 4 * h:4 * h + 4, :]
                order.done(nc.vector.tensor_tensor(r, bank(6 + h).rearrange("p (t d) -> p t d", t=4),
                                                   col("quant_bias").unsqueeze(1).to_broadcast((P, 4, D)), ALU.add))
            order.wait()
            tokens_in(dve, order, 5, xn)
            norm_dve_tokens(dve, order, 7, res, xn, lambda: wide_weights(dve, 1, 0, raw_a, RB3, ld["b3"]))
            norm_dve_tokens(dve, order, 8, xn, xn)
            norm_dve_split(dve, order, 7, xh, xl, False)
            order.step(nc.vector.tensor_copy(xn[:, :, :], col("bo").unsqueeze(1).to_broadcast((P, NT, D))))
            wide_dve(dve, order, 1, raw_a, RB3)
            dve.wait_ge(W["acc"].sem, W["acc"].at(1, NQ, 0))
            tokens_in(dve, order, 6, xn)
            norm_dve_tokens(dve, order, 9, res, xn, lambda: f3_first(dve))
            norm_dve_split(dve, order, 8, xh, xl)
            f3_dve(dve, order)
            back_dve(dve, order, 4, 7, s_res)

        @block.tensor
        def _(pe):
            pe.wait_ge(ld["small"], 16)
            norm_pe(pe, 0, 0)
            pe.wait_ge(ld["ctx_t"], 16)
            for t in range(NT):
                last = nc.tensor.matmul(ps[:, t // 4, (t % 4) * P:(t % 4 + 1) * P], out_t[:, t * P:(t + 1) * P],
                                        col("wv0"), start=True, stop=True)
            last.then_inc(s_vp, 1)
            pe.wait_ge(s_va, 1)
            pe.wait_ge(s_ctx, 1)
            small_pe(pe, 0, 0)
            quant_pe(pe)
            small_out_pe(pe)
            norm_pe(pe, 1, 1)
            f0_pe(pe, 1)
            norm_pe(pe, 2, 2)
            wide_pe(pe, 0, 2, raw_b, RB1)
            f1_shifts_pe(pe)
            norm_pe(pe, 3, 3)
            f1_pe(pe, 3)
            norm_pe(pe, 4, 4)
            small_pe(pe, 1, 4)
            norm_pe(pe, 5, 5, ctok)
            norm_pe(pe, 6, 6)
            pe.wait_ge(s_xf, 2 * 6 + 2)
            pe.wait_ge(s_qw, 1)
            tokens_pe(xf, q_w[:, :])
            norm_pe(pe, 8, 7)
            wide_pe(pe, 1, 7, raw_a, RB3)
            norm_pe(pe, 9, 8)
            f3_pe(pe, 8)

def tokens_first(a):
    return np.ascontiguousarray(a.reshape(NT, P, D).transpose(1, 0, 2))


def small_heads(wq, wk):
    a = np.zeros((P, NG, W_A), np.float32)
    for g in range(NG):
        for j in range(GH):
            r = (g * GH + j) * DH8
            for rep in range(3):
                at = BLK * j + DH8 * rep
                a[:, g, at:at + DH8] = wq[r:r + DH8, :].T
                a[:, g, P + at:P + at + DH8] = wk[r:r + DH8, :].T
    return a.reshape(P, NG * W_A)


def kernel(**inputs):
    import concourse.bacc as _bacc
    from concourse.bass_utils import run_bass_kernel_spmd as _run
    arrays = layout({k: np.asarray(v) for k, v in inputs.items()})
    nc = _bacc.Bacc("TRN2", target_bir_lowering=False, num_devices=1)
    aps = {n: nc.dram_tensor("in_" + n, a.shape, mybir.dt.from_np(a.dtype), kind="ExternalInput").ap()
           for n, a in arrays.items()}
    out = nc.dram_tensor("out_tokens", (P, NT, D), F32, kind="ExternalOutput").ap()
    build(nc, out=out, **aps)
    r = _run(nc, [{"in_" + n: a for n, a in arrays.items()}], core_ids=[0])
    got = np.asarray(r.results[0]["out_tokens"])
    return np.ascontiguousarray(got.transpose(1, 0, 2)).reshape(B, S, D)


def layout(v):
    f = np.float32
    sm = np.zeros((P, N_SMALL), f)

    def put(name, a, rows=slice(None)):
        at, width = SMALL[name]
        sm[rows, at:at + width] = a

    r = np.arange(P)
    put("ident", np.eye(P, dtype=f))
    c = np.arange(2 * P)
    put("spread", (r[:, None] == BLK * (2 * (c[None, :] % P // DH) + c[None, :] // P)).astype(f))
    put("lo_q", -((r % BLK) // DH8 == 2).astype(f)[:, None])
    put("lo_k", -((r % BLK) // DH8 == 1).astype(f)[:, None])
    put("one_rows", ((r % BLK == 24) | (r % BLK == 25)).astype(f)[:, None])
    put("head", (r[:, None] // BLK == np.arange(GH)[None, :]).astype(f))
    put("inv_n", np.stack([f(1) / (r + 1).astype(f), f(1) / (P + r + 1).astype(f)], 1))
    put("iota", np.arange(E, dtype=f)[None, :])
    put("gates", np.stack([v["g_xattn"], v["g_ffn"]], 1).reshape(1, 8))
    put("nbias", v["L1_xattn_nbias"].reshape(1, 1))
    put("alpha", v["L0_ffn_alpha_bi"].reshape(1, 1))
    put("rb2", v["L0_ffn_router_b2"][None, :])
    put("ebias", v["L0_ffn_expert_bias"][None, :])
    put("rb1", v["L0_ffn_router_b1"][:, None])
    put("gamma", v["L1_ffn_gamma"].T)
    put("beta", v["L1_ffn_beta"].T)
    put("b1", v["L1_ffn_b1"].reshape(E, NF, P).transpose(2, 0, 1).reshape(P, E * NF))
    put("b2", v["L1_ffn_b2"].T)
    put("quant_bias", v["L2_ffn_bias"][None, :])
    put("bo", v["L3_xattn_bo"][None, :])
    for n in ("ln_l_w", "ln_l_b", "ln_c_w", "ln_c_b"):
        put(n, v["L3_xattn_" + n][:, None])
    put("centroids", v["L1_ffn_centroids"].T)
    put("gate_w", v["L3_ffn_gate_w"].T)
    put("router_w2", v["L0_ffn_router_w2"].T)
    for k, n in enumerate(("b_fwd", "b_fwd", "b_inv", "b_inv")):
        put("b_experts", v["L0_ffn_" + n], slice(E * k, E * (k + 1)))
    for n in ("W_Q", "W_K", "W_inv", "W_O", "router_w1"):
        put(n, v["L0_ffn_" + n].T)
    put("wv0", v["L0_xattn_Wv"].T)
    put("wo0", v["L0_xattn_Wo"].T)
    put("quant_w", v["L2_ffn_kernel"])
    put("lora_a", v["L2_ffn_a"].T, slice(0, 16))
    put("lora_b", v["L2_ffn_b"], slice(0, 16))
    e = np.arange(E)
    sel_e = ((r[:, None] % E == e[None, :]) & (r[:, None] < 2 * E)).astype(f)
    put("sel_e", np.repeat(sel_e, P, axis=1))

    wf0 = np.zeros((P, NKT, 2, W_F0), f)
    for br, (nv, nw, nu) in enumerate((("V_fwd", "W_fwd", "U_fwd"), ("W_inv_exp", "V_inv", "U_inv"))):
        for k in range(NKT):
            two = slice(2 * k, 2 * k + 2)
            wf0[:, k, br, 0:P] = v["L0_ffn_" + nv][two].transpose(1, 0, 2).reshape(D, P)
            wf0[:, k, br, P:2 * P] = v["L0_ffn_" + nw][two].transpose(1, 0, 2).reshape(D, P)
            wf0[:, k, br, 2 * P:3 * P] = v["L0_ffn_" + nu][two].transpose(0, 2, 1).reshape(P, D)
            expert = 2 * k + r[None, :] // 64
            wf0[:, k, br, 3 * P:] = ((r[:, None] // (2 * E) == br) & (r[:, None] % E == expert)).astype(f)

    def wide(wq_t, wk_t, wv_t, wo):
        a = np.zeros((P, NQ, W_B), f)
        for q in range(NQ):
            s = slice(q * QW, (q + 1) * QW)
            a[:, q, 0:QW], a[:, q, QW:2 * QW], a[:, q, 2 * QW:3 * QW] = wq_t[:, s], wk_t[:, s], wv_t[:, s]
            a[:, q, 3 * QW:] = wo[s, :].reshape(2, P, D).transpose(1, 0, 2).reshape(P, 2 * D)
        return a.reshape(P, NQ * W_B)

    w = NQ * QW
    kv1, kv3 = v["L1_xattn_Wkv"], v["L3_xattn_Wkv"]
    wf1 = np.zeros((P, E, W_F1), f)
    wf1[:, :, :512] = v["L1_ffn_W1"].transpose(2, 0, 1)
    wf1[:, :, 512:] = v["L1_ffn_W2"].reshape(E, D, NF, P).transpose(3, 0, 2, 1).reshape(P, E, NF * D)
    wf3 = np.zeros((P, E * W_F3 + W_SH), f)
    a = wf3[:, :E * W_F3].reshape(P, E, W_F3)
    a[:, :, 0:512] = v["L3_ffn_gate_k"].transpose(1, 0, 2)
    a[:, :, 512:1024] = v["L3_ffn_up_k"].transpose(1, 0, 2)
    a[:, :, 1024:] = v["L3_ffn_down_k"].reshape(E, NF, P, D).transpose(2, 0, 1, 3).reshape(P, E, NF * D)
    wf3[:, :E * W_F3] = a.reshape(P, E * W_F3)
    sh = wf3[:, E * W_F3:]
    sh[:, 0:256], sh[:, 256:512] = v["L3_ffn_sh_gate"], v["L3_ffn_sh_up"]
    sh[:, 512:] = v["L3_ffn_sh_down"].reshape(2, P, D).transpose(1, 0, 2).reshape(P, 2 * D)
    eye = np.eye(D, dtype=f)
    c = v["ctx_1024"]
    arrays = dict(
        x=tokens_first(v["x"]), ctx_tok=tokens_first(c), ctx_t=np.ascontiguousarray(c.reshape(T, D).T),
        mask=np.ascontiguousarray(v["mask_BxSxS2_bk0"].reshape(B, S, 2, P).transpose(3, 0, 2, 1)).reshape(P, 2 * T),
        small=sm,
        wa0=small_heads(v["L0_xattn_Wq"], v["L0_xattn_Wk"]),
        wa2=small_heads(eye, eye),
        wf0=wf0.reshape(P, 2 * NKT * W_F0),
        wb1=wide(v["L1_xattn_Wq"].T, kv1[:w].T, kv1[w:].T, v["L1_xattn_Wo"].T),
        wf1=wf1.reshape(P, E * W_F1),
        wb3=wide(v["L3_xattn_Wq"], kv3[:, :w], kv3[:, w:], v["L3_xattn_Wo"]),
        wf3=wf3,
    )
    return arrays
```

```python
from contextlib import ExitStack

import numpy as np

import concourse.bass as bass
from concourse import mybir

F32 = mybir.dt.float32
F32R = mybir.dt.float32r
U8 = mybir.dt.uint8
ALU = mybir.AluOpType
ACT = mybir.ActivationFunctionType
AX = mybir.AxisListType

P = 128
B, S, D = 4, 256, 128
T = B * S
NT = T // P
H = 16
HALF = 512
E = 8
BLK = 32
GH = P // BLK
NG = H // GH
DH8 = D // H
DH = 64
NQ = 4
QW = 4 * DH
NKT = 4
BIG = 3.0e38
EPS = 1e-5
IEPS = 1e-32
CLIP = 11.0
ROUND = 12582912.0

SMALL = {}
N_SMALL = 0
for _name, _width in (
    ("ident", P), ("spread", 2 * P), ("lo_q", 1), ("lo_k", 1), ("one_rows", 1), ("head", GH),
    ("inv_n", 2), ("iota", E), ("gates", 8), ("nbias", 1), ("alpha", 1), ("rb2", E), ("ebias", E),
    ("rb1", 1), ("gamma", E), ("beta", E), ("b1", 4 * E), ("b2", E), ("quant_bias", P),
    ("ln_l_w", 1), ("ln_l_b", 1), ("ln_c_w", 1), ("ln_c_b", 1), ("bo", P),
    ("centroids", E), ("gate_w", E), ("router_w2", E), ("b_experts", P),
    ("W_Q", P), ("W_K", P), ("W_inv", P), ("router_w1", P), ("W_O", P), ("wv0", P), ("wo0", P),
    ("quant_w", P), ("lora_a", P), ("lora_b", P), ("sel_e", E * P),
):
    SMALL[_name] = (N_SMALL, _width)
    N_SMALL += _width
W_A = 2 * P
W_F0 = 4 * P
W_B = 4 * QW
W_F1 = 1024
W_F3 = 1536
W_SH = 768
NF = 4


class Order:

    def __init__(self, eng, sem):
        self.eng, self.sem = eng, sem
        self.base, self.i, self.per, self.local = 0, None, 0, 0

    def loop(self, i, per):
        self.i, self.per, self.local = i, per, 0

    def end(self, passes):
        assert self.local == self.per, (self.local, self.per)
        self.base += passes * self.per
        self.i, self.per, self.local = None, 0, 0

    def done(self, ins):
        ins.then_inc(self.sem, 1)
        if self.i is None:
            self.base += 1
        else:
            self.local += 1
        return ins

    def wait(self):
        self.eng.wait_ge(self.sem, self.base if self.i is None else self.i * self.per + (self.base + self.local))

    def step(self, ins):
        self.done(ins)
        self.wait()


START = 4


class Signal:

    def __init__(self, sem, per, passes):
        self.sem, self.per, self.passes = sem, per, passes

    def at(self, call, i, k):
        return i * self.per + (call * self.per * self.passes + k + START)


def build(nc, x, ctx_tok, ctx_t, mask, small, wa0, wf0, wb1, wf1, wa2, wb3, wf3, out):
    stack = ExitStack()
    with stack:
        def sb(name, shape, dt=F32):
            return stack.enter_context(nc.sbuf_tensor(name, shape, dt))

        def sem(name):
            return stack.enter_context(nc.semaphore(name))

        sm = sb("small_operands", [P, N_SMALL])
        res = sb("residual", [P, NT, D])
        xn = sb("normed_tokens", [P, NT, D])
        xf = sb("normed_t", [P, T])
        xh = sb("normed_t_high", [P, T], F32R)
        xl = sb("normed_t_low", [P, T], F32R)
        out_t = sb("sublayer_out_t", [P, T])
        ctok = sb("context_tokens", [P, NT, D])
        ch = sb("context_t_high", [P, T], F32R)
        cl = sb("context_t_low", [P, T], F32R)
        gate = sb("tanh_gates", [P, 8])
        mask_u8 = sb("mask_bytes", [P, 2 * T], U8)
        w_floor_t = sb("score_floor", [P, 1])
        w_floor = w_floor_t[:, :]
        stats = sb("ln_stats", [P, NT, 6])
        mv = sb("ln_mean_var", [P, NT, 2])
        ve = sb("ln_var_eps", [P, NT])
        mhalf = sb("minus_half", [P, NT])
        rs = sb("ln_rstd", [P, NT])
        rt = sb("ln_newton", [P, NT])
        raw_a = sb("raw_a", [P, E * W_F1])
        raw_b = sb("raw_b", [P, E * W_F3 + W_SH])
        RA0, RF0 = 0, NG * W_A
        RB3 = 0
        RB1, RA2, CAP = 0, NQ * W_B, NQ * W_B + NG * W_A
        cap = raw_b[:, CAP:CAP + B * 2 * S].rearrange("p (b k q) -> p b k q", b=B, k=2)
        NWF, NWR = 8192, 9472
        wf = sb("work", [P, NWF])
        wr = sb("work_split", [P, NWR], F32R)

        def col(name, a=0, n=None):
            at, width = SMALL[name]
            return sm[:, at + a:at + (width if n is None else a + n)]

        ident = col("ident")
        ps = stack.enter_context(nc.psum_tensor("banks", [P, 8, HALF], F32))

        def bank(i, n=1):
            return ps[:, i, :] if n == 1 else ps[:, i:i + n, :].rearrange("p a b -> p (a b)")

        def half(t, h):
            return t[:, h * HALF:(h + 1) * HALF]

        def mm3(o, w, m, start=True, stop=True):
            nc.tensor.matmul(o, w[0], m[0], start=start, stop=False)
            nc.tensor.matmul(o, w[0], m[1], start=False, stop=False)
            return nc.tensor.matmul(o, w[1], m[0], start=False, stop=stop)

        ld = {n: sem("loaded_" + n) for n in ("x", "ctx_t", "ctx_tok", "small", "mask", "a0", "f0", "b1", "f1", "a2", "b3", "f3")}
        s_dve = sem("vector_own_steps")
        s_act = sem("scalar_own_steps")
        s_init = sem("constants_ready")
        s_gate = sem("gates_ready")
        s_ctx = sem("context_split")
        s_ve = sem("ln_variance_ready")
        s_pow = sem("ln_power_ready")
        s_xn = sem("ln_tile_ready")
        s_xt = sem("ln_half_transposed")
        s_xf = sem("ln_half_copied")
        s_xs = sem("ln_half_split")
        s_rt = sem("out_half_back")
        s_vp = sem("values_tile_product")
        s_va = sem("values_ready")
        s_out = sem("stored")
        s_pcl, s_clear = sem("parts_cleared"), sem("feed_forward_cleared")
        s_res = sem("residual_done")
        s_ot, s_oc = sem("heads_transposed"), sem("heads_copied")

        def signals(prefix, passes, **per):
            return {k: Signal(sem(f"{prefix}_{k}"), n, passes) for k, n in per.items()}

        def splits(m):
            return m - (m > 6)

        def norm_dve_tokens(dve, order, n, src, dst, meanwhile=None):
            if src is xn:
                dve.wait_ge(s_xn, NT * n)
            for t in range(NT):
                order.done(nc.vector.bn_stats(stats[:, t, :], src[:, t, :]))
            order.wait()
            for t in range(NT):
                order.done(nc.vector.bn_aggr(mv[:, t, :], stats[:, t, :]))
            order.wait()
            nc.vector.tensor_scalar(ve[:, :], mv[:, :, 1], EPS, None, ALU.add).then_inc(s_ve, 1)
            dve.wait_ge(s_ve, n + 1)
            if meanwhile is not None:
                meanwhile()
            dve.wait_ge(s_pow, n + 1)
            order.step(nc.vector.tensor_tensor(rt[:, :], rs[:, :], rs[:, :], ALU.mult))
            order.step(nc.vector.scalar_tensor_tensor(out=rt[:, :], in0=rt[:, :], scalar=-0.5, in1=ve[:, :],
                                                      op0=ALU.mult, op1=ALU.mult))
            order.step(nc.vector.scalar_tensor_tensor(out=rs[:, :], in0=rt[:, :], scalar=1.5, in1=rs[:, :],
                                                      op0=ALU.add, op1=ALU.mult))
            for t in range(NT):
                nc.vector.tensor_scalar(dst[:, t, :], src[:, t, :], mv[:, t, 0:1], rs[:, t:t + 1],
                                        ALU.subtract, ALU.mult).then_inc(s_xn, 1)

        def norm_pool(pool, n):
            pool.wait_ge(s_ve, n + 1)
            nc.gpsimd.tensor_tensor(rs[:, :], ve[:, :], mhalf[:, :], ALU.pow).then_inc(s_pow, 1)

        def norm_pe(pe, n, m, src=xn):
            for h in range(2):
                for t in range(4 * h, 4 * h + 4):
                    pe.wait_ge(s_xn, NT * n + t + 1)
                    last = nc.tensor.transpose(ps[:, 6 + h, (t % 4) * P:(t % 4 + 1) * P], src[:, t, :], ident)
                last.then_inc(s_xt, 1)

        def norm_act(act, m, f32=True, high=None, w=None, b=None):
            for h in range(2):
                act.wait_ge(s_xt, 2 * m + h + 1)
                act.wait_ge(s_xs, 2 * splits(m))
                if f32 and w is None:
                    ins = nc.scalar.activation(half(xf, h), bank(6 + h), ACT.Copy)
                elif f32:
                    ins = nc.scalar.activation(half(xf, h), bank(6 + h), ACT.Identity, bias=b, scale=w)
                if high is not None:
                    ins = nc.scalar.activation(half(high, h), bank(6 + h), ACT.Copy)
                ins.then_inc(s_xf, 1)

        def norm_dve_split(dve, order, m, hi, lo, from_bank=True):
            for h in range(2):
                dve.wait_ge(s_xf, 2 * m + h + 1)
                src = bank(6 + h) if from_bank else half(xf, h)
                if not from_bank:
                    order.step(nc.vector.tensor_copy(half(hi, h), src))
                nc.vector.tensor_tensor(half(lo, h), src, half(hi, h).bitcast(F32), ALU.subtract).then_inc(s_xs, 1)

        def back_pe(pe):
            for h in range(2):
                for t in range(4):
                    last = nc.tensor.transpose(ps[:, 6 + h, t * P:(t + 1) * P],
                                               out_t[:, (4 * h + t) * P:(4 * h + t + 1) * P], ident)
                last.then_inc(s_rt, 1)

        def tokens_pe(src, w):
            for h in range(2):
                for t in range(4):
                    last = nc.tensor.matmul(ps[:, 6 + h, t * P:(t + 1) * P],
                                            src[:, (4 * h + t) * P:(4 * h + t + 1) * P], w, start=True, stop=True)
                last.then_inc(s_rt, 1)

        def back_dve(dve, order, r, n, signal=None):
            for h in range(2):
                dve.wait_ge(s_rt, 2 * r + h + 1)
                t = res[:, 4 * h:4 * h + 4, :].rearrange("p t d -> p (t d)")
                ins = nc.vector.scalar_tensor_tensor(out=t, in0=bank(6 + h), scalar=gate[:, n:n + 1], in1=t,
                                                     op0=ALU.mult, op1=ALU.add)
                if signal is None:
                    order.done(ins)
                else:
                    ins.then_inc(signal, 1)
            if signal is None:
                order.wait()

        A = signals("a", NG, w=2, q=4, hi=4, y=4, km=8, v=2, mx=16, red=16, m2=2, mt=2, yf=2, s=8, p=8, pv=8,
                    raw=2, rt=2, att=2)
        s_acl = sem("a_tile_cleared")
        s_ainit = sem("a_cleared")
        a_y, a_yf, a_ky = wr[:, 0:1024], wr[:, 1024:2048], wr[:, 2048:3072]
        a_km = [wr[:, 3072 + 1024 * j:4096 + 1024 * j] for j in range(GH)]
        a_hi = wr[:, 7168:8192]
        a_wh, a_wl = wr[:, 8192:8448], wr[:, 8448:8704]
        a_vall = wf[:, 0:1024]
        a_vg = wf[:, 1024:2048].rearrange("p (t j c) -> p t j c", t=NT, j=GH)
        a_p = [wf[:, 2048 + 1024 * k:3072 + 1024 * k] for k in range(2)]
        a_m2 = wf[:, 4096:5120].rearrange("p (t j c) -> p t j c", t=NT, j=GH)
        a_raw = wf[:, 5120:6144]
        a_nm = wf[:, 6144:6176].rearrange("p (t j) -> p t j", t=NT)
        a_rec = wf[:, 6176:6208].rearrange("p (t j) -> p t j", t=NT)
        a_att = wf[:, 7168:8192].rearrange("p (t d) -> p t d", t=NT)
        a_att_t = wf[:, 1024:2048]

        def small_passes(eng, slot):
            with eng.Fori(0, NG - 2) as i:
                slot(i, 0, True, True, True)
                slot(i, 1, True, True, True)
            slot(NG - 2, 0, True, True, True)
            slot(NG - 2, 1, False, True, True)
            slot(NG - 1, 0, False, False, True)
            slot(NG - 1, 1, False, False, False)

        def small_pe(pe, c, m):
            def at(i, name, k):
                pe.wait_ge(A[name].sem, A[name].at(c, i, k))

            def project(i, x, k):
                h = x % 2
                at(i, "w", 2 * (x // 2) + 2)
                if k:
                    at(i, "y", 2 * x + 1)
                src = (half(ch, h), half(cl, h)) if k else (half(xh, h), half(xl, h))
                mm3(bank(5), (a_wh[:, k * P:(k + 1) * P], a_wl[:, k * P:(k + 1) * P]), src).then_inc(A["q"].sem, 1)

            def maxima(i, x, n):
                t, j0 = 4 * (x % 2) + n // 2, 2 * (n % 2)
                if n == 0:
                    at(i, "km", 4 * x + 4)
                if n >= 2:
                    at(i, "red", 8 * x + n - 1)
                for j in range(j0, j0 + 2):
                    last = nc.tensor.matmul(ps[:, 6 + n % 2, (j % 2) * S:(j % 2 + 1) * S],
                                            a_y[:, t * P:(t + 1) * P], a_km[j][:, (t // 2) * S:(t // 2 + 1) * S],
                                            start=True, stop=True)
                last.then_inc(A["mx"].sem, 1)

            def maxima_back(i, x):
                at(i, "m2", x + 1)
                for t in range(4):
                    last = nc.tensor.transpose(ps[:, 6, t * P:(t + 1) * P],
                                               a_m2[:, 4 * (x % 2) + t, :, :].rearrange("p j c -> p (j c)"), ident)
                last.then_inc(A["mt"].sem, 1)

            def scores(x, u):
                b, kb = 2 * (x % 2) + u // 2, u % 2
                for j in range(GH):
                    last = nc.tensor.matmul(ps[:, 2 * (u % 2) + j // 2, (j % 2) * S:(j % 2 + 1) * S],
                                            a_km[j][:, b * S + kb * P:b * S + (kb + 1) * P],
                                            a_yf[:, b * S:(b + 1) * S], start=True, stop=True)
                last.then_inc(A["s"].sem, 1)

            def values(i, x, u):
                if u == 0:
                    at(i, "v", x + 1)
                at(i, "p", 4 * x + u + 1)
                for j in range(GH):
                    last = nc.tensor.matmul(ps[BLK * j:BLK * (j + 1), 4, (u // 2) * S:(u // 2 + 1) * S],
                                            a_vg[:, 4 * (x % 2) + u, j, :], a_p[u % 2][:, j * S:(j + 1) * S],
                                            start=u % 2 == 0, stop=u % 2 == 1)
                last.then_inc(A["pv"].sem, 1)

            def sums_back(i, x):
                at(i, "raw", x + 1)
                for t in range(4 * (x % 2), 4 * (x % 2) + 4):
                    last = nc.tensor.transpose(ps[:, 5, (t % 4) * P:(t % 4 + 1) * P],
                                               a_raw[:, t * P:(t + 1) * P], ident)
                last.then_inc(A["rt"].sem, 1)

            def slot(i, x, asking, projecting, maxing):
                def more(*tiles):
                    for n in tiles if maxing else ():
                        maxima(i, x + 1, n)

                at(i, "yf", x + 1)
                scores(x, 0)
                more(0, 1)
                scores(x, 1)
                more(2)
                more(3)
                values(i, x, 0)
                scores(x, 2)
                if projecting:
                    project(i, x + 2, 1)
                more(4)
                values(i, x, 1)
                more(5)
                scores(x, 3)
                more(6)
                values(i, x, 2)
                more(7)
                values(i, x, 3)
                if projecting:
                    at(i, "y", 2 * (x + 2) + 2)
                sums_back(i, x)
                if maxing:
                    maxima_back(i, x + 1)
                if asking:
                    at(i, "att", x + 1)
                    project(i, x + 3, 0)

            for x in range(2):
                pe.wait_ge(s_xs, 2 * splits(m) + x + 1)
                if x:
                    at(0, "y", 2)
                project(0, x, 0)
                project(0, x, 1)
            for n in range(8):
                maxima(0, 0, n)
            maxima_back(0, 0)
            at(0, "y", 4)
            project(0, 2, 0)
            small_passes(pe, slot)

        def small_act(act, c):
            if c == 0:
                act.wait_ge(s_va, 1)
            else:
                act.wait_ge(ld["ctx_tok"], 16)
            vsrc = a_vall if c == 0 else ctok[:, :, :].rearrange("p t d -> p (t d)")
            vsrc = vsrc.rearrange("p (t d) -> p t d", t=NT)

            def at(i, name, k):
                act.wait_ge(A[name].sem, A[name].at(c, i, k))

            def high(i, x, k, used=True):
                at(i, "q", 2 * x + k + 1)
                if used:
                    at(i, "y", 2 * (x - 1) + k + 1)
                nc.scalar.activation(half(a_hi, k), bank(5), ACT.Copy).then_inc(A["hi"].sem, 1)

            def value_tiles(i, x):
                t = slice(4 * (x % 2), 4 * (x % 2) + 4)
                nc.scalar.activation(a_vg[:, t, :, 0:DH8],
                                     vsrc[:, t, bass.ds((i + x // 2) * BLK, BLK)].rearrange("p t (j d) -> p t j d", j=GH),
                                     ACT.Copy).then_inc(A["v"].sem, 1)

            def slot(i, x, asking, projecting, maxing):
                for u in range(4):
                    if projecting and u == 3:
                        high(i, x + 2, 1)
                    at(i, "s", 4 * x + u + 1)
                    if u >= 2:
                        at(i, "pv", 4 * x + u - 1)
                    nc.scalar.activation(a_p[u % 2], bank(2 * (u % 2), 2), ACT.Exp,
                                         scale=float(1.0 / np.sqrt(np.float32(DH8)))).then_inc(A["p"].sem, 1)
                at(i, "pv", 4 * x + 4)
                nc.scalar.activation(half(a_raw, x % 2), bank(4), ACT.Copy).then_inc(A["raw"].sem, 1)
                if projecting:
                    value_tiles(i, x + 2)
                if asking:
                    high(i, x + 3, 0)

            act.wait_ge(s_ainit, c + 1)
            for x in range(2):
                value_tiles(0, x)
            for x in range(2):
                for k in range(2):
                    high(0, x, k, used=x == 1)
            high(0, 2, 0)
            small_passes(act, slot)

        def small_pool(pool, c):
            for t in (a_m2, a_vg):
                nc.gpsimd.memset(t, 0.0).then_inc(s_acl, 1)
            pool.wait_ge(s_acl, 2 * (c + 1))
            nc.gpsimd.memset(a_vg[:, :, :, DH8:DH8 + 1], 1.0).then_inc(s_ainit, 1)

        def small_weights(dve, c, i, raw, r0, loaded=None):
            if loaded is not None:
                dve.wait_ge(loaded, 16)
            wqk = raw[:, bass.ds(i * W_A + r0, 2 * P)]
            nc.vector.tensor_copy(a_wh, wqk).then_inc(A["w"].sem, 1)
            dve.wait_ge(A["w"].sem, A["w"].at(c, i, 1))
            nc.vector.tensor_tensor(a_wl, wqk, a_wh.bitcast(F32), ALU.subtract).then_inc(A["w"].sem, 1)

        def small_dve(dve, order, c, raw, r0, before_last=None):
            def at(i, name, k):
                dve.wait_ge(A[name].sem, A[name].at(c, i, k))

            def stack(i, x, k):
                at(i, "hi", 2 * x + k + 1)
                nc.vector.scalar_tensor_tensor(out=half((a_y, a_ky)[k], x % 2), in0=half(a_hi, k).bitcast(F32),
                                               scalar=col(("lo_q", "lo_k")[k]), in1=bank(5),
                                               op0=ALU.mult, op1=ALU.add).then_inc(A["y"].sem, 1)

            def masked_keys(i, x, heads=range(GH)):
                at(i, "y", 2 * x + 2)
                for j in heads:
                    nc.vector.tensor_scalar(half(a_km[j], x % 2), half(a_ky, x % 2).bitcast(F32), col("one_rows"),
                                            col("head", j, 1), ALU.add, ALU.mult).then_inc(A["km"].sem, 1)

            def largest(i, x, n):
                t, j0 = 4 * (x % 2) + n // 2, 2 * (n % 2)
                at(i, "mx", 8 * x + n + 1)
                nc.vector.tensor_reduce(a_nm[:, t, j0:j0 + 2], bank(6 + n % 2).rearrange("p (j k) -> p j k", j=2),
                                        AX.X, ALU.max, negate=True).then_inc(A["red"].sem, 1)

            def minus(i, x):
                h = x % 2
                at(i, "red", 8 * x + 8)
                nm = a_nm[:, 4 * h:4 * h + 4, :]
                hi = a_m2[:, 4 * h:4 * h + 4, :, 24]
                lo = a_m2[:, 4 * h:4 * h + 4, :, 25]
                order.step(nc.vector.tensor_copy(hi.bitcast(F32R), nm))
                nc.vector.tensor_tensor(lo.bitcast(F32R), nm, hi, ALU.subtract).then_inc(A["m2"].sem, 1)

            def queries(i, x):
                at(i, "mt", x + 1)
                nc.vector.tensor_tensor(half(a_yf, x % 2), bank(6), half(a_y, x % 2).bitcast(F32), ALU.add)\
                    .then_inc(A["yf"].sem, 1)

            def normalise(i, x):
                at(i, "rt", x + 1)
                h = x % 2
                sums = bank(5).rearrange("p (t j c) -> p t j c", t=4, j=GH)
                rec = a_rec[:, 4 * h:4 * h + 4, :]
                order.step(nc.vector.reciprocal(rec, sums[:, :, :, DH8]))
                nc.vector.tensor_tensor(
                    a_att[:, 4 * h:4 * h + 4, bass.ds(i * BLK, BLK)].rearrange("p t (j d) -> p t j d", j=GH),
                    sums[:, :, :, 0:DH8], rec.unsqueeze(3).to_broadcast((P, 4, GH, DH8)), ALU.mult)\
                    .then_inc(A["att"].sem, 1)

            def slot(i, x, asking, projecting, maxing):
                def more(*tiles):
                    for n in tiles if maxing else ():
                        largest(i, x + 1, n)

                more(0, 1, 2)
                if projecting:
                    stack(i, x + 2, 0)
                more(3, 4)
                if projecting:
                    stack(i, x + 2, 1)
                if asking and x == 1:
                    small_weights(dve, c, i + 2, raw, r0)
                more(5, 6, 7)
                if maxing:
                    minus(i, x + 1)
                if projecting:
                    at(i, "s", 4 * x + 4)
                    masked_keys(i, x + 2, (0, 1))
                normalise(i, x)
                if maxing:
                    queries(i, x + 1)
                if projecting:
                    masked_keys(i, x + 2, (2, 3))

            for x in range(2):
                stack(0, x, 0)
                stack(0, x, 1)
                masked_keys(0, x)
            small_weights(dve, c, 1, raw, r0)
            for n in range(8):
                largest(0, 0, n)
            dve.wait_ge(s_ainit, c + 1)
            minus(0, 0)
            queries(0, 0)
            with dve.Fori(0, NG - 2) as i:
                order.loop(i, 4)
                slot(i, 0, True, True, True)
                slot(i, 1, True, True, True)
            order.end(NG - 2)
            slot(NG - 2, 0, True, True, True)
            slot(NG - 2, 1, False, True, True)
            slot(NG - 1, 0, False, False, True)
            if before_last is not None:
                before_last()
            slot(NG - 1, 1, False, False, False)

        def small_out_pe(pe):
            pe.wait_ge(A["att"].sem, A["att"].at(0, NG, 0))
            for h in range(2):
                for t in range(4 * h, 4 * h + 4):
                    last = nc.tensor.transpose(ps[:, h, (t % 4) * P:(t % 4 + 1) * P], a_att[:, t, :], ident)
                last.then_inc(s_ot, 1)
            pe.wait_ge(s_oc, 2)
            tokens_pe(a_att_t, col("wo0"))

        def small_out_act(act):
            for h in range(2):
                act.wait_ge(s_ot, h + 1)
                nc.scalar.activation(half(a_att_t, h), bank(h), ACT.Copy).then_inc(s_oc, 1)

        W = signals("w", NQ, w=2, qk=8, eh=12, el=12, vp=4, va=4, s=8, y=8, p=8, ps=8, pv=8, pvc=4, dn=4,
                    rec=4, rb=4, at=4, o=4, acc=4)
        s_wcl, s_winit = sem("w_keys_cleared"), sem("w_cleared")
        w_q = (wr[:, 0:1024], wr[:, 1024:2048])
        w_k = [(wr[:, 2048 + 2048 * h:3072 + 2048 * h], wr[:, 3072 + 2048 * h:4096 + 2048 * h]) for h in range(2)]
        w_w = (wr[:, 6144:6912], wr[:, 6912:7680])
        w_v = wf[:, 0:2048].rearrange("p (t c) -> p t c", t=NT)
        w_p = [wf[:, 2048 + 1024 * k:3072 + 1024 * k] for k in range(3)]
        w_ps = [wf[:, 5120 + 512 * k:5632 + 512 * k] for k in range(2)]
        w_pv, w_at, w_rec = wf[:, 6144:6656], wf[:, 6656:7168], wf[:, 7168:7424]
        w_den, w_ones = wf[:, 7680:7936], wf[:, 7936:7968]

        def wide_passes(eng, body):
            with eng.Fori(0, NQ - 1) as i:
                body(i, True)
            body(NQ - 1, False)

        def wide_values(n, k):
            for t in range(2):
                tile = slice((2 * (n % 4) + t) * P, (2 * (n % 4) + t + 1) * P)
                last = mm3(ps[:, k, t * QW:(t + 1) * QW], (ch[:, tile], cl[:, tile]),
                           [v[:, 2 * QW:3 * QW] for v in w_w])
            last.then_inc(W["vp"].sem, 1)

        def wide_first_values_pe(pe, c):
            pe.wait_ge(W["w"].sem, W["w"].at(c, 0, 2))
            for n in range(4):
                wide_values(n, n)

        def wide_pe(pe, c, m, raw, r0):
            def at(i, name, k):
                pe.wait_ge(W[name].sem, W[name].at(c, i, k))

            def project(i, k):
                p, h = k // 2 % 2, k % 2
                at(i, "w", 2 * (k // 4) + 2)
                for n in range(2):
                    w = [t[:, n * QW + p * P:n * QW + (p + 1) * P] for t in w_w]
                    src = (half(ch, h), half(cl, h)) if n else (half(xh, h), half(xl, h))
                    if n == 1 and k in (3, 4, 5):
                        at(i, "el", 3 * k)
                    mm3(bank(6 + n), w, src).then_inc(W["qk"].sem, 1)

            def scores(i, g):
                b = g % 4
                if b % 2 == 0:
                    at(i, "el", 3 * (g // 2) + 3)
                if g >= 2:
                    at(i, "y", g - 1)
                for h in range(2):
                    for kb in range(2):
                        keys = slice(b * S + kb * P, b * S + (kb + 1) * P)
                        last = mm3(ps[:, 2 * (g % 2) + h, kb * S:(kb + 1) * S], [t[:, keys] for t in w_k[h]],
                                   [t[:, b * S:(b + 1) * S] for t in w_q])
                last.then_inc(W["s"].sem, 1)

            def values(i, g):
                b, p = g % 4, g // 4
                at(i, "p", g + 1)
                if g == 0:
                    at(i, "va", 4)
                elif g % 2 == 0:
                    at(i, "pvc", g // 2)
                for kb in range(2):
                    for h in range(2):
                        last = nc.tensor.matmul(ps[DH * h:DH * (h + 1), 4, (b % 2) * S:(b % 2 + 1) * S],
                                                w_v[:, 2 * b + kb, (2 * p + h) * DH:(2 * p + h + 1) * DH],
                                                w_p[g % 3][:, (2 * h + kb) * S:(2 * h + kb + 1) * S],
                                                start=kb == 0, stop=kb == 1)
                last.then_inc(W["pv"].sem, 1)

            def denominators(i, k):
                if k:
                    at(i, "at", k)
                at(i, "ps", 2 * k + 2)
                for h in range(2):
                    for b in range(2):
                        r = BLK * (2 * h + b)
                        last = nc.tensor.matmul(ps[r:r + BLK, 5, 0:S], w_ones, w_ps[b][:, h * S:(h + 1) * S],
                                                start=True, stop=True)
                last.then_inc(W["dn"].sem, 1)

            def spread(i, k):
                at(i, "rec", k + 1)
                for b in range(2):
                    last = nc.tensor.matmul(ps[:, 5, b * S:(b + 1) * S], col("spread", b * P, P), w_rec,
                                            start=True, stop=True)
                last.then_inc(W["rb"].sem, 1)

            def output(i, k):
                at(i, "at", k + 1)
                wo = raw[:, bass.ds(i * W_B + (r0 + 3 * QW + (k // 2) * P), P)]
                for t in range(4):
                    last = nc.tensor.matmul(ps[:, 6, t * P:(t + 1) * P], w_at[:, t * P:(t + 1) * P], wo,
                                            start=True, stop=True)
                last.then_inc(W["o"].sem, 1)

            def body(i, ahead):
                for g in range(8):
                    k = g // 2
                    values(i, g)
                    if g + 2 < 8 or ahead:
                        scores(i, g + 2)
                    if g % 2 == 0:
                        if k < 2 or ahead:
                            at(i, "acc", (0, 0, 1, 2)[k])
                            if k == 0:
                                at(i, "va", 4)
                            if k == 1:
                                at(i, "el", 7)
                            project(i, k + 2)
                        if k >= 1:
                            spread(i, k - 1)
                        if g == 6 and ahead:
                            at(i, "el", 16)
                            wide_values(4, 6)
                    else:
                        denominators(i, k)
                        if k == 3 and ahead:
                            at(i, "el", 18)
                            wide_values(5, 7)
                        if k == 1:
                            at(i, "el", 10)
                        elif k == 2:
                            at(i, "acc", 1)
                            if ahead:
                                at(i, "el", 13)
                        elif k == 3:
                            at(i, "acc", 2)
                            if ahead:
                                at(i, "va", 5)
                        if k >= 1:
                            output(i, k - 1)
                at(i, "acc", 3)
                if ahead:
                    wide_values(6, 6)
                spread(i, 3)
                if ahead:
                    at(i, "va", 6)
                    wide_values(7, 7)
                    at(i, "va", 7)
                output(i, 3)

            pe.wait_ge(s_xs, 2 * splits(m) + 2)
            project(0, 0)
            at(0, "el", 3)
            project(0, 1)
            pe.wait_ge(s_winit, c + 1)
            at(0, "va", 2)
            scores(0, 0)
            at(0, "va", 4)
            scores(0, 1)
            at(0, "el", 6)
            wide_passes(pe, body)

        def wide_act(act, c, func, bias):
            def at(i, name, k):
                act.wait_ge(W[name].sem, W[name].at(c, i, k))

            def high(i, k):
                h = k % 2
                if k >= 2:
                    at(i, "s", 2 * k - 2)
                at(i, "qk", 2 * k + 1)
                nc.scalar.activation(half(w_q[0], h), bank(6), ACT.Copy).then_inc(W["eh"].sem, 1)
                at(i, "qk", 2 * k + 2)
                for j in range(2):
                    rows = slice(DH * j, DH * (j + 1))
                    nc.scalar.activation(half(w_k[j][0], h)[rows, :], ps[rows, 7, :], ACT.Copy)\
                        .then_inc(W["eh"].sem, 1)

            def sums(i, k):
                at(i, "pv", 2 * k + 2)
                if k:
                    at(i, "at", k)
                nc.scalar.activation(w_pv, bank(4), ACT.Copy).then_inc(W["pvc"].sem, 1)

            def value_tiles(i, n):
                if n >= 4:
                    at(i, "pv", 6 if n < 6 else 8)
                at(i, "vp", n + 1)
                m = n % 4
                nc.scalar.activation(w_v[:, 2 * m:2 * m + 2, :].rearrange("p t c -> p (t c)"),
                                     bank(n if n < 4 else 6 + n % 2), ACT.Copy).then_inc(W["va"].sem, 1)

            def weights(i, g):
                at(i, "y", g + 1)
                p = w_p[g % 8 % 3]
                nc.scalar.activation(p, p, func, bias=bias, scale=0.125).then_inc(W["p"].sem, 1)

            def body(i, ahead):
                high(i, 2)
                for g in range(2, 8):
                    k = g // 2
                    weights(i, g)
                    if g % 2 == 0:
                        sums(i, k - 1)
                    elif k < 2 or ahead:
                        high(i, k + 2)
                if ahead:
                    value_tiles(i, 4)
                sums(i, 3)
                if ahead:
                    weights(i, 8)
                    value_tiles(i, 5)
                    weights(i, 9)
                    value_tiles(i, 6)
                    value_tiles(i, 7)

            for n in range(4):
                value_tiles(0, n)
            high(0, 0)
            high(0, 1)
            weights(0, 0)
            weights(0, 1)
            wide_passes(act, body)

        def wide_pool_init(pool, c, n):
            pool.wait_ge(s_pow, n + 1)
            for j in range(2):
                rows = slice(DH * (1 - j), DH * (2 - j))
                for t in w_k[j]:
                    nc.gpsimd.memset(t[rows, :].bitcast(F32), 0.0).then_inc(s_wcl, 1)
                pool.wait_ge(s_wcl, 4 * c + 2 * (j + 1))
            nc.gpsimd.memset(w_ones, 1.0).then_inc(s_winit, 1)
            pool.wait_ge(s_winit, c + 1)

        def wide_pool(pool, c):
            def add(i, g):
                pool.wait_ge(W["p"].sem, W["p"].at(c, i, g + 1))
                if g >= 2:
                    pool.wait_ge(W["dn"].sem, W["dn"].at(c, i, g // 2))
                v = w_p[g % 8 % 3].rearrange("p (h k q) -> p h k q", h=2, k=2)
                nc.gpsimd.tensor_tensor(w_ps[g % 2].rearrange("p (h q) -> p h q", h=2), v[:, :, 0, :],
                                        v[:, :, 1, :], ALU.add).then_inc(W["ps"].sem, 1)

            def body(i, ahead):
                for g in range(2, 10 if ahead else 8):
                    add(i, g)

            add(0, 0)
            add(0, 1)
            wide_passes(pool, body)

        def wide_weights(dve, c, i, raw, r0, loaded=None):
            if loaded is not None:
                dve.wait_ge(loaded, 16)
            qkv = raw[:, bass.ds(i * W_B + r0, 3 * QW)]
            nc.vector.tensor_copy(w_w[0], qkv).then_inc(W["w"].sem, 1)
            dve.wait_ge(W["w"].sem, W["w"].at(c, i, 1))
            nc.vector.tensor_tensor(w_w[1], qkv, w_w[0].bitcast(F32), ALU.subtract).then_inc(W["w"].sem, 1)

        def wide_dve(dve, order, c, raw, r0):
            def at(i, name, k):
                dve.wait_ge(W[name].sem, W[name].at(c, i, k))

            def low(i, k):
                h = k % 2
                at(i, "eh", 3 * k + 1)
                nc.vector.tensor_tensor(half(w_q[1], h), bank(6), half(w_q[0], h).bitcast(F32), ALU.subtract)\
                    .then_inc(W["el"].sem, 1)
                at(i, "eh", 3 * k + 3)
                for j in range(2):
                    rows = slice(DH * j, DH * (j + 1))
                    nc.vector.tensor_tensor(half(w_k[j][1], h)[rows, :], ps[rows, 7, :],
                                            half(w_k[j][0], h)[rows, :].bitcast(F32), ALU.subtract)\
                        .then_inc(W["el"].sem, 1)

            def bound(i, g):
                at(i, "s", g + 1)
                if g >= 3:
                    at(i, "ps", g - 2 if g < 8 else g - 1)
                v = w_p[g % 8 % 3].rearrange("p (h c) -> p h c", h=2)
                s = ps[:, 2 * (g % 2):2 * (g % 2) + 2, :]
                if c == 0:
                    ins = nc.vector.scalar_tensor_tensor(
                        out=v, in0=s, scalar=w_floor, op0=ALU.max, op1=ALU.min,
                        in1=cap[:, g % 4, :, :].rearrange("p k q -> p (k q)").unsqueeze(1).to_broadcast((P, 2, HALF)))
                else:
                    ins = nc.vector.tensor_scalar(v, s, -8.0 * CLIP, 8.0 * CLIP, ALU.max, ALU.min)
                ins.then_inc(W["y"].sem, 1)

            def reciprocal(i, k):
                at(i, "dn", k + 1)
                if c == 0:
                    order.step(nc.vector.tensor_scalar(w_den, ps[:, 5, 0:S], IEPS, None, ALU.add))
                    nc.vector.reciprocal(w_rec, w_den).then_inc(W["rec"].sem, 1)
                else:
                    nc.vector.reciprocal(w_rec, ps[:, 5, 0:S]).then_inc(W["rec"].sem, 1)

            def normalise(i, k):
                at(i, "rb", k + 1)
                at(i, "pvc", k + 1)
                nc.vector.tensor_tensor(w_at, w_pv, bank(5), ALU.mult).then_inc(W["at"].sem, 1)

            def add(i, k):
                at(i, "o", k + 1)
                at(i, "acc", k)
                h = k % 2
                r = xn[:, 4 * h:4 * h + 4, :].rearrange("p t d -> p (t d)")
                nc.vector.tensor_tensor(r, r, bank(6), ALU.add).then_inc(W["acc"].sem, 1)

            def body(i, ahead):
                for k in range(4):
                    if k < 3 or ahead:
                        bound(i, 2 * k + 2)
                    if k < 2 or ahead:
                        low(i, k + 2)
                    if k:
                        normalise(i, k - 1)
                    if k < 3 or ahead:
                        bound(i, 2 * k + 3)
                    if k == 1 and ahead:
                        at(i, "qk", 8)
                        wide_weights(dve, c, i + 1, raw, r0)
                    reciprocal(i, k)
                    if k:
                        add(i, k - 1)
                normalise(i, 3)
                add(i, 3)

            low(0, 0)
            low(0, 1)
            bound(0, 0)
            bound(0, 1)
            per = 4 if c == 0 else 0
            with dve.Fori(0, NQ - 1) as i:
                order.loop(i, per)
                body(i, True)
            order.end(NQ - 1)
            body(NQ - 1, False)

        def tokens_in(dve, order, n, src):
            for h in range(2):
                r = res[:, 4 * h:4 * h + 4, :].rearrange("p t d -> p (t d)")
                s = src[:, 4 * h:4 * h + 4, :].rearrange("p t d -> p (t d)")
                order.done(nc.vector.scalar_tensor_tensor(out=r, in0=s, scalar=gate[:, n:n + 1], in1=r,
                                                          op0=ALU.mult, op1=ALU.add))
            order.wait()

        def pick_max(order, oh, s, t1, m):
            order.step(nc.vector.tensor_reduce(m, s, AX.X, ALU.max))
            mb = m.unsqueeze(2).to_broadcast((P, NT, E))
            order.step(nc.vector.tensor_tensor(t1, s, mb, ALU.is_equal))
            iota = col("iota").unsqueeze(1).to_broadcast((P, NT, E))
            order.step(nc.vector.tensor_scalar(t1, t1, -float(E), None, ALU.mult))
            order.step(nc.vector.tensor_tensor(t1, t1, iota, ALU.add))
            order.step(nc.vector.tensor_reduce(m2col, t1, AX.X, ALU.min))
            order.step(nc.vector.tensor_tensor(oh, t1, m2col.unsqueeze(2).to_broadcast((P, NT, E)), ALU.is_equal))

        def split_stack(order, w, at, last=False):
            hi, lo = stk[:, :, at:at + E], stk[:, :, at + E:at + 2 * E]
            order.step(nc.vector.tensor_copy(hi.bitcast(F32R), w))
            ins = nc.vector.tensor_tensor(lo.bitcast(F32R), w, hi, ALU.subtract)
            if last:
                ins.then_inc(s_st, 1)
            else:
                order.step(ins)

        sp_ = [sb(f"router_{k}", [P, NT, E]) for k in range(5)]
        lg, ex, t1, oh, oh2 = [t[:, :, :] for t in sp_]
        mcol_t, m2col_t, rcol_t = sb("router_max", [P, NT]), sb("router_first", [P, NT]), sb("router_sum", [P, NT])
        mcol, m2col, rcol = mcol_t[:, :], m2col_t[:, :], rcol_t[:, :]
        stk_t = sb("router_stack", [P, NT, BLK])
        stk = stk_t[:, :, :]
        s_lg, s_lx, s_le, s_st, s_sk, s_wt = [sem(n) for n in (
            "logits_product", "logits_less_max", "logits_exponentials", "stack_ready", "stack_transposed", "stack_copied")]

        def softmax_dve(dve, order, n):
            order.step(nc.vector.tensor_reduce(mcol, lg, AX.X, ALU.max))
            nc.vector.tensor_tensor(lg, lg, mcol.unsqueeze(2).to_broadcast((P, NT, E)), ALU.subtract).then_inc(s_lx, 1)
            dve.wait_ge(s_le, n + 1)
            order.step(nc.vector.tensor_reduce(rcol, ex, AX.X, ALU.add))
            order.step(nc.vector.reciprocal(rcol, rcol))
            order.step(nc.vector.tensor_tensor(ex, ex, rcol.unsqueeze(2).to_broadcast((P, NT, E)), ALU.mult))

        def softmax_act(act, n, scale=1.0):
            act.wait_ge(s_lx, n + 1)
            nc.scalar.activation(ex, lg, ACT.Exp, scale=scale).then_inc(s_le, 1)

        def logits_pe(src, w, k):
            for t in range(NT):
                last = nc.tensor.matmul(ps[:, k, t * E:(t + 1) * E], src[:, t * P:(t + 1) * P], w, start=True, stop=True)
            last.then_inc(s_lg, 1)

        def stack_pe(pe, n):
            pe.wait_ge(s_st, n + 1)
            for t in range(NT):
                last = nc.tensor.transpose(ps[0:BLK, 6 + t // 4, (t % 4) * P:(t % 4 + 1) * P], stk[:, t, :], ident)
            last.then_inc(s_sk, 1)

        def stack_act(act, n, wt):
            act.wait_ge(s_sk, n + 1)
            nc.scalar.activation(wt[0:BLK, :], ps[0:BLK, 6:8, :].rearrange("p a b -> p (a b)"), ACT.Copy).then_inc(s_wt, 1)

        F = signals("f0", NKT, w=8, x=4, yw=4, xs=4, z=4, u=4, acc=4)
        s_fp, s_fh, s_fl, s_fc, s_fb, s_fo = [sem("f0_" + n) for n in ("product", "high", "low", "sums_split", "bias", "whole")]
        f_slots = [(wr[:, 1024 * 2 * k:1024 * (2 * k + 1)], wr[:, 1024 * (2 * k + 1):1024 * (2 * k + 2)]) for k in range(3)]
        f_q, f_k, f_ik = f_slots
        f_iq = (xh[:, :], xl[:, :])
        f_wt = wr[:, 6144:7168]
        f_w = (wr[:, 7168:7680], wr[:, 7680:8192])
        f_vw = [(wr[:, 8192 + 640 * b:8448 + 640 * b], wr[:, 8448 + 640 * b:8704 + 640 * b]) for b in range(2)]
        f_sel = [wr[:, 8704 + 640 * b:8832 + 640 * b] for b in range(2)]
        f_cum = wf[:, 0:1024]
        f_xs = [wf[:, 1024 + 512 * k:1536 + 512 * k] for k in range(2)]
        f_z = [wf[:, 2048 + 512 * k:2560 + 512 * k] for k in range(2)]
        f_u = [wf[:, 3072 + 128 * k:3200 + 128 * k] for k in range(2)]
        f_ones = wf[:, 3328:3584]
        f_h = [wf[:, 4096 + 1024 * k:5120 + 1024 * k] for k in range(2)]
        f_zz = [wf[:, 6144 + 512 * k:6656 + 512 * k] for k in range(2)]
        f_steps = ((0, "x", f_q), (1, "cum", f_k), (3, "q", None), (2, "q", f_iq), (3, "iq", None), (2, "k", f_ik))

        def f0_passes(eng, body):
            with eng.Fori(0, NKT - 1) as i:
                body(i, True)
            body(NKT - 1, False)

        def f0_pe(pe, m):
            pe.wait_ge(s_xs, 2 * splits(m) + 2)
            pe.wait_ge(s_fc, 1)
            src = {"x": (xh[:, :], xl[:, :]), "cum": f_ik, "q": f_q, "k": f_k, "iq": f_iq}
            low = {2: 1, 3: 1, 4: 3, 5: 2}
            for j, (w, s, _) in enumerate(f_steps):
                if j in low:
                    pe.wait_ge(s_fl, low[j])
                if j == 5:
                    pe.wait_ge(s_fh, 3)
                for h in range(2):
                    last = mm3(bank(2 * (j % 3) + h), [v[:, w * P:(w + 1) * P] for v in f_w],
                               [half(v, h) for v in src[s]])
                last.then_inc(s_fp, 1)
                if j >= 4:
                    pe.wait_ge(s_fh, (3, 5)[j - 4])
                    logits_pe(f_h[j - 4], col("router_w2"), 2 + j)
            stack_pe(pe, 0)
            pe.wait_ge(s_wt, 1)
            pe.wait_ge(s_fl, 4)

            def at(i, name, k):
                pe.wait_ge(F[name].sem, F[name].at(0, i, k))

            def products(i, n):
                br, h = n // 2 % 2, n % 2
                if h == 0:
                    at(i, "w", 4 * (n // 2) + 4)
                if n >= 2:
                    at(i, "xs", n - 1)
                    at(i, "z", n - 1)
                q, k = ((f_q, f_k), (f_iq, f_ik))[br]
                mm3(bank(h), [v[:, 0:P] for v in f_vw[br]], [half(v, h) for v in q]).then_inc(F["x"].sem, 1)
                mm3(bank(2 + h), [v[:, P:2 * P] for v in f_vw[br]], [half(v, h) for v in k])
                nc.tensor.matmul(bank(4 + h), f_sel[br], half(f_wt, h), start=True, stop=True)\
                    .then_inc(F["yw"].sem, 1)

            def out(i, n):
                br, h = n // 2, n % 2
                at(i, "z", n + 1)
                if n >= 2:
                    at(i, "acc", n - 1)
                nc.tensor.matmul(bank(6 + h), f_u[br], f_zz[h], start=True, stop=True).then_inc(F["u"].sem, 1)

            def body(i, ahead):
                for n in range(4):
                    out(i, n)
                    if n < 2 or ahead:
                        products(i, n + 2)

            products(0, 0)
            products(0, 1)
            f0_passes(pe, body)
            pe.wait_ge(F["acc"].sem, F["acc"].at(0, NKT, 0))
            for h in range(2):
                last = nc.tensor.matmul(bank(6 + h), col("b_experts"), half(f_wt, h).bitcast(F32), start=True, stop=True)
            last.then_inc(s_fb, 1)
            pe.wait_ge(s_fo, 1)
            tokens_pe(out_t, col("W_O"))

        def f0_act(act):
            for j, (_, _, dst) in enumerate(f_steps):
                if j == 5:
                    softmax_act(act, 0)
                act.wait_ge(s_fp, j + 1)
                if dst is None:
                    ins = nc.scalar.activation(f_h[j // 2 - 1], bank(2 * (j % 3), 2), ACT.Gelu, bias=col("rb1"))
                else:
                    ins = nc.scalar.activation(dst[0], bank(2 * (j % 3), 2), ACT.Copy)
                ins.then_inc(s_fh, 1)
            softmax_act(act, 1)
            stack_act(act, 0, f_wt)
            with act.Fori(0, NKT) as i:
                for n in range(4):
                    act.wait_ge(F["x"].sem, F["x"].at(0, i, n + 1))
                    if n >= 2:
                        act.wait_ge(F["z"].sem, F["z"].at(0, i, n - 1))
                    nc.scalar.activation(f_xs[n % 2], bank(n % 2), ACT.Copy).then_inc(F["xs"].sem, 1)

        def f0_weights(dve, order):
            order.step(nc.vector.tensor_copy(f_w[0], col("W_Q", 0, 4 * P)))
            order.done(nc.vector.tensor_tensor(f_w[1], col("W_Q", 0, 4 * P), f_w[0].bitcast(F32), ALU.subtract))

        def clear_pool(pool, n, t, *values):
            for v, x in values:
                nc.gpsimd.memset(v, x).then_inc(s_pcl, 1)
            pool.wait_ge(s_pcl, t)
            nc.gpsimd.memset(out_t[:, :], 0.0).then_inc(s_clear, 1)
            pool.wait_ge(s_clear, n + 1)

        def f0_dve(dve, order):
            dve.wait_ge(s_clear, 1)
            for b in range(B):
                order.done(nc.vector.tensor_tensor_scan(f_cum[:, b * S:(b + 1) * S], f_ones, xf[:, b * S:(b + 1) * S],
                                                        0.0, ALU.mult, ALU.add))
            order.wait()
            order.step(nc.vector.tensor_copy(f_ik[0], f_cum))
            nc.vector.tensor_tensor(f_ik[1], f_cum, f_ik[0].bitcast(F32), ALU.subtract).then_inc(s_fc, 1)
            def low(j):
                dve.wait_ge(s_fh, j + 1)
                dst = f_steps[j][2]
                nc.vector.tensor_tensor(dst[1], bank(2 * (j % 3), 2), dst[0].bitcast(F32), ALU.subtract).then_inc(s_fl, 1)

            for j in (0, 1, 3):
                low(j)
            for br in range(2):
                if br:
                    low(5)
                dve.wait_ge(s_lg, br + 1)
                src = ps[:, 6 + br, 0:NT * E].rearrange("p (t e) -> p t e", t=NT)
                order.step(nc.vector.tensor_tensor(lg, src, col("rb2").unsqueeze(1).to_broadcast((P, NT, E)), ALU.add))
                order.step(nc.vector.tensor_tensor(lg, lg, col("ebias").unsqueeze(1).to_broadcast((P, NT, E)), ALU.add))
                softmax_dve(dve, order, br)
                e2 = ex.rearrange("p (b q) e -> p b q e", b=B)
                for q in range(2):
                    order.done(nc.vector.tensor_scalar(e2[:, :, q, :], e2[:, :, q, :], col("inv_n", q, 1), None, ALU.mult))
                order.wait()
                if br:
                    order.step(nc.vector.tensor_scalar(ex, ex, col("alpha"), None, ALU.mult))
                split_stack(order, ex, 2 * E * br, br == 1)
            dve.wait_ge(ld["f0"], 16)
            dve.wait_ge(s_wt, 1)

            def at(i, name, k):
                dve.wait_ge(F[name].sem, F[name].at(0, i, k))

            def weights(i, br):
                base = i * (2 * W_F0) + (RF0 + br * W_F0)
                vw = raw_a[:, bass.ds(base, 2 * P)]
                nc.vector.tensor_copy(f_vw[br][0], vw).then_inc(F["w"].sem, 1)
                nc.vector.tensor_copy(f_u[br], raw_a[:, bass.ds(base + 2 * P, P)]).then_inc(F["w"].sem, 1)
                nc.vector.tensor_copy(f_sel[br], raw_a[:, bass.ds(base + 3 * P, P)]).then_inc(F["w"].sem, 1)
                at(i, "w", 4 * br + 1)
                nc.vector.tensor_tensor(f_vw[br][1], vw, f_vw[br][0].bitcast(F32), ALU.subtract)\
                    .then_inc(F["w"].sem, 1)

            def weigh(i, n):
                h = n % 2
                at(i, "xs", n + 1)
                at(i, "yw", n + 1)
                order.step(nc.vector.tensor_tensor(f_z[h], f_xs[h], bank(2 + h), ALU.mult))
                if n >= 2:
                    at(i, "u", n - 1)
                nc.vector.tensor_tensor(f_zz[h], f_z[h], bank(4 + h), ALU.mult).then_inc(F["z"].sem, 1)

            def add(i, n):
                h = n % 2
                at(i, "u", n + 1)
                nc.vector.tensor_tensor(half(out_t, h), half(out_t, h), bank(6 + h), ALU.add)\
                    .then_inc(F["acc"].sem, 1)

            def body(i, ahead):
                for n in range(4):
                    add(i, n)
                    if n < 2 or ahead:
                        weigh(i, n + 2)
                    if n % 2 == 1 and ahead:
                        weights(i + 1, n // 2)

            weights(0, 0)
            weights(0, 1)
            weigh(0, 0)
            weigh(0, 1)
            with dve.Fori(0, NKT - 1) as i:
                order.loop(i, 4)
                body(i, True)
            order.end(NKT - 1)
            body(NKT - 1, False)
            dve.wait_ge(F["acc"].sem, F["acc"].at(0, NKT, 0))
            dve.wait_ge(s_fb, 1)
            nc.vector.tensor_tensor(out_t[:, :], out_t[:, :], bank(6, 2), ALU.add).then_inc(s_fo, 1)

        G = signals("f1", E // 2, w=10, up=16, a=16, al=16, dn=16, cb=2, cc=2, t=4, acc=4)
        s_gb = sem("f1_bias_product")
        g_w = [(wr[:, 2048 * s:2048 * s + 1024], wr[:, 2048 * s + 1024:2048 * s + 2048]) for s in range(2)]
        g_a = [(wr[:, 4096 + 1024 * k:4608 + 1024 * k], wr[:, 4608 + 1024 * k:5120 + 1024 * k]) for k in range(4)]
        g_wt = wr[:, 8192:9216]
        g_sel = [wr[:, 9216 + 128 * k:9344 + 128 * k] for k in range(2)]
        g_af = [wf[:, 4096 + 512 * k:4608 + 512 * k] for k in range(4)]
        g_cw = wf[:, 1024:2048]
        g_t = [wf[:, 2048 + 512 * k:2560 + 512 * k] for k in range(2)]
        g_shift = wf[:, 3072:3072 + E * NF]
        g_b1 = [wf[:, 3104 + NF * k:3104 + NF * (k + 1)] for k in range(2)]
        PASSES = E // 2

        def passes(eng, body):
            with eng.Fori(0, PASSES - 1) as i:
                body(i, False)
            body(PASSES - 1, True)

        def f1_shifts_pe(pe):
            pe.wait_ge(ld["f1"], 16)
            for e in range(E):
                for f in range(NF):
                    last = nc.tensor.matmul(ps[:, 4, e * NF + f:e * NF + f + 1],
                                            raw_a[:, e * W_F1 + f * P:e * W_F1 + (f + 1) * P], col("beta", e, 1),
                                            start=True, stop=True)
            last.then_inc(s_gb, 1)

        def f1_pe(pe, m):
            pe.wait_ge(s_xf, 2 * m + 2)
            logits_pe(xf, col("centroids"), 5)
            def up(i, n):
                s, h, f = n // 8, n // 4 % 2, n % 4
                if n % 8 == 0:
                    pe.wait_ge(G["w"].sem, G["w"].at(0, i, 5 * s + 5))
                pe.wait_ge(G["a"].sem, G["a"].at(0, i, max(0, n - 2)))
                mm3(ps[:, (0, 1, 2, 7)[n % 4], :], [v[:, f * P:(f + 1) * P] for v in g_w[s % 2]],
                    (half(xh, h), half(xl, h))).then_inc(G["up"].sem, 1)

            def body(i, last_pass):
                def at(name, k):
                    pe.wait_ge(G[name].sem, G[name].at(0, i, k))

                def down(n):
                    s, h, f = n // 8, n // 4 % 2, n % 4
                    at("al", n + 1)
                    if f == 0:
                        at("t", 2 * s + h - 1)
                    last = mm3(bank(3 + h), [v[:, 512 + f * P:512 + (f + 1) * P] for v in g_w[s]], g_a[n % 4],
                               start=f == 0, stop=f == NF - 1)
                    last.then_inc(G["dn"].sem, 1)

                for n in range(16):
                    if n + 2 < 16 or not last_pass:
                        up(i, n + 2)
                    if n % 8 == 2:
                        s = n // 8
                        at("cc", s)
                        for h in range(2):
                            last = nc.tensor.matmul(bank(5 + h), g_sel[s], half(g_wt, h), start=True, stop=True)
                        last.then_inc(G["cb"].sem, 1)
                    down(n)

            pe.wait_ge(s_xs, 2 * splits(m) + 2)
            up(0, 0)
            up(0, 1)
            stack_pe(pe, 1)
            pe.wait_ge(s_wt, 2)
            passes(pe, body)
            pe.wait_ge(G["acc"].sem, G["acc"].at(0, PASSES, 0))
            back_pe(pe)

        def f1_act(act):
            softmax_act(act, 2, scale=-1.0)
            stack_act(act, 1, g_wt)

            def body(i, last_pass):
                def at(name, k):
                    act.wait_ge(G[name].sem, G[name].at(0, i, k))

                for n in range(16):
                    s, f = n // 8, n % 4
                    at("up", n + 1)
                    at("al", n - 3)
                    at("dn", n - 3)
                    b, hidden = g_b1[s][:, f:f + 1], bank((0, 1, 2, 7)[n % 4])
                    nc.scalar.activation(g_af[n % 4], hidden, ACT.Relu, bias=b).then_inc(s_act, 1)
                    nc.scalar.activation(g_a[n % 4][0], hidden, ACT.Relu, bias=b).then_inc(G["a"].sem, 1)
                    if n % 8 == 4:
                        at("cb", s + 1)
                        at("t", 2 * s)
                        nc.scalar.activation(g_cw, bank(5, 2), ACT.Copy).then_inc(G["cc"].sem, 1)

            passes(act, body)

        def f1_pool(pool):

            def body(i, last_pass):
                for n in range(4):
                    h = n % 2
                    pool.wait_ge(G["t"].sem, G["t"].at(0, i, n + 1))
                    pool.wait_ge(G["acc"].sem, G["acc"].at(0, i, n - 1))
                    nc.gpsimd.tensor_tensor(half(out_t, h), half(out_t, h), g_t[h], ALU.add).then_inc(G["acc"].sem, 1)

            passes(pool, body)

        def f1_piece(dve, i, s, k):
            def expert(base, n):
                return sm[:, bass.ds(i * (2 * n) + (s * n + SMALL[base][0]), n)]

            w1 = raw_a[:, bass.ds(i * (2 * W_F1) + s * W_F1, 512)]
            w2 = raw_a[:, bass.ds(i * (2 * W_F1) + (s * W_F1 + 512), 512)]
            (hi, lo), gam = g_w[s], expert("gamma", 1)
            if k == 0:
                ins = nc.vector.tensor_scalar(hi[:, 0:512], w1, gam, None, ALU.mult)
            elif k == 1:
                ins = nc.vector.tensor_copy(hi[:, 512:1024], w2)
            elif k == 2:
                dve.wait_ge(G["w"].sem, G["w"].at(0, i, 5 * s + 1))
                ins = nc.vector.scalar_tensor_tensor(out=lo[:, 0:512], in0=w1, scalar=gam,
                                                     in1=hi[:, 0:512].bitcast(F32), op0=ALU.mult, op1=ALU.subtract)
            elif k == 3:
                dve.wait_ge(G["w"].sem, G["w"].at(0, i, 5 * s + 2))
                ins = nc.vector.tensor_tensor(lo[:, 512:1024], w2, hi[:, 512:1024].bitcast(F32), ALU.subtract)
            else:
                nc.vector.tensor_tensor(g_b1[s], g_shift[:, bass.ds(i * (2 * NF) + s * NF, NF)], expert("b1", NF), ALU.add)
                ins = nc.vector.tensor_copy(g_sel[s], expert("sel_e", P))
            ins.then_inc(G["w"].sem, 1)

        def f1_first(dve):
            dve.wait_ge(ld["f1"], 16)
            for k in range(4):
                f1_piece(dve, 0, 0, k)

        def f1_shifts_dve(dve, order):
            dve.wait_ge(s_gb, 1)
            order.step(nc.vector.tensor_copy(g_shift, ps[:, 4, 0:E * NF]))
            f1_piece(dve, 0, 0, 4)

        def f1_dve(dve, order):
            dve.wait_ge(s_lg, 3)
            order.step(nc.vector.tensor_copy(lg, ps[:, 5, 0:NT * E].rearrange("p (t e) -> p t e", t=NT)))
            pick_max(order, oh, lg, t1, mcol)
            nc.vector.tensor_copy(lg, mcol.unsqueeze(2).to_broadcast((P, NT, E))).then_inc(s_lx, 1)
            dve.wait_ge(s_le, 3)
            order.step(nc.vector.tensor_scalar(ex, ex, 1.0, None, ALU.add))
            order.step(nc.vector.reciprocal(ex, ex))
            order.step(nc.vector.tensor_tensor(ex, ex, oh, ALU.mult))
            dve.wait_ge(s_clear, 2)
            split_stack(order, ex, 0, True)

            def step(i, n, last_pass=False):
                def at(name, k):
                    dve.wait_ge(G[name].sem, G[name].at(0, i, k))

                s = n // 8
                at("a", n + 1)
                at("dn", n - 3)
                nc.vector.tensor_tensor(g_a[n % 4][1], g_af[n % 4], g_a[n % 4][0].bitcast(F32), ALU.subtract)\
                    .then_inc(G["al"].sem, 1)
                if n % 4 == 1 and n > 1:
                    weigh(dve, i, (n - 5) // 4)
                for k in () if s == 1 and last_pass or n >= 16 else {2: (0, 1), 3: (2,), 4: (3, 4)}.get(n % 8, ()):
                    if k == 0:
                        at("dn", 8 * s)
                        at("cb", s)
                    if s == 0:
                        f1_piece(dve, i, 1, k)
                    else:
                        f1_piece(dve, i + 1, 0, k)

            def body(i, last_pass):
                for n in range(2, 16 if last_pass else 18):
                    step(i, n, last_pass)
                if last_pass:
                    weigh(dve, i, 3)

            def weigh(dve, i, q):
                s, h = q // 2, q % 2
                dve.wait_ge(G["dn"].sem, G["dn"].at(0, i, 4 * q + 4))
                dve.wait_ge(G["cc"].sem, G["cc"].at(0, i, s + 1))
                dve.wait_ge(G["acc"].sem, G["acc"].at(0, i, q - 1))
                b2 = sm[:, bass.ds(i * 2 + (s + SMALL["b2"][0]), 1)]
                nc.vector.scalar_tensor_tensor(out=g_t[h], in0=bank(3 + h), scalar=b2, in1=half(g_cw, h),
                                               op0=ALU.add, op1=ALU.mult).then_inc(G["t"].sem, 1)

            step(0, 0)
            step(0, 1)
            passes(dve, body)

        q_s = [sb(f"quant_{n}", [P, 1]) for n in ("max", "all", "scale", "inverse")]
        q_w = sb("quant_weights", [P, D])
        s_qm, s_qa, s_ql, s_qw = [sem("quant_" + n) for n in ("row_max", "all_max", "low_rank", "ready")]

        def quant_pool(pool):
            pool.wait_ge(s_qm, 1)
            nc.gpsimd.partition_all_reduce(q_s[1][:, :], q_s[0][:, :], P, bass.bass_isa.ReduceOp.max).then_inc(s_qa, 1)

        def quant_pe(pe):
            nc.tensor.matmul(ps[:, 4, 0:D], col("lora_a"), col("lora_b"), start=True, stop=True).then_inc(s_ql, 1)

        def quant_dve_max(dve):
            nc.vector.tensor_reduce(q_s[0][:, :], col("quant_w"), AX.X, ALU.max, apply_absolute_value=True).then_inc(s_qm, 1)

        def quant_dve(dve, order):
            dve.wait_ge(s_qa, 1)
            dve.wait_ge(s_ql, 1)
            scale, inv, w = q_s[2][:, :], q_s[3][:, :], q_w[:, :]
            order.step(nc.vector.tensor_scalar(scale, q_s[1][:, :], 1.0 / 7.0, None, ALU.mult))
            order.step(nc.vector.reciprocal(inv, scale))
            order.step(nc.vector.tensor_scalar(w, col("quant_w"), inv, None, ALU.mult))
            order.step(nc.vector.tensor_scalar(w, w, ROUND, None, ALU.add))
            order.step(nc.vector.tensor_scalar(w, w, -ROUND, 7.0, ALU.add, ALU.min))
            order.step(nc.vector.tensor_scalar(w, w, -8.0, scale, ALU.max, ALU.mult))
            nc.vector.tensor_tensor(w, w, ps[:, 4, 0:D], ALU.add).then_inc(s_qw, 1)

        K = signals("f3", E // 2, w=10, gu=16, sg=16, a=16, ah=16, al=16, dn=16, cb=2, cc=2, t=4, acc=4)
        s_kw = sem("f3_shared_weights")
        k_w = [(wr[:, 3072 * s:3072 * s + 1536], wr[:, 3072 * s + 1536:3072 * s + 3072]) for s in range(2)]
        k_a = [(wr[:, 6144 + 512 * k:6656 + 512 * k], wr[:, 7168 + 512 * k:7680 + 512 * k]) for k in range(2)]
        k_wt = wr[:, 8192:9216]
        k_sel = [wr[:, 9216 + 128 * k:9344 + 128 * k] for k in range(2)]
        k_sg = [wf[:, 512 * k:512 * (k + 1)] for k in range(2)]
        k_af = [wf[:, 1024 + 512 * k:1536 + 512 * k] for k in range(2)]
        k_cw = wf[:, 2048:3072]
        k_t = [wf[:, 3072 + 512 * k:3584 + 512 * k] for k in range(2)]
        FULL = [(s, h, f, NF) for s in range(2) for h in range(2) for f in range(NF)]
        SHARED = [(0, h, f, 2) for h in range(2) for f in range(2)]

        def f3_pe(pe, m):
            pe.wait_ge(s_xf, 2 * m + 2)
            logits_pe(xf, col("gate_w"), 5)
            pe.wait_ge(s_xs, 2 * splits(m) + 2)

            def up(i, n, shared=False):
                s, h, f, nf = (SHARED if shared else FULL)[n % 16]
                if h == 0 and f == 0:
                    if shared:
                        pe.wait_ge(s_kw, 2)
                    else:
                        pe.wait_ge(K["w"].sem, K["w"].at(0, i, 5 * (n // 8) + 5))
                pe.wait_ge(K["a"].sem, K["a"].at(0, i, n - 1))
                for k in range(2):
                    c0 = (k * nf + f) * P
                    last = mm3(bank(2 * k + n % 2), [v[:, c0:c0 + P] for v in k_w[s]], (half(xh, h), half(xl, h)))
                last.then_inc(K["gu"].sem, 1)

            def body(i, last_pass, shared):
                steps = SHARED if shared else FULL

                def at(name, k):
                    pe.wait_ge(K[name].sem, K[name].at(0, i, k))

                def down(n):
                    s, h, f, nf = steps[n]
                    at("al", n + 1)
                    if f == 0:
                        at("t", 2 * s + h - 1)
                    c0 = (2 * nf + f) * P
                    mm3(bank(4 + h), [v[:, c0:c0 + P] for v in k_w[s]], k_a[n % 2], start=f == 0, stop=f == nf - 1)\
                        .then_inc(K["dn"].sem, 1)

                for n in range(len(steps)):
                    if n + 2 < len(steps) or not shared:
                        up(i, n + 2, shared or (last_pass and n + 2 >= 16))
                    if n % 8 == 3 and not shared:
                        s = n // 8
                        at("cc", s)
                        for h in range(2):
                            last = nc.tensor.matmul(bank(6 + h), k_sel[s], half(k_wt, h), start=True, stop=True)
                        last.then_inc(K["cb"].sem, 1)
                    down(n)

            up(0, 0)
            up(0, 1)
            stack_pe(pe, 2)
            pe.wait_ge(s_wt, 3)
            with pe.Fori(0, PASSES - 1) as i:
                body(i, False, False)
            body(PASSES - 1, True, False)
            body(PASSES, True, True)
            pe.wait_ge(K["acc"].sem, K["acc"].at(0, PASSES, 2))
            back_pe(pe)

        def f3_act(act):
            softmax_act(act, 3)
            stack_act(act, 2, k_wt)

            def at(i, name, k):
                act.wait_ge(K[name].sem, K[name].at(0, i, k))

            def gates(i, n):
                at(i, "gu", n + 1)
                at(i, "a", n - 1)
                nc.scalar.activation(k_sg[n % 2], bank(n % 2), ACT.Silu).then_inc(K["sg"].sem, 1)

            def high(i, n):
                at(i, "a", n + 1)
                at(i, "dn", n - 1)
                nc.scalar.activation(k_a[n % 2][0], k_af[n % 2], ACT.Copy).then_inc(K["ah"].sem, 1)

            def body(i, last_pass):
                for n in range(1, 20 if last_pass else 17):
                    gates(i, n)
                    high(i, n - 1)
                    if n % 8 == 5:
                        s = n // 8
                        at(i, "cb", s + 1)
                        at(i, "t", 2 * s)
                        nc.scalar.activation(k_cw, bank(6, 2), ACT.Copy).then_inc(K["cc"].sem, 1)
                if last_pass:
                    high(i, 19)

            gates(0, 0)
            passes(act, body)

        def f3_pool(pool):
            def body(i, count):
                for n in range(count):
                    h = n % 2
                    pool.wait_ge(K["t"].sem, K["t"].at(0, i, n + 1))
                    pool.wait_ge(K["acc"].sem, K["acc"].at(0, i, n - 1))
                    nc.gpsimd.tensor_tensor(half(out_t, h), half(out_t, h), k_t[h], ALU.add).then_inc(K["acc"].sem, 1)

            with pool.Fori(0, PASSES) as i:
                body(i, 4)
            body(PASSES, 2)

        def f3_piece(dve, i, s, k):
            w = raw_b[:, bass.ds(i * (2 * W_F3) + s * W_F3, W_F3)]
            hi, lo = k_w[s]
            c = slice(768 * (k % 2), 768 * (k % 2 + 1))
            if k < 2:
                ins = nc.vector.tensor_copy(hi[:, c], w[:, c])
            elif k < 4:
                dve.wait_ge(K["w"].sem, K["w"].at(0, i, 5 * s + k - 1))
                ins = nc.vector.tensor_tensor(lo[:, c], w[:, c], hi[:, c].bitcast(F32), ALU.subtract)
            else:
                ins = nc.vector.tensor_copy(k_sel[s], sm[:, bass.ds(i * (2 * P) + (s * P + SMALL["sel_e"][0]), P)])
            ins.then_inc(K["w"].sem, 1)

        def f3_first(dve):
            dve.wait_ge(ld["f3"], 16)
            for k in range(5):
                f3_piece(dve, 0, 0, k)

        def f3_dve(dve, order):
            dve.wait_ge(s_lg, 4)
            order.step(nc.vector.tensor_copy(lg, ps[:, 5, 0:NT * E].rearrange("p (t e) -> p t e", t=NT)))
            softmax_dve(dve, order, 3)
            pick_max(order, oh, ex, t1, mcol)
            order.step(nc.vector.scalar_tensor_tensor(out=lg.rearrange("p t e -> p (t e)"), in0=oh.rearrange("p t e -> p (t e)"),
                                                      scalar=-2.0, in1=ex.rearrange("p t e -> p (t e)"),
                                                      op0=ALU.mult, op1=ALU.add))
            pick_max(order, oh2, lg, t1, mcol)
            order.step(nc.vector.tensor_tensor(oh, oh, oh2, ALU.add))
            order.step(nc.vector.tensor_tensor(ex, ex, oh, ALU.mult))
            dve.wait_ge(s_clear, 3)
            split_stack(order, ex, 0, True)

            def at(i, name, k):
                dve.wait_ge(K[name].sem, K[name].at(0, i, k))

            def low(i, n):
                at(i, "ah", n + 1)
                at(i, "dn", n - 1)
                nc.vector.tensor_tensor(k_a[n % 2][1], k_af[n % 2], k_a[n % 2][0].bitcast(F32), ALU.subtract)\
                    .then_inc(K["al"].sem, 1)

            def weigh(i, q):
                h = q % 2
                at(i, "dn", 4 * (q + 1) if q < 4 else 16 + 2 * (q - 3))
                at(i, "acc", q - 1)
                if q >= 4:
                    ins = nc.vector.tensor_copy(k_t[h], bank(4 + h))
                else:
                    at(i, "cc", q // 2 + 1)
                    ins = nc.vector.tensor_tensor(k_t[h], bank(4 + h), half(k_cw, h), ALU.mult)
                ins.then_inc(K["t"].sem, 1)

            def next_weights(i, s, k, last_pass):
                if k == 0:
                    at(i, "dn", 8 * s)
                    at(i, "cb", s)
                if s == 0:
                    f3_piece(dve, i, 1, k)
                elif not last_pass:
                    f3_piece(dve, i + 1, 0, k)
                elif k < 2:
                    w = raw_b[:, E * W_F3:E * W_F3 + W_SH]
                    hi, lo = k_w[0][0][:, 0:W_SH], k_w[0][1][:, 0:W_SH]
                    if k == 0:
                        ins = nc.vector.tensor_copy(hi, w)
                    else:
                        dve.wait_ge(s_kw, 1)
                        ins = nc.vector.tensor_tensor(lo, w, hi.bitcast(F32), ALU.subtract)
                    ins.then_inc(s_kw, 1)

            def step(i, n, last_pass=False):
                at(i, "sg", n + 1)
                at(i, "al", n - 1)
                at(i, "ah", n - 1)
                nc.vector.tensor_tensor(k_af[n % 2], k_sg[n % 2], bank(2 + n % 2), ALU.mult).then_inc(K["a"].sem, 1)
                if n >= 1:
                    low(i, n - 1)
                if n % 4 == 2 and n > 2:
                    weigh(i, (n - 6) // 4)
                if n == 19:
                    weigh(i, 4)
                if n < 16:
                    for k in {3: (0, 1), 4: (2,), 5: (3, 4)}.get(n % 8, ()):
                        next_weights(i, n // 8, k, last_pass)

            def body(i, last_pass):
                for n in range(3, 20 if last_pass else 19):
                    step(i, n, last_pass)
                if last_pass:
                    low(i, 19)
                    weigh(i, 5)

            for n in range(3):
                step(0, n)
            passes(dve, body)

        def split_ctx(dve, order):
            dve.wait_ge(ld["ctx_t"], 16)
            order.step(nc.vector.tensor_copy(ch[:, :], out_t[:, :]))
            nc.vector.tensor_tensor(cl[:, :], out_t[:, :], ch[:, :].bitcast(F32), ALU.subtract).then_inc(s_ctx, 1)

        def mask_cap(dve, order):
            dve.wait_ge(ld["mask"], 16)
            order.step(nc.vector.tensor_scalar(w_floor, col("nbias"), -8.0, None, ALU.mult))
            flat_cap = raw_b[:, CAP:CAP + 2 * T]
            order.step(nc.vector.tensor_scalar(flat_cap, mask_u8[:, :], -BIG, BIG, ALU.mult, ALU.add))
            order.step(nc.vector.tensor_scalar(flat_cap, flat_cap, w_floor, None, ALU.add))

        block = stack.enter_context(nc.Block())

        def start(eng, *uses):
            for use, names in uses:
                for name in names.split():
                    eng.sem_inc(use[name].sem, START)

        @block.sync
        def _(sp):
            def load(dst, src, name):
                sp.dma_start(dst, src).then_inc(ld[name], 16)

            load(res[:, :, :], x, "x")
            load(sm[:, :], small, "small")
            load(out_t[:, :], ctx_t, "ctx_t")
            load(raw_a[:, RA0:RA0 + NG * W_A], wa0, "a0")
            load(raw_a[:, RF0:RF0 + 2 * NKT * W_F0], wf0, "f0")
            load(mask_u8[:, :], mask, "mask")
            load(raw_b[:, RB1:RB1 + NQ * W_B], wb1, "b1")
            load(ctok[:, :, :], ctx_tok, "ctx_tok")
            load(raw_b[:, RA2:RA2 + NG * W_A], wa2, "a2")
            sp.wait_ge(A["w"].sem, A["w"].at(0, NG, 0))
            sp.wait_ge(F["w"].sem, F["w"].at(0, NKT, 0))
            load(raw_a[:, :], wf1, "f1")
            sp.wait_ge(G["w"].sem, G["w"].at(0, PASSES, 0))
            load(raw_a[:, RB3:RB3 + NQ * W_B], wb3, "b3")
            sp.wait_ge(W["acc"].sem, W["acc"].at(0, NQ, 0))
            sp.wait_ge(A["w"].sem, A["w"].at(1, NG, 0))
            load(raw_b[:, :], wf3, "f3")
            sp.wait_ge(s_res, 2)
            sp.dma_start(out, res[:, :, :]).then_inc(s_out, 16)
            sp.wait_ge(s_out, 16)

        @block.gpsimd
        def _(pool):
            start(pool, (W, "ps"), (G, "acc"), (K, "acc"))
            nc.gpsimd.memset(mhalf[:, :], -0.5).then_inc(s_init, 1)
            pool.wait_ge(s_init, 1)
            norm_pool(pool, 0)
            small_pool(pool, 0)
            quant_pool(pool)
            norm_pool(pool, 1)
            clear_pool(pool, 0, 3, (f_ones, 1.0), (f_wt.bitcast(F32), 0.0), (stk, 0.0))
            norm_pool(pool, 2)
            wide_pool_init(pool, 0, 2)
            wide_pool(pool, 0)
            norm_pool(pool, 3)
            clear_pool(pool, 1, 5, (g_wt.bitcast(F32), 0.0), (stk, 0.0))
            f1_pool(pool)
            small_pool(pool, 1)
            norm_pool(pool, 4)
            norm_pool(pool, 5)
            norm_pool(pool, 6)
            norm_pool(pool, 7)
            norm_pool(pool, 8)
            wide_pool_init(pool, 1, 8)
            wide_pool(pool, 1)
            norm_pool(pool, 9)
            clear_pool(pool, 2, 6, (k_wt.bitcast(F32), 0.0))
            f3_pool(pool)

        @block.scalar
        def _(act):
            start(act, (A, "hi v p raw"), (F, "xs"), (W, "eh va p pvc"), (G, "a cc"), (K, "sg ah cc"))
            act.wait_ge(ld["small"], 16)
            nc.scalar.activation(gate[:, :], col("gates"), ACT.Tanh).then_inc(s_gate, 1)
            norm_act(act, 0, f32=False, high=xh)
            act.wait_ge(s_vp, 1)
            nc.scalar.activation(a_vall, bank(0, 2), ACT.Copy).then_inc(s_va, 1)
            small_act(act, 0)
            small_out_act(act)
            norm_act(act, 1, high=xh)
            f0_act(act)
            norm_act(act, 2, f32=False, high=xh)
            wide_act(act, 0, ACT.Square, col("nbias"))
            norm_act(act, 3, high=xh)
            f1_act(act)
            norm_act(act, 4, f32=False, high=xh)
            small_act(act, 1)
            norm_act(act, 5, w=col("ln_c_w"), b=col("ln_c_b"))
            norm_act(act, 6)
            norm_act(act, 7, w=col("ln_l_w"), b=col("ln_l_b"))
            wide_act(act, 1, ACT.Exp, 0.0)
            norm_act(act, 8, high=xh)
            f3_act(act)

        @block.vector
        def _(dve):
            order = Order(dve, s_dve)
            start(dve, (A, "w y km red m2 yf att"), (F, "w z acc"), (W, "w el y rec at acc"), (G, "w al t"),
                  (K, "w a al t"))
            dve.wait_ge(ld["small"], 16)
            quant_dve_max(dve)
            dve.wait_ge(ld["x"], 16)
            norm_dve_tokens(dve, order, 0, res, xn, lambda: small_weights(dve, 0, 0, raw_a, RA0, ld["a0"]))
            norm_dve_split(dve, order, 0, xh, xl)
            split_ctx(dve, order)
            dve.wait_ge(s_gate, 1)
            small_dve(dve, order, 0, raw_a, RA0, lambda: (f0_weights(dve, order), mask_cap(dve, order)))
            quant_dve(dve, order)
            back_dve(dve, order, 0, 0)
            norm_dve_tokens(dve, order, 1, res, xn)
            norm_dve_split(dve, order, 1, xh, xl)
            f0_dve(dve, order)
            back_dve(dve, order, 1, 1)
            norm_dve_tokens(dve, order, 2, res, xn, lambda: wide_weights(dve, 0, 0, raw_b, RB1, ld["b1"]))
            norm_dve_split(dve, order, 2, xh, xl)
            order.step(nc.vector.memset(xn[:, :, :], 0.0))
            wide_dve(dve, order, 0, raw_b, RB1)
            dve.wait_ge(W["acc"].sem, W["acc"].at(0, NQ, 0))
            tokens_in(dve, order, 2, xn)
            norm_dve_tokens(dve, order, 3, res, xn, lambda: f1_first(dve))
            norm_dve_split(dve, order, 3, xh, xl)
            f1_shifts_dve(dve, order)
            f1_dve(dve, order)
            tokens_in(dve, order, 3, xn)
            back_dve(dve, order, 2, 3)
            norm_dve_tokens(dve, order, 4, res, xn, lambda: small_weights(dve, 1, 0, raw_b, RA2, ld["a2"]))
            norm_dve_split(dve, order, 4, xh, xl)
            small_dve(dve, order, 1, raw_b, RA2, lambda: norm_dve_tokens(dve, order, 5, ctok, ctok))
            dve.wait_ge(A["att"].sem, A["att"].at(1, NG, 0))
            tokens_in(dve, order, 4, a_att)
            norm_dve_tokens(dve, order, 6, res, xn, lambda: norm_dve_split(dve, order, 5, ch, cl, False))
            for h in range(2):
                dve.wait_ge(s_rt, 2 * 3 + h + 1)
                r = xn[:, 4 * h:4 * h + 4, :]
                order.done(nc.vector.tensor_tensor(r, bank(6 + h).rearrange("p (t d) -> p t d", t=4),
                                                   col("quant_bias").unsqueeze(1).to_broadcast((P, 4, D)), ALU.add))
            order.wait()
            tokens_in(dve, order, 5, xn)
            norm_dve_tokens(dve, order, 7, res, xn, lambda: wide_weights(dve, 1, 0, raw_a, RB3, ld["b3"]))
            norm_dve_tokens(dve, order, 8, xn, xn)
            norm_dve_split(dve, order, 7, xh, xl, False)
            order.step(nc.vector.tensor_copy(xn[:, :, :], col("bo").unsqueeze(1).to_broadcast((P, NT, D))))
            wide_dve(dve, order, 1, raw_a, RB3)
            dve.wait_ge(W["acc"].sem, W["acc"].at(1, NQ, 0))
            tokens_in(dve, order, 6, xn)
            norm_dve_tokens(dve, order, 9, res, xn, lambda: f3_first(dve))
            norm_dve_split(dve, order, 8, xh, xl)
            f3_dve(dve, order)
            back_dve(dve, order, 4, 7, s_res)

        @block.tensor
        def _(pe):
            start(pe, (A, "q mx mt s pv rt"), (F, "x yw u"), (W, "qk vp s pv dn rb o"), (G, "up dn cb"), (K, "gu dn cb"))
            pe.wait_ge(ld["small"], 16)
            norm_pe(pe, 0, 0)
            pe.wait_ge(ld["ctx_t"], 16)
            for t in range(NT):
                last = nc.tensor.matmul(ps[:, t // 4, (t % 4) * P:(t % 4 + 1) * P], out_t[:, t * P:(t + 1) * P],
                                        col("wv0"), start=True, stop=True)
            last.then_inc(s_vp, 1)
            pe.wait_ge(s_va, 1)
            pe.wait_ge(s_ctx, 1)
            small_pe(pe, 0, 0)
            quant_pe(pe)
            small_out_pe(pe)
            norm_pe(pe, 1, 1)
            f0_pe(pe, 1)
            wide_first_values_pe(pe, 0)
            norm_pe(pe, 2, 2)
            wide_pe(pe, 0, 2, raw_b, RB1)
            f1_shifts_pe(pe)
            norm_pe(pe, 3, 3)
            f1_pe(pe, 3)
            norm_pe(pe, 4, 4)
            small_pe(pe, 1, 4)
            norm_pe(pe, 5, 5, ctok)
            norm_pe(pe, 6, 6)
            pe.wait_ge(s_xf, 2 * 6 + 2)
            pe.wait_ge(s_qw, 1)
            tokens_pe(xf, q_w[:, :])
            pe.wait_ge(s_xs, 2 * splits(5) + 2)
            wide_first_values_pe(pe, 1)
            norm_pe(pe, 8, 7)
            wide_pe(pe, 1, 7, raw_a, RB3)
            norm_pe(pe, 9, 8)
            f3_pe(pe, 8)

def tokens_first(a):
    return np.ascontiguousarray(a.reshape(NT, P, D).transpose(1, 0, 2))


def small_heads(wq, wk):
    a = np.zeros((P, NG, W_A), np.float32)
    for g in range(NG):
        for j in range(GH):
            r = (g * GH + j) * DH8
            for rep in range(3):
                at = BLK * j + DH8 * rep
                a[:, g, at:at + DH8] = wq[r:r + DH8, :].T
                a[:, g, P + at:P + at + DH8] = wk[r:r + DH8, :].T
    return a.reshape(P, NG * W_A)


def kernel(**inputs):
    import concourse.bacc as _bacc
    from concourse.bass_utils import run_bass_kernel_spmd as _run
    arrays = layout({k: np.asarray(v) for k, v in inputs.items()})
    nc = _bacc.Bacc("TRN2", target_bir_lowering=False, num_devices=1)
    aps = {n: nc.dram_tensor("in_" + n, a.shape, mybir.dt.from_np(a.dtype), kind="ExternalInput").ap()
           for n, a in arrays.items()}
    out = nc.dram_tensor("out_tokens", (P, NT, D), F32, kind="ExternalOutput").ap()
    build(nc, out=out, **aps)
    r = _run(nc, [{"in_" + n: a for n, a in arrays.items()}], core_ids=[0])
    got = np.asarray(r.results[0]["out_tokens"])
    return np.ascontiguousarray(got.transpose(1, 0, 2)).reshape(B, S, D)


def layout(v):
    f = np.float32
    sm = np.zeros((P, N_SMALL), f)

    def put(name, a, rows=slice(None)):
        at, width = SMALL[name]
        sm[rows, at:at + width] = a

    r = np.arange(P)
    put("ident", np.eye(P, dtype=f))
    c = np.arange(2 * P)
    put("spread", (r[:, None] == BLK * (2 * (c[None, :] % P // DH) + c[None, :] // P)).astype(f))
    put("lo_q", -((r % BLK) // DH8 == 2).astype(f)[:, None])
    put("lo_k", -((r % BLK) // DH8 == 1).astype(f)[:, None])
    put("one_rows", ((r % BLK == 24) | (r % BLK == 25)).astype(f)[:, None])
    put("head", (r[:, None] // BLK == np.arange(GH)[None, :]).astype(f))
    put("inv_n", np.stack([f(1) / (r + 1).astype(f), f(1) / (P + r + 1).astype(f)], 1))
    put("iota", np.arange(E, dtype=f)[None, :])
    put("gates", np.stack([v["g_xattn"], v["g_ffn"]], 1).reshape(1, 8))
    put("nbias", v["L1_xattn_nbias"].reshape(1, 1))
    put("alpha", v["L0_ffn_alpha_bi"].reshape(1, 1))
    put("rb2", v["L0_ffn_router_b2"][None, :])
    put("ebias", v["L0_ffn_expert_bias"][None, :])
    put("rb1", v["L0_ffn_router_b1"][:, None])
    put("gamma", v["L1_ffn_gamma"].T)
    put("beta", v["L1_ffn_beta"].T)
    put("b1", v["L1_ffn_b1"].reshape(E, NF, P).transpose(2, 0, 1).reshape(P, E * NF))
    put("b2", v["L1_ffn_b2"].T)
    put("quant_bias", v["L2_ffn_bias"][None, :])
    put("bo", v["L3_xattn_bo"][None, :])
    for n in ("ln_l_w", "ln_l_b", "ln_c_w", "ln_c_b"):
        put(n, v["L3_xattn_" + n][:, None])
    put("centroids", v["L1_ffn_centroids"].T)
    put("gate_w", v["L3_ffn_gate_w"].T)
    put("router_w2", v["L0_ffn_router_w2"].T)
    for k, n in enumerate(("b_fwd", "b_fwd", "b_inv", "b_inv")):
        put("b_experts", v["L0_ffn_" + n], slice(E * k, E * (k + 1)))
    for n in ("W_Q", "W_K", "W_inv", "W_O", "router_w1"):
        put(n, v["L0_ffn_" + n].T)
    put("wv0", v["L0_xattn_Wv"].T)
    put("wo0", v["L0_xattn_Wo"].T)
    put("quant_w", v["L2_ffn_kernel"])
    put("lora_a", v["L2_ffn_a"].T, slice(0, 16))
    put("lora_b", v["L2_ffn_b"], slice(0, 16))
    e = np.arange(E)
    sel_e = ((r[:, None] % E == e[None, :]) & (r[:, None] < 2 * E)).astype(f)
    put("sel_e", np.repeat(sel_e, P, axis=1))

    wf0 = np.zeros((P, NKT, 2, W_F0), f)
    for br, (nv, nw, nu) in enumerate((("V_fwd", "W_fwd", "U_fwd"), ("W_inv_exp", "V_inv", "U_inv"))):
        for k in range(NKT):
            two = slice(2 * k, 2 * k + 2)
            wf0[:, k, br, 0:P] = v["L0_ffn_" + nv][two].transpose(1, 0, 2).reshape(D, P)
            wf0[:, k, br, P:2 * P] = v["L0_ffn_" + nw][two].transpose(1, 0, 2).reshape(D, P)
            wf0[:, k, br, 2 * P:3 * P] = v["L0_ffn_" + nu][two].transpose(0, 2, 1).reshape(P, D)
            expert = 2 * k + r[None, :] // 64
            wf0[:, k, br, 3 * P:] = ((r[:, None] // (2 * E) == br) & (r[:, None] % E == expert)).astype(f)

    def wide(wq_t, wk_t, wv_t, wo):
        a = np.zeros((P, NQ, W_B), f)
        for q in range(NQ):
            s = slice(q * QW, (q + 1) * QW)
            a[:, q, 0:QW], a[:, q, QW:2 * QW], a[:, q, 2 * QW:3 * QW] = wq_t[:, s], wk_t[:, s], wv_t[:, s]
            a[:, q, 3 * QW:] = wo[s, :].reshape(2, P, D).transpose(1, 0, 2).reshape(P, 2 * D)
        return a.reshape(P, NQ * W_B)

    w = NQ * QW
    kv1, kv3 = v["L1_xattn_Wkv"], v["L3_xattn_Wkv"]
    wf1 = np.zeros((P, E, W_F1), f)
    wf1[:, :, :512] = v["L1_ffn_W1"].transpose(2, 0, 1)
    wf1[:, :, 512:] = v["L1_ffn_W2"].reshape(E, D, NF, P).transpose(3, 0, 2, 1).reshape(P, E, NF * D)
    wf3 = np.zeros((P, E * W_F3 + W_SH), f)
    a = wf3[:, :E * W_F3].reshape(P, E, W_F3)
    a[:, :, 0:512] = v["L3_ffn_gate_k"].transpose(1, 0, 2)
    a[:, :, 512:1024] = v["L3_ffn_up_k"].transpose(1, 0, 2)
    a[:, :, 1024:] = v["L3_ffn_down_k"].reshape(E, NF, P, D).transpose(2, 0, 1, 3).reshape(P, E, NF * D)
    wf3[:, :E * W_F3] = a.reshape(P, E * W_F3)
    sh = wf3[:, E * W_F3:]
    sh[:, 0:256], sh[:, 256:512] = v["L3_ffn_sh_gate"], v["L3_ffn_sh_up"]
    sh[:, 512:] = v["L3_ffn_sh_down"].reshape(2, P, D).transpose(1, 0, 2).reshape(P, 2 * D)
    eye = np.eye(D, dtype=f)
    c = v["ctx_1024"]
    arrays = dict(
        x=tokens_first(v["x"]), ctx_tok=tokens_first(c), ctx_t=np.ascontiguousarray(c.reshape(T, D).T),
        mask=np.ascontiguousarray(v["mask_BxSxS2_bk0"].reshape(B, S, 2, P).transpose(3, 0, 2, 1)).reshape(P, 2 * T),
        small=sm,
        wa0=small_heads(v["L0_xattn_Wq"], v["L0_xattn_Wk"]),
        wa2=small_heads(eye, eye),
        wf0=wf0.reshape(P, 2 * NKT * W_F0),
        wb1=wide(v["L1_xattn_Wq"].T, kv1[:w].T, kv1[w:].T, v["L1_xattn_Wo"].T),
        wf1=wf1.reshape(P, E * W_F1),
        wb3=wide(v["L3_xattn_Wq"], kv3[:, :w], kv3[:, w:], v["L3_xattn_Wo"]),
        wf3=wf3,
    )
    return arrays
```
